# Optimizing a Trainium2 kernel written in Bass

```python
import numpy as np
import jax
import jax.numpy as jnp

def _softmax(x, axis=-1):
    return jax.nn.softmax(x, axis=axis)

def _gelu(x):
    return jax.nn.gelu(x, approximate=True)

def _silu(x):
    return jax.nn.silu(x)

def _sigmoid(x):
    return jax.nn.sigmoid(x)

def _layernorm(x, axis=-1, eps=1e-05):
    m = jnp.mean(x, axis=axis, keepdims=True)
    v = jnp.var(x, axis=axis, keepdims=True)
    return (x - m) / jnp.sqrt(v + eps)

def _scatter_add(tgt, idx, src, axis=0):
    return tgt.at[idx].add(src)

def _segment_sum(src, seg, n):
    return jax.ops.segment_sum(src, seg, n)
kernel_name = 'mk_seq_postln_d2_jaxref_r8_fca0ee'

def setup_inputs(seed: int=0):
    np.random.seed(seed)
    _w = jnp.asarray

    def _L0_attn_setup():
        import jax, jax.numpy as jnp
        import numpy as np
        E2M1_GRID = jnp.array([0.0, 0.5, 1.0, 1.5, 2.0, 3.0, 4.0, 6.0], dtype=jnp.float32)
        E2M1_MIDS = (E2M1_GRID[1:] + E2M1_GRID[:-1]) / 2.0
        FP4_MAX = 6.0
        FP8_E4M3_MAX = 448.0

        def nvfp4_quant_dequant(w):
            O, I = w.shape
            w16 = w.reshape(O, I // 128, 8, 16)
            amax128 = jnp.max(jnp.abs(w16), axis=(-2, -1))
            outer = amax128 / (FP4_MAX * FP8_E4M3_MAX)
            outer = jnp.where(outer > 0, outer, 1.0)
            amax16 = jnp.max(jnp.abs(w16), axis=-1)
            inner = amax16 / FP4_MAX / outer[..., None]
            inner = inner.astype(jnp.float8_e4m3fn).astype(jnp.float32)
            scale = outer[..., None] * inner
            safe = jnp.where(scale > 0, scale, 1.0)[..., None]
            code = w16 / safe
            a = jnp.abs(code)
            idx = jnp.searchsorted(E2M1_MIDS, a)
            q = E2M1_GRID[idx] * jnp.sign(code)
            return (q * scale[..., None]).reshape(O, I)
        key = jax.random.key(seed)
        k0, k1, k2 = jax.random.split(key, 3)
        B, S, H = (2, 256, 256)
        hidden_states = jax.random.normal(k0, (B, S, H), dtype=jnp.float32)
        w_qkv = jax.random.normal(k1, (3 * H, H), dtype=jnp.float32) * 0.023
        w_o = jax.random.normal(k2, (H, H), dtype=jnp.float32) * 0.023
        w_qkv = nvfp4_quant_dequant(w_qkv)
        w_o = nvfp4_quant_dequant(w_o)
        return {'hidden_states': hidden_states, 'w_qkv': w_qkv, 'w_o': w_o}
    _L0_attn_in = _L0_attn_setup()

    def _L0_ffn_setup():
        import jax, jax.numpy as jnp
        import numpy as np
        import math
        B, S, D = (2, 256, 256)
        H, HD = (16, 128)
        E, I = (4, 256)
        TOP_K = 2
        ROPE_THETA = 10000.0

        def _layernorm(x, w, b):
            mu = jnp.mean(x, axis=-1, keepdims=True)
            var = jnp.mean(jnp.square(x - mu), axis=-1, keepdims=True)
            return (x - mu) * jax.lax.rsqrt(var + 1e-05) * w + b

        def _rotate_half(x):
            x1, x2 = jnp.split(x, 2, axis=-1)
            return jnp.concatenate((-x2, x1), axis=-1)

        def _attention(h, wq, bq, wk, bk, wv, bv, wo, bo):
            b, s, _ = h.shape
            q = (h @ wq + bq).reshape(b, s, H, HD).transpose(0, 2, 1, 3)
            k = (h @ wk + bk).reshape(b, s, H, HD).transpose(0, 2, 1, 3)
            v = (h @ wv + bv).reshape(b, s, H, HD).transpose(0, 2, 1, 3)
            inv_freq = 1.0 / ROPE_THETA ** (jnp.arange(0, HD, 2, dtype=jnp.float32) / HD)
            freqs = jnp.arange(s, dtype=jnp.float32)[:, None] * inv_freq[None, :]
            emb = jnp.concatenate((freqs, freqs), axis=-1)
            cos = jnp.cos(emb)[None, None]
            sin = jnp.sin(emb)[None, None]
            q = q * cos + _rotate_half(q) * sin
            k = k * cos + _rotate_half(k) * sin
            scores = jnp.einsum('bhqd,bhkd->bhqk', q, k) / math.sqrt(HD)
            causal = jnp.tril(jnp.ones((s, s), bool))
            scores = jnp.where(causal[None, None], scores, jnp.finfo(jnp.float32).min)
            probs = jax.nn.softmax(scores.astype(jnp.float32), axis=-1).astype(q.dtype)
            out = jnp.einsum('bhqk,bhkd->bhqd', probs, v)
            out = out.transpose(0, 2, 1, 3).reshape(b, s, H * HD)
            return out @ wo + bo

        def _moe(h, w_gate, we1, be1, we2, be2):
            b, s, d = h.shape
            x = h.reshape(-1, d)
            t = x.shape[0]
            raw = jax.nn.softmax(x @ w_gate, axis=-1)
            top_vals, top_idx = jax.lax.top_k(raw, TOP_K)
            w = jax.nn.softmax(top_vals, axis=-1)
            comb = jnp.zeros((t, E), x.dtype).at[jnp.arange(t)[:, None], top_idx].add(w)
            hmid = jax.nn.gelu(jnp.einsum('td,edi->tei', x, we1) + be1[None], approximate=False)
            eout = jnp.einsum('tei,eid->ted', hmid, we2) + be2[None]
            out = jnp.einsum('te,ted->td', comb, eout)
            return out.reshape(b, s, d)
        key = jax.random.key(seed)
        ks = jax.random.split(key, 20)
        s = 0.02
        p = {'hidden_states': jax.random.normal(ks[0], (B, S, D), jnp.float32), 'wq': jax.random.normal(ks[1], (D, H * HD), jnp.float32) * s, 'bq': jnp.zeros((H * HD,), jnp.float32), 'wk': jax.random.normal(ks[2], (D, H * HD), jnp.float32) * s, 'bk': jnp.zeros((H * HD,), jnp.float32), 'wv': jax.random.normal(ks[3], (D, H * HD), jnp.float32) * s, 'bv': jnp.zeros((H * HD,), jnp.float32), 'wo': jax.random.normal(ks[4], (H * HD, D), jnp.float32) * s, 'bo': jnp.zeros((D,), jnp.float32), 'ln1_w': jnp.ones((D,), jnp.float32), 'ln1_b': jnp.zeros((D,), jnp.float32), 'ln2_w': jnp.ones((D,), jnp.float32), 'ln2_b': jnp.zeros((D,), jnp.float32), 'w_gate': jax.random.normal(ks[5], (D, E), jnp.float32) * s, 'we1': jax.random.normal(ks[6], (E, D, I), jnp.float32) * s, 'be1': jnp.zeros((E, I), jnp.float32), 'we2': jax.random.normal(ks[7], (E, I, D), jnp.float32) * s, 'be2': jnp.zeros((E, D), jnp.float32)}
        return p
    _L0_ffn_in = _L0_ffn_setup()

    def _L1_attn_setup():
        import jax, jax.numpy as jnp
        import numpy as np
        D_MODEL = 256
        STATE = 16
        KCONV = 4
        EXPAND = 2
        D_INNER = D_MODEL * EXPAND
        EPS = 1e-05

        def _silu(v):
            return v * jax.nn.sigmoid(v)
        key = jax.random.key(seed)
        ks = jax.random.split(key, 10)
        s = 0.02
        x = jax.random.normal(ks[0], (2, 256, D_MODEL), dtype=jnp.float32)
        norm_w = jnp.ones((D_MODEL,), jnp.float32)
        in_proj_w = jax.random.normal(ks[1], (D_INNER * 2, D_MODEL), jnp.float32) * s
        conv_w = jax.random.normal(ks[2], (D_INNER, 1, KCONV), jnp.float32) * s
        conv_b = jnp.zeros((D_INNER,), jnp.float32)
        x_proj_w = jax.random.normal(ks[3], (STATE * 2 + 1, D_INNER), jnp.float32) * s
        dt_w = jax.random.normal(ks[4], (D_INNER, 1), jnp.float32) * s
        dt_b = jnp.zeros((D_INNER,), jnp.float32)
        A_log = jnp.log(jnp.broadcast_to(jnp.arange(1, STATE + 1, dtype=jnp.float32)[None, :], (D_INNER, STATE)))
        D_param = jnp.ones((D_INNER,), jnp.float32)
        out_proj_w = jax.random.normal(ks[5], (D_MODEL, D_INNER), jnp.float32) * s
        return {'x': x, 'norm_w': norm_w, 'in_proj_w': in_proj_w, 'conv_w': conv_w, 'conv_b': conv_b, 'x_proj_w': x_proj_w, 'dt_w': dt_w, 'dt_b': dt_b, 'A_log': A_log, 'D_param': D_param, 'out_proj_w': out_proj_w}
    _L1_attn_in = _L1_attn_setup()

    def _L1_ffn_setup():
        import jax, jax.numpy as jnp
        import numpy as np
        B, T, D = (4, 256, 256)
        E = 8
        K = 2
        F = 1024 // (E // 2)
        key = jax.random.key(seed)
        ks = jax.random.split(key, 5)
        s_in = 1.0 / np.sqrt(D)
        s_mid = 1.0 / np.sqrt(F)
        x = jax.random.normal(ks[0], (B, T, D), dtype=jnp.float32)
        Wr = jax.random.normal(ks[1], (D, E), dtype=jnp.float32) * s_in
        Wg = jax.random.normal(ks[2], (E, D, F), dtype=jnp.float32) * s_in
        Wu = jax.random.normal(ks[3], (E, D, F), dtype=jnp.float32) * s_in
        Wd = jax.random.normal(ks[4], (E, F, D), dtype=jnp.float32) * s_mid
        return {'x': x, 'Wr': Wr, 'Wg': Wg, 'Wu': Wu, 'Wd': Wd}
    _L1_ffn_in = _L1_ffn_setup()
    _d = {'L0_attn_hidden_states': _L0_attn_in['hidden_states'], 'L0_attn_w_qkv': _L0_attn_in['w_qkv'], 'L0_attn_w_o': _L0_attn_in['w_o'], 'L0_ffn_wq': _L0_ffn_in['wq'], 'L0_ffn_bq': _L0_ffn_in['bq'], 'L0_ffn_wk': _L0_ffn_in['wk'], 'L0_ffn_bk': _L0_ffn_in['bk'], 'L0_ffn_wv': _L0_ffn_in['wv'], 'L0_ffn_bv': _L0_ffn_in['bv'], 'L0_ffn_wo': _L0_ffn_in['wo'], 'L0_ffn_bo': _L0_ffn_in['bo'], 'L0_ffn_ln1_w': _L0_ffn_in['ln1_w'], 'L0_ffn_ln1_b': _L0_ffn_in['ln1_b'], 'L0_ffn_ln2_w': _L0_ffn_in['ln2_w'], 'L0_ffn_ln2_b': _L0_ffn_in['ln2_b'], 'L0_ffn_w_gate': _L0_ffn_in['w_gate'], 'L0_ffn_we1': _L0_ffn_in['we1'], 'L0_ffn_be1': _L0_ffn_in['be1'], 'L0_ffn_we2': _L0_ffn_in['we2'], 'L0_ffn_be2': _L0_ffn_in['be2'], 'L1_attn_norm_w': _L1_attn_in['norm_w'], 'L1_attn_in_proj_w': _L1_attn_in['in_proj_w'], 'L1_attn_conv_w': _L1_attn_in['conv_w'], 'L1_attn_conv_b': _L1_attn_in['conv_b'], 'L1_attn_x_proj_w': _L1_attn_in['x_proj_w'], 'L1_attn_dt_w': _L1_attn_in['dt_w'], 'L1_attn_dt_b': _L1_attn_in['dt_b'], 'L1_attn_A_log': _L1_attn_in['A_log'], 'L1_attn_D_param': _L1_attn_in['D_param'], 'L1_attn_out_proj_w': _L1_attn_in['out_proj_w'], 'L1_ffn_Wr': _L1_ffn_in['Wr'], 'L1_ffn_Wg': _L1_ffn_in['Wg'], 'L1_ffn_Wu': _L1_ffn_in['Wu'], 'L1_ffn_Wd': _L1_ffn_in['Wd']}
    _x0 = _d['L0_attn_hidden_states']
    _d['L0_attn_hidden_states'] = jax.random.normal(jax.random.fold_in(jax.random.key(seed), 1), (2, 512, 256), dtype=_x0.dtype)
    del _x0
    return _d

def reference(L0_attn_hidden_states, L0_attn_w_qkv, L0_attn_w_o, L0_ffn_wq, L0_ffn_bq, L0_ffn_wk, L0_ffn_bk, L0_ffn_wv, L0_ffn_bv, L0_ffn_wo, L0_ffn_bo, L0_ffn_ln1_w, L0_ffn_ln1_b, L0_ffn_ln2_w, L0_ffn_ln2_b, L0_ffn_w_gate, L0_ffn_we1, L0_ffn_be1, L0_ffn_we2, L0_ffn_be2, L1_attn_norm_w, L1_attn_in_proj_w, L1_attn_conv_w, L1_attn_conv_b, L1_attn_x_proj_w, L1_attn_dt_w, L1_attn_dt_b, L1_attn_A_log, L1_attn_D_param, L1_attn_out_proj_w, L1_ffn_Wr, L1_ffn_Wg, L1_ffn_Wu, L1_ffn_Wd):

    def _L0_attn_ref(hidden_states, w_qkv, w_o):
        import jax, jax.numpy as jnp
        import numpy as np
        E2M1_GRID = jnp.array([0.0, 0.5, 1.0, 1.5, 2.0, 3.0, 4.0, 6.0], dtype=jnp.float32)
        E2M1_MIDS = (E2M1_GRID[1:] + E2M1_GRID[:-1]) / 2.0
        FP4_MAX = 6.0
        FP8_E4M3_MAX = 448.0

        def nvfp4_quant_dequant(w):
            O, I = w.shape
            w16 = w.reshape(O, I // 128, 8, 16)
            amax128 = jnp.max(jnp.abs(w16), axis=(-2, -1))
            outer = amax128 / (FP4_MAX * FP8_E4M3_MAX)
            outer = jnp.where(outer > 0, outer, 1.0)
            amax16 = jnp.max(jnp.abs(w16), axis=-1)
            inner = amax16 / FP4_MAX / outer[..., None]
            inner = inner.astype(jnp.float8_e4m3fn).astype(jnp.float32)
            scale = outer[..., None] * inner
            safe = jnp.where(scale > 0, scale, 1.0)[..., None]
            code = w16 / safe
            a = jnp.abs(code)
            idx = jnp.searchsorted(E2M1_MIDS, a)
            q = E2M1_GRID[idx] * jnp.sign(code)
            return (q * scale[..., None]).reshape(O, I)
        B, S, H = hidden_states.shape
        num_heads = 16
        head_dim = H // num_heads
        qkv = jnp.einsum('bsh,oh->bso', hidden_states, w_qkv)
        qkv = qkv.reshape(B, S, 3, num_heads, head_dim)
        qkv = jnp.transpose(qkv, (2, 0, 3, 1, 4))
        q, k, v = (qkv[0], qkv[1], qkv[2])
        scale = 1.0 / jnp.sqrt(jnp.float32(head_dim))
        scores = jnp.einsum('bhqd,bhkd->bhqk', q, k) * scale
        causal = jnp.tril(jnp.ones((S, S), dtype=bool))
        scores = jnp.where(causal, scores, jnp.finfo(scores.dtype).min)
        probs = jax.nn.softmax(scores, axis=-1)
        attn = jnp.einsum('bhqk,bhkd->bhqd', probs, v)
        attn = jnp.transpose(attn, (0, 2, 1, 3)).reshape(B, S, H)
        return jnp.einsum('bsh,oh->bso', attn, w_o)

    def _L0_ffn_ref(hidden_states, wq, bq, wk, bk, wv, bv, wo, bo, ln1_w, ln1_b, ln2_w, ln2_b, w_gate, we1, be1, we2, be2):
        import jax, jax.numpy as jnp
        import numpy as np
        import math
        B, S, D = (2, 256, 256)
        H, HD = (16, 128)
        E, I = (4, 256)
        TOP_K = 2
        ROPE_THETA = 10000.0

        def _layernorm(x, w, b):
            mu = jnp.mean(x, axis=-1, keepdims=True)
            var = jnp.mean(jnp.square(x - mu), axis=-1, keepdims=True)
            return (x - mu) * jax.lax.rsqrt(var + 1e-05) * w + b

        def _rotate_half(x):
            x1, x2 = jnp.split(x, 2, axis=-1)
            return jnp.concatenate((-x2, x1), axis=-1)

        def _attention(h, wq, bq, wk, bk, wv, bv, wo, bo):
            b, s, _ = h.shape
            q = (h @ wq + bq).reshape(b, s, H, HD).transpose(0, 2, 1, 3)
            k = (h @ wk + bk).reshape(b, s, H, HD).transpose(0, 2, 1, 3)
            v = (h @ wv + bv).reshape(b, s, H, HD).transpose(0, 2, 1, 3)
            inv_freq = 1.0 / ROPE_THETA ** (jnp.arange(0, HD, 2, dtype=jnp.float32) / HD)
            freqs = jnp.arange(s, dtype=jnp.float32)[:, None] * inv_freq[None, :]
            emb = jnp.concatenate((freqs, freqs), axis=-1)
            cos = jnp.cos(emb)[None, None]
            sin = jnp.sin(emb)[None, None]
            q = q * cos + _rotate_half(q) * sin
            k = k * cos + _rotate_half(k) * sin
            scores = jnp.einsum('bhqd,bhkd->bhqk', q, k) / math.sqrt(HD)
            causal = jnp.tril(jnp.ones((s, s), bool))
            scores = jnp.where(causal[None, None], scores, jnp.finfo(jnp.float32).min)
            probs = jax.nn.softmax(scores.astype(jnp.float32), axis=-1).astype(q.dtype)
            out = jnp.einsum('bhqk,bhkd->bhqd', probs, v)
            out = out.transpose(0, 2, 1, 3).reshape(b, s, H * HD)
            return out @ wo + bo

        def _moe(h, w_gate, we1, be1, we2, be2):
            b, s, d = h.shape
            x = h.reshape(-1, d)
            t = x.shape[0]
            raw = jax.nn.softmax(x @ w_gate, axis=-1)
            top_vals, top_idx = jax.lax.top_k(raw, TOP_K)
            w = jax.nn.softmax(top_vals, axis=-1)
            comb = jnp.zeros((t, E), x.dtype).at[jnp.arange(t)[:, None], top_idx].add(w)
            hmid = jax.nn.gelu(jnp.einsum('td,edi->tei', x, we1) + be1[None], approximate=False)
            eout = jnp.einsum('tei,eid->ted', hmid, we2) + be2[None]
            out = jnp.einsum('te,ted->td', comb, eout)
            return out.reshape(b, s, d)
        a = _attention(_layernorm(hidden_states, ln1_w, ln1_b), wq, bq, wk, bk, wv, bv, wo, bo)
        h = hidden_states + a
        m = _moe(_layernorm(h, ln2_w, ln2_b), w_gate, we1, be1, we2, be2)
        return h + m

    def _L1_attn_ref(x, norm_w, in_proj_w, conv_w, conv_b, x_proj_w, dt_w, dt_b, A_log, D_param, out_proj_w):
        import jax, jax.numpy as jnp
        import numpy as np
        D_MODEL = 256
        STATE = 16
        KCONV = 4
        EXPAND = 2
        D_INNER = D_MODEL * EXPAND
        EPS = 1e-05

        def _silu(v):
            return v * jax.nn.sigmoid(v)
        residual = x
        xn = x * jax.lax.rsqrt(jnp.mean(x * x, axis=-1, keepdims=True) + EPS) * norm_w
        xz = jnp.einsum('bld,ed->ble', xn, in_proj_w)
        x_inner, z = jnp.split(xz, 2, axis=-1)
        xc = jnp.transpose(x_inner, (0, 2, 1))
        xc = jax.lax.conv_general_dilated(xc, conv_w, window_strides=(1,), padding=[(KCONV - 1, 0)], dimension_numbers=('NCH', 'OIH', 'NCH'), feature_group_count=D_INNER)
        xc = xc + conv_b[None, :, None]
        xc = _silu(jnp.transpose(xc, (0, 2, 1)))
        x_ssm = jnp.einsum('bld,ed->ble', xc, x_proj_w)
        dt = jax.nn.softplus(x_ssm[..., -1:] * dt_w[:, 0] + dt_b)
        B_p = x_ssm[..., :STATE]
        C_p = x_ssm[..., STATE:2 * STATE]
        A = -jnp.exp(A_log)
        batch = x.shape[0]
        h0 = jnp.zeros((batch, D_INNER, STATE), x.dtype)

        def step(h, inp):
            dt_t, B_t, C_t, u_t = inp
            dA = jnp.exp(dt_t[..., None] * A)
            h = dA * h + (dt_t * u_t)[..., None] * B_t[:, None, :]
            y_t = jnp.sum(h * C_t[:, None, :], axis=-1) + D_param * u_t
            return (h, y_t)
        seq_first = lambda a: jnp.swapaxes(a, 0, 1)
        _, ys = jax.lax.scan(step, h0, (seq_first(dt), seq_first(B_p), seq_first(C_p), seq_first(xc)))
        y = jnp.swapaxes(ys, 0, 1)
        y = y * _silu(z)
        return jnp.einsum('ble,de->bld', y, out_proj_w) + residual

    def _L1_ffn_ref(x, Wr, Wg, Wu, Wd):
        import jax, jax.numpy as jnp
        import numpy as np
        B, T, D = (4, 256, 256)
        E = 8
        K = 2
        F = 1024 // (E // 2)
        probs = jax.nn.softmax(x @ Wr, axis=-1)
        topk_w, topk_idx = jax.lax.top_k(probs, K)
        topk_w = topk_w / jnp.sum(topk_w, axis=-1, keepdims=True)
        output = jnp.zeros_like(x)
        for i in range(E):
            sel = topk_idx == i
            w_i = jnp.sum(topk_w * sel.astype(x.dtype), axis=-1, keepdims=True)
            h = jax.nn.silu(x @ Wg[i]) * (x @ Wu[i])
            e_out = h @ Wd[i]
            output = output + w_i * e_out
        return output
    x = L0_attn_hidden_states
    x = _layernorm(x + _L0_attn_ref(x, L0_attn_w_qkv, L0_attn_w_o), axis=-1)
    x = _layernorm(x + _L0_ffn_ref(x, L0_ffn_wq, L0_ffn_bq, L0_ffn_wk, L0_ffn_bk, L0_ffn_wv, L0_ffn_bv, L0_ffn_wo, L0_ffn_bo, L0_ffn_ln1_w, L0_ffn_ln1_b, L0_ffn_ln2_w, L0_ffn_ln2_b, L0_ffn_w_gate, L0_ffn_we1, L0_ffn_be1, L0_ffn_we2, L0_ffn_be2), axis=-1)
    x = _layernorm(x + _L1_attn_ref(x, L1_attn_norm_w, L1_attn_in_proj_w, L1_attn_conv_w, L1_attn_conv_b, L1_attn_x_proj_w, L1_attn_dt_w, L1_attn_dt_b, L1_attn_A_log, L1_attn_D_param, L1_attn_out_proj_w), axis=-1)
    x = _layernorm(x + _L1_ffn_ref(x, L1_ffn_Wr, L1_ffn_Wg, L1_ffn_Wu, L1_ffn_Wd), axis=-1)
    return x

_drawn_inputs = setup_inputs


def setup_inputs(seed=0):
    import zlib

    import numpy as np

    out = dict(_drawn_inputs(seed))
    spreads = {'L0_ffn_bq': (0.0, 0.8),
     'L0_ffn_bk': (0.0, 0.8),
     'L0_ffn_bv': (0.0, 0.1),
     'L0_ffn_bo': (0.0, 0.1),
     'L0_ffn_ln1_w': (1.0, 0.6),
     'L0_ffn_ln1_b': (0.0, 0.1),
     'L0_ffn_ln2_w': (1.0, 0.2),
     'L0_ffn_ln2_b': (0.0, 0.1),
     'L0_ffn_be1': (0.0, 0.281),
     'L0_ffn_be2': (0.0, 0.1),
     'L1_attn_norm_w': (1.0, 0.6),
     'L1_attn_conv_b': (0.0, 0.364),
     'L1_attn_dt_b': (0.0, 0.8),
     'L1_attn_D_param': (1.0, 0.6)}
    factors = {'L0_ffn_wq': 4.381,
     'L0_ffn_wk': 3.63,
     'L1_attn_in_proj_w': 4.058,
     'L1_attn_conv_w': 8.0,
     'L1_attn_x_proj_w': 8.0,
     'L1_attn_dt_w': 8.0,
     'L1_attn_A_log': 8.0,
     'L1_attn_out_proj_w': 4.146}
    for name, (base, spread) in spreads.items():
        noise = np.random.default_rng([zlib.crc32(name.encode()), seed]).standard_normal(out[name].shape)
        drawn = base * np.exp(spread * noise) if base else spread * noise
        out[name] = jnp.asarray(drawn.astype(out[name].dtype))
    for name, factor in factors.items():
        out[name] = (out[name] * factor).astype(out[name].dtype)
    return out
```

```python
from contextlib import ExitStack

import concourse.bass as bass
from concourse import mybir

ALU = mybir.AluOpType
ACT = mybir.ActivationFunctionType
AX = mybir.AxisListType
F32 = mybir.dt.float32
BF16 = mybir.dt.bfloat16
U32 = mybir.dt.uint32
ds = bass.ds

P = 128
D = 256
KD = D // P
T = 1024
NT = T // P
B = 2
S = T // B
QT = S // P
EPS = 1e-5

A_H, A_HD = 16, 16
A_G = 4
A_GROUPS = A_H // A_G
A_STEPS = B * A_G * QT
B_H, B_HD = 16, 128
B_STEPS = B * QT
MOE_B, MOE_D = 4, 8
F = 256
KF = F // P
DI = 512
KI = DI // P
NS = 16
TAPS = 4


class Order:

    def __init__(self, eng, sem, base=0):
        self.eng, self.sem, self.base, self.n = eng, sem, base, 0

    def mark(self, ins):
        ins.then_inc(self.sem, 1)
        self.n += 1

    def sync(self, behind=0):
        self.eng.wait_ge(self.sem, self.base + (self.n - behind))


def build_program(nc, a, out):
    top = ExitStack()
    with top:
        def sb(name, shape, dt=F32, ctx=top):
            return ctx.enter_context(nc.sbuf_tensor(name, shape, dt))

        sems = {}

        def sem(name):
            if name not in sems:
                sems[name] = top.enter_context(nc.semaphore(name))
            return sems[name]

        psum = top.enter_context(nc.psum_tensor("psum", [P, 8, 512], F32))
        bank = [psum[:, i, :] for i in range(8)]

        ident = sb("ident", [P, P])
        ident_bf = sb("ident_bf", [P, P], BF16)
        mask_bf = sb("mask_bf", [P, P], BF16)
        iota = sb("iota", [P, 8])
        power = sb("power", [P, NT])
        res = sb("res", [P, NT, D])
        pre = sb("pre", [P, NT, D])
        nrm = sb("nrm", [P, NT, D])
        xT = sb("xT", [P, KD, T])
        stats = sb("stats", [P, NT, 6])
        mv = sb("mv", [P, NT, 2])
        var_eps = sb("var_eps", [P, NT])
        rstd = sb("rstd", [P, NT])
        ln1w, ln1b = sb("ln1w", [P, KD]), sb("ln1b", [P, KD])
        ln2w, ln2b = sb("ln2w", [P, KD]), sb("ln2b", [P, KD])
        rmsw = sb("rmsw", [P, KD])
        probs8 = sb("probs8", [P, NT, 8])
        top8 = sb("top8", [P, NT, 8])
        idx8 = sb("idx8", [P, NT, 8], U32)
        idxf = sb("idxf", [P, NT, 2])
        comb = sb("comb", [P, NT, 8])
        pick = sb("pick", [P, NT, 8])
        row1 = sb("row1", [P, NT])
        row2 = sb("row2", [P, NT])
        wts = sb("wts", [P, NT, 2])

        norms = [0]

        def norm_stats(v, own, t, src):
            own.mark(v.bn_stats(stats[:, t, :], src[:, t, :]))
            own.sync()
            own.mark(v.bn_aggr(mv[:, t, :], stats[:, t, :]))

        def norm_apply(v, own, k, src, dst, ready=None):
            own.sync()
            v.tensor_scalar(var_eps[:, :], mv[:, :, 1], EPS, None, ALU.add).then_inc(sem("var_ready"), 1)
            v.wait_ge(sem("rstd_ready"), k)
            for t in range(NT):
                ins = v.tensor_scalar(dst[:, t, :], src[:, t, :], mv[:, t, 0:1], rstd[:, t:t + 1],
                                      ALU.subtract, ALU.mult)
                if ready is not None:
                    ins.then_inc(ready, 1)
                else:
                    own.mark(ins)

        def pool_rstd(pool, k):
            pool.wait_ge(sem("var_ready"), k)
            pool.tensor_tensor(rstd[:, :], var_eps[:, :], power[:, :], ALU.pow).then_inc(sem("rstd_ready"), 1)

        def transpose_tokens(pe, src, src_ready, done, kt_n=KD, base=0):
            for half in range(2):
                for kt in range(kt_n):
                    pe.wait_ge(src_ready, 4 * (half + 1))
                    for j in range(4):
                        ins = pe.transpose(bank[base + half * kt_n + kt][:, j * P:(j + 1) * P],
                                           src[:, 4 * half + j, kt * P:(kt + 1) * P], ident[:, :])
                    ins.then_inc(done, 1)

        def evac_transposed(eng, which, done, ready, scale=None, bias=None):
            for half in range(2):
                eng.wait_ge(done, half * KD + which + 1)
                src = bank[half * KD + which][:, :]
                dst = xT[:, which, half * S:(half + 1) * S]
                w = scale[:, which:which + 1] if scale is not None else 1.0
                b = bias[:, which:which + 1] if bias is not None else 0.0
                if which == 0:
                    ins = eng.activation(dst, src, ACT.Identity, bias=b, scale=w)
                elif scale is None:
                    ins = eng.tensor_copy(dst, src)
                else:
                    ins = eng.tensor_scalar(dst, src, w, b, ALU.mult, ALU.add)
                ins.then_inc(ready, 1)

        lay = ExitStack()
        with lay:
            wqk = sb("a_wqk", [P, 2, KD, P], ctx=lay)
            wv = sb("a_wv", [P, KD, D], ctx=lay)
            wo = sb("a_wo", [P, KD, D], ctx=lay)
            qT = [sb(f"a_qT{b}", [P, S], ctx=lay) for b in range(B)]
            kT = [sb(f"a_kT{b}", [P, S], ctx=lay) for b in range(B)]
            val = sb("a_val", [P, NT, D], ctx=lay)
            att = sb("a_att", [P, NT, D], ctx=lay)
            attT = sb("a_attT", [P, KD, T], ctx=lay)
            pr = [sb(f"a_pr{i}", [P, S], ctx=lay) for i in range(3)]
            prT = [sb(f"a_prT{i}", [P, S], ctx=lay) for i in range(2)]
            nmax = sb("a_nmax", [P, A_STEPS], ctx=lay)
            ssum = sb("a_ssum", [P, A_STEPS], ctx=lay)
            rsum = sb("a_rsum", [P, A_STEPS], ctx=lay)
            sc, tp, ob, xb = bank[0:3], bank[3:5], bank[5], bank[6:8]

            def step(s):
                return s // (A_G * QT), s // QT % A_G, s % QT

            def on_act(s):
                return s % QT == 1

            with nc.Block() as blk:
                @blk.sync
                def _(sp):
                    sp.dma_start(xT[:, :, :], a["xT"].rearrange("(k p) t -> p k t", p=P)).then_inc(sem("a_x"), 16)
                    sp.dma_start(wv[:, :, :], a["a_wv"].rearrange("(k p) n -> p k n", p=P)).then_inc(sem("a_wv"), 16)
                    sp.dma_start(wqk[:, :, :, :], a["a_wqk"][0]).then_inc(sem("a_wqk"), 16)
                    for dst, name in ((ident_bf, "ident_bf"), (mask_bf, "mask_bf"), (ident, "ident")):
                        sp.dma_start(dst[:, :], a[name]).then_inc(sem("consts"), 16)
                    for dst, name in ((ln1w, "ln1w"), (ln1b, "ln1b"), (ln2w, "ln2w"), (ln2b, "ln2b"), (rmsw, "rmsw"),
                                      (iota, "iota")):
                        sp.dma_start(dst[:, :], a[name]).then_inc(sem("consts2"), 16)
                    sp.dma_start(wo[:, :, :], a["a_wo"].rearrange("(k p) n -> p k n", p=P)).then_inc(sem("a_wo"), 16)
                    sp.dma_start(res[:, :, :], a["x"].rearrange("(t p) d -> p t d", p=P)).then_inc(sem("a_res"), 16)
                    with sp.Fori(1, A_GROUPS) as g:
                        src = a["a_wqk"][ds(g, 1), :, :, :, :].rearrange("a p c k n -> p (a c k) n")
                        sp.wait_ge(sem("a_proj"), g * 4)
                        sp.dma_start(wqk[:, :, :, :].rearrange("p c k n -> p (c k) n"), src).then_inc(sem("a_wqk"), 16)

                @blk.tensor
                def _(pe):
                    def project(g, b, c):
                        if b == 0 and c == 0:
                            pe.wait_ge(sem("a_wqk"), g * 16 + 16)
                        if b == 1:
                            pe.wait_ge(sem("a_q" if c == 0 else "a_k"), g * 2 + 1)
                        for kt in range(KD):
                            ins = pe.matmul(xb[c][:, :], wqk[:, c, kt, :], xT[:, kt, b * S:(b + 1) * S],
                                            start=(kt == 0), stop=(kt == KD - 1))
                        ins.then_inc(sem("a_proj"), 1)

                    def scores(g, s):
                        b, h, i = step(s)
                        if s % (A_G * QT) == 0:
                            pe.wait_ge(sem("a_q"), g * 2 + (b + 1))
                            pe.wait_ge(sem("a_k"), g * 2 + (b + 1))
                        w, rows = (i + 1) * P, slice(32 * h, 32 * h + A_HD)
                        pe.matmul(sc[s % 3][:, 0:w], qT[b][rows, i * P:w], kT[b][rows, 0:w], start=True, stop=False)
                        pe.matmul(sc[s % 3][:, i * P:w], ident_bf[:, :], mask_bf[:, :],
                                  start=False, stop=True).then_inc(sem("a_scores"), 1)

                    def turn(g, s):
                        i = step(s)[2]
                        pe.wait_ge(sem("a_exp"), g * A_STEPS + (s + 1))
                        for j in range(i + 1):
                            ins = pe.transpose(tp[s % 2][:, j * P:(j + 1) * P], pr[s % 3][:, j * P:(j + 1) * P],
                                               ident[:, :])
                        ins.then_inc(sem("a_turned"), 1)

                    def weigh(g, s):
                        b, h, i = step(s)
                        done = [on_act(x) for x in range(s + 1)]
                        if on_act(s):
                            pe.wait_ge(sem("a_prT_act"), g * (A_STEPS // QT) + sum(done))
                        else:
                            pe.wait_ge(sem("a_prT_dve"), g * (A_STEPS - A_STEPS // QT) + (s + 1 - sum(done)))
                        if s == A_G * QT:
                            pe.wait_ge(sem("a_out"), g * 2 + 1)
                        if s == 0:
                            pe.wait_ge(sem("a_out"), g * 2)
                        col = (s % (A_G * QT)) * A_HD
                        for j in range(i + 1):
                            v = val[:, b * QT + j, ds(g * (A_G * A_HD) + h * A_HD, A_HD)]
                            ins = pe.matmul(ob[:, col:col + A_HD], prT[s % 2][:, j * P:(j + 1) * P], v,
                                            start=(j == 0), stop=(j == i))
                        if s % (A_G * QT) == A_G * QT - 1:
                            ins.then_inc(sem("a_weighed"), 1)

                    def group(g, last):
                        for s in range(A_STEPS):
                            scores(g, s)
                            if s >= 2:
                                turn(g, s - 2)
                            if s >= 3:
                                weigh(g, s - 3)
                        for b in range(B):
                            if not last:
                                project(g + 1, b, 0)
                                project(g + 1, b, 1)
                            turn(g, A_STEPS - 2 + b)
                            weigh(g, A_STEPS - 3 + b)
                        weigh(g, A_STEPS - 1)

                    pe.wait_ge(sem("a_x"), 16)
                    pe.wait_ge(sem("a_wv"), 16)
                    for t in range(NT):
                        for kt in range(KD):
                            ins = pe.matmul(bank[t // 2][:, t % 2 * D:(t % 2 + 1) * D], xT[:, kt, t * P:(t + 1) * P],
                                            wv[:, kt, :], start=(kt == 0), stop=(kt == KD - 1))
                        if t % 2:
                            ins.then_inc(sem("a_vproj"), 1)
                    for b in range(B):
                        for c in range(2):
                            project(0, b, c)
                    pe.wait_ge(sem("consts"), 48)
                    pe.wait_ge(sem("a_val_act"), 2)
                    pe.wait_ge(sem("a_val_dve"), 2)
                    with pe.Fori(0, A_GROUPS - 1) as g:
                        group(g, False)
                    group(A_GROUPS - 1, True)

                    pe.wait_ge(sem("a_out"), 2 * A_GROUPS)
                    for half in range(2):
                        for kt in range(KD):
                            for j in range(4):
                                ins = pe.transpose(bank[half * KD + kt][:, j * P:(j + 1) * P],
                                                   att[:, 4 * half + j, kt * P:(kt + 1) * P], ident[:, :])
                            ins.then_inc(sem("a_att_turned"), 1)
                    pe.wait_ge(sem("a_wo"), 16)
                    for t in range(NT):
                        if t % 4 == 0:
                            pe.wait_ge(sem("a_attT_act"), t // 4 + 1)
                            pe.wait_ge(sem("a_attT_dve"), t // 4 + 1)
                        if t >= 4:
                            pe.wait_ge(sem("a_pre"), t - 3)
                        for kt in range(KD):
                            ins = pe.matmul(bank[4 + t % 4][:, 0:D], attT[:, kt, t * P:(t + 1) * P], wo[:, kt, :],
                                            start=(kt == 0), stop=(kt == KD - 1))
                        ins.then_inc(sem("a_oproj"), 1)
                    transpose_tokens(pe, nrm, sem("a_nrm"), sem("a_turn2"))

                @blk.scalar
                def _(act):
                    def group(g, last):
                        for s in range(A_STEPS + 2):
                            if s < A_STEPS:
                                w = (step(s)[2] + 1) * P
                                act.wait_ge(sem("a_max"), g * A_STEPS + (s + 1))
                                if s >= 3:
                                    act.wait_ge(sem("a_turned"), g * A_STEPS + (s - 2))
                                act.activation(pr[s % 3][:, 0:w], sc[s % 3][:, 0:w], ACT.Exp, bias=nmax[:, s:s + 1],
                                               scale=1.0, accum_out=ssum[:, s:s + 1]).then_inc(sem("a_exp"), 1)
                            if s >= 2 and on_act(s - 2):
                                w = (step(s - 2)[2] + 1) * P
                                act.wait_ge(sem("a_turned"), g * A_STEPS + (s - 1))
                                act.activation(prT[s % 2][:, 0:w], tp[s % 2][:, 0:w],
                                               ACT.Copy).then_inc(sem("a_prT_act"), 1)
                        if not last:
                            queries(g + 1)

                    def queries(g):
                        for b in range(B):
                            act.wait_ge(sem("a_proj"), g * 4 + (2 * b + 1))
                            act.activation(qT[b][:, :], xb[0][:, :], ACT.Copy,
                                           scale=float(A_HD) ** -0.5).then_inc(sem("a_q"), 1)

                    for n in range(0, 4, 2):
                        act.wait_ge(sem("a_vproj"), n + 1)
                        act.activation(val[:, 2 * n:2 * n + 2, :].rearrange("p t d -> p (t d)"), bank[n][:, :],
                                       ACT.Copy).then_inc(sem("a_val_act"), 1)
                    queries(0)
                    with act.Fori(0, A_GROUPS - 1) as g:
                        group(g, False)
                    group(A_GROUPS - 1, True)
                    for half in range(2):
                        act.wait_ge(sem("a_att_turned"), half * KD + 1)
                        act.activation(attT[:, 0, half * S:(half + 1) * S], bank[half * KD][:, :],
                                       ACT.Copy).then_inc(sem("a_attT_act"), 1)
                    act.wait_ge(sem("consts2"), 96)
                    evac_transposed(act, 0, sem("a_turn2"), sem("a_xT"), ln1w, ln1b)

                @blk.vector
                def _(v):
                    own = Order(v, sem("v_own"))

                    def group(g, last):
                        for s in range(A_STEPS + 2):
                            if s < A_STEPS:
                                w = (step(s)[2] + 1) * P
                                v.wait_ge(sem("a_scores"), g * A_STEPS + (s + 1))
                                v.tensor_reduce(nmax[:, s:s + 1], sc[s % 3][:, 0:w], AX.X, ALU.max,
                                                negate=True).then_inc(sem("a_max"), 1)
                            if s >= A_STEPS and not last:
                                keys(g + 1, s - A_STEPS)
                            if s >= 2 and not on_act(s - 2):
                                w = (step(s - 2)[2] + 1) * P
                                v.wait_ge(sem("a_turned"), g * A_STEPS + (s - 1))
                                v.tensor_copy(prT[s % 2][:, 0:w], tp[s % 2][:, 0:w]).then_inc(sem("a_prT_dve"), 1)
                            if s == A_G * QT + 2:
                                results(g, 0)
                        results(g, 1)

                    def keys(g, b):
                        v.wait_ge(sem("a_proj"), g * 4 + (2 * b + 2))
                        v.tensor_copy(kT[b][:, :], xb[1][:, :]).then_inc(sem("a_k"), 1)

                    def results(g, b):
                        n = A_G * QT
                        v.wait_ge(sem("a_weighed"), g * 2 + (b + 1))
                        v.reciprocal(rsum[:, b * n:(b + 1) * n], ssum[:, b * n:(b + 1) * n]).then_inc(sem("a_rsum"), 1)
                        dst = att[:, b * QT:(b + 1) * QT, ds(g * (A_G * A_HD), A_G * A_HD)]
                        v.wait_ge(sem("a_rsum"), g * 2 + (b + 1))
                        v.tensor_tensor(dst.rearrange("p i (h d) -> p h i d", h=A_G),
                                        ob[:, 0:n * A_HD].rearrange("p (h i d) -> p h i d", h=A_G, i=QT),
                                        rsum[:, b * n:(b + 1) * n].rearrange("p (h i) -> p h i", h=A_G).unsqueeze(3)
                                        .to_broadcast([P, A_G, QT, A_HD]), ALU.mult).then_inc(sem("a_out"), 1)

                    v.memset(power[:, :], -0.5).then_inc(sem("power"), 1)
                    for n in range(1, 4, 2):
                        v.wait_ge(sem("a_vproj"), n + 1)
                        v.tensor_copy(val[:, 2 * n:2 * n + 2, :].rearrange("p t d -> p (t d)"),
                                      bank[n][:, :]).then_inc(sem("a_val_dve"), 1)
                    keys(0, 0)
                    keys(0, 1)
                    with v.Fori(0, A_GROUPS - 1) as g:
                        group(g, False)
                    group(A_GROUPS - 1, True)
                    for half in range(2):
                        v.wait_ge(sem("a_att_turned"), half * KD + 2)
                        v.tensor_copy(attT[:, 1, half * S:(half + 1) * S],
                                      bank[half * KD + 1][:, :]).then_inc(sem("a_attT_dve"), 1)
                    v.wait_ge(sem("a_res"), 16)
                    for t in range(NT):
                        v.wait_ge(sem("a_oproj"), t + 1)
                        v.tensor_tensor(pre[:, t, :], bank[4 + t % 4][:, 0:D], res[:, t, :],
                                        ALU.add).then_inc(sem("a_pre"), 1)
                        v.wait_ge(sem("a_pre"), t + 1)
                        norm_stats(v, own, t, pre)
                    norm_apply(v, own, 1, pre, res)
                    own.sync()
                    for t in range(NT):
                        norm_stats(v, own, t, res)
                    norm_apply(v, own, 2, res, nrm, sem("a_nrm"))
                    v.wait_ge(sem("consts2"), 96)
                    evac_transposed(v, 1, sem("a_turn2"), sem("a_xT"), ln1w, ln1b)

                @blk.gpsimd
                def _(pool):
                    pool.wait_ge(sem("power"), 1)
                    pool_rstd(pool, 1)
                    pool_rstd(pool, 2)

        lay = ExitStack()
        with lay:
            wqk = sb("b_wqk", [P, 2, KD, P], ctx=lay)
            wv = sb("b_wv", [P, KD, P], ctx=lay)
            wo = sb("b_wo", [P, B_H, D], ctx=lay)
            rope = sb("b_rope", [P, 2, 2, S], ctx=lay)
            bqk = sb("b_bqk", [P, 2, 2, B_H], ctx=lay)
            bv = sb("b_bv", [P, B_H], ctx=lay)
            bo = sb("b_bo", [P, D], ctx=lay)
            part = [sb(f"b_part{i}", [P, 2, S], ctx=lay) for i in range(2)]
            qk = [[sb(f"b_qk{b}{c}", [P, S], ctx=lay) for c in range(2)] for b in range(B)]
            val = sb("b_val", [P, NT, B_HD], ctx=lay)
            pr = [sb(f"b_pr{i}", [P, S], ctx=lay) for i in range(3)]
            prT = [sb(f"b_prT{b}", [P, QT, S], ctx=lay) for b in range(B)]
            attT = sb("b_attT", [P, B_H, T], ctx=lay)
            hb = sb("b_hb", [P, NT, D], ctx=lay)
            nmax = sb("b_nmax", [P, B_STEPS], ctx=lay)
            ssum = sb("b_ssum", [P, B_STEPS], ctx=lay)
            rsum = sb("b_rsum", [P, B_STEPS], ctx=lay)
            sc, tp, ob, xb = bank[0:3], bank[3:5], bank[5], bank[6:8]
            CHUNKS = [(b, c) for b in range(B) for c in range(2)]

            with nc.Block() as blk:
                @blk.sync
                def _(sp):
                    sp.dma_start(wqk[:, :, :, :], a["b_wqk"][0]).then_inc(sem("b_wqk"), 16)
                    sp.dma_start(wv[:, :, :], a["b_wv"][0]).then_inc(sem("b_wv"), 16)
                    sp.dma_start(rope[:, :, :, :], a["b_rope"]).then_inc(sem("b_rope_in"), 16)
                    sp.dma_start(bqk[:, :, :, :], a["b_bqk"]).then_inc(sem("b_rope_in"), 16)
                    sp.dma_start(bv[:, :], a["b_bv"]).then_inc(sem("b_bv"), 16)
                    sp.dma_start(bo[:, :], a["b_bo"].partition_broadcast(P)).then_inc(sem("b_bo"), 16)
                    sp.dma_start(wo[:, :, :], a["b_wo"].rearrange("(h p) n -> p h n", p=P)).then_inc(sem("b_wo"), 16)
                    with sp.Fori(1, B_H) as h:
                        src_qk = a["b_wqk"][ds(h, 1), :, :, :, :].rearrange("a p c k n -> p (a c k) n")
                        src_v = a["b_wv"][ds(h, 1), :, :, :].rearrange("a p k n -> p (a k) n")
                        sp.wait_ge(sem("b_proj"), h * 4)
                        sp.dma_start(wqk[:, :, :, :].rearrange("p c k n -> p (c k) n"), src_qk).then_inc(sem("b_wqk"), 16)
                        sp.wait_ge(sem("b_vproj"), h * 2)
                        sp.dma_start(wv[:, :, :], src_v).then_inc(sem("b_wv"), 16)

                @blk.tensor
                def _(pe):
                    def project(h, n):
                        b, c = CHUNKS[n]
                        if n == 0:
                            pe.wait_ge(sem("b_wqk"), h * 16 + 16)
                        if n == 1:
                            pe.wait_ge(sem("b_val"), h * 2)
                        if n >= 2:
                            pe.wait_ge(sem("b_parts"), h * 12 + 3 * (n - 1))
                        for kt in range(KD):
                            ins = pe.matmul(xb[n % 2][:, :], wqk[:, c, kt, :], xT[:, kt, b * S:(b + 1) * S],
                                            start=(kt == 0), stop=(kt == KD - 1))
                        ins.then_inc(sem("b_proj"), 1)

                    def values(h, b):
                        if b == 0:
                            pe.wait_ge(sem("b_wv"), h * 16 + 16)
                        pe.wait_ge(sem("b_parts"), h * 12 + (9 + 3 * b))
                        for j in range(QT):
                            for kt in range(KD):
                                ins = pe.matmul(xb[b][:, j * P:(j + 1) * P],
                                                xT[:, kt, (b * QT + j) * P:(b * QT + j + 1) * P], wv[:, kt, :],
                                                start=(kt == 0), stop=(kt == KD - 1))
                        ins.then_inc(sem("b_vproj"), 1)

                    def scores(h, s):
                        b, i = s // QT, s % QT
                        if i == 0:
                            pe.wait_ge(sem("b_qk"), h * 4 + 2 * (b + 1))
                        w = (i + 1) * P
                        pe.matmul(sc[s % 3][:, 0:w], qk[b][0][:, i * P:w], qk[b][1][:, 0:w], start=True, stop=False)
                        pe.matmul(sc[s % 3][:, i * P:w], ident_bf[:, :], mask_bf[:, :],
                                  start=False, stop=True).then_inc(sem("b_scores"), 1)

                    def turn(h, s):
                        pe.wait_ge(sem("b_pr"), h * B_STEPS + (s + 1))
                        if s >= 2:
                            pe.wait_ge(sem("b_prT"), h * B_STEPS + (s - 1))
                        for j in range(s % QT + 1):
                            ins = pe.transpose(tp[s % 2][:, j * P:(j + 1) * P], pr[s % 3][:, j * P:(j + 1) * P],
                                               ident[:, :])
                        ins.then_inc(sem("b_turned"), 1)

                    def weigh(h, b):
                        pe.wait_ge(sem("b_prT"), h * B_STEPS + QT * (b + 1))
                        pe.wait_ge(sem("b_val"), h * 2 + (b + 1))
                        pe.wait_ge(sem("b_out"), h * 2 + b)
                        for j in range(QT):
                            ins = pe.matmul(ob[:, j * P:S], val[:, b * QT + j, :], prT[b][:, j, j * P:S],
                                            start=(j == 0), stop=(j == QT - 1))
                        ins.then_inc(sem("b_weighed"), 1)

                    def head(h, last):
                        values(h, 0)
                        values(h, 1)
                        for s in range(B_STEPS):
                            scores(h, s)
                            if s >= 2:
                                turn(h, s - 2)
                            if s == QT + 2:
                                weigh(h, 0)
                        for n in range(2):
                            if not last:
                                project(h + 1, n)
                            turn(h, B_STEPS - 2 + n)
                        if not last:
                            project(h + 1, 2)
                            project(h + 1, 3)
                        weigh(h, 1)

                    for n in range(4):
                        project(0, n)
                    with pe.Fori(0, B_H - 1) as h:
                        head(h, False)
                    head(B_H - 1, True)

                    pe.wait_ge(sem("b_wo"), 16)
                    pe.wait_ge(sem("b_out"), 2 * B_H)
                    for t in range(NT):
                        if t >= 4:
                            pe.wait_ge(sem("b_h"), t - 3)
                        for h in range(B_H):
                            ins = pe.matmul(bank[t % 4][:, 0:D], attT[:, h, t * P:(t + 1) * P], wo[:, h, :],
                                            start=(h == 0), stop=(h == B_H - 1))
                        ins.then_inc(sem("b_oproj"), 1)
                    pe.wait_ge(sem("b_h"), NT)
                    transpose_tokens(pe, nrm, sem("b_nrm"), sem("b_turn2"))

                @blk.scalar
                def _(act):
                    def out_head(h, b):
                        act.wait_ge(sem("b_weighed"), h * 2 + (b + 1))
                        act.wait_ge(sem("b_bv"), 16)
                        act.activation(attT[:, ds(h, 1), b * S:(b + 1) * S].rearrange("p a s -> p (a s)"), ob[:, :],
                                       ACT.Identity, bias=bv[:, ds(h, 1)]).then_inc(sem("b_out"), 1)

                    def head(h, last):
                        for b in range(B):
                            act.wait_ge(sem("b_vproj"), h * 2 + (b + 1))
                            act.activation(val[:, b * QT:(b + 1) * QT, :].rearrange("p t d -> p (t d)"), xb[b][:, :],
                                           ACT.Copy).then_inc(sem("b_val"), 1)
                        for s in range(B_STEPS + 2):
                            if s < B_STEPS:
                                w = (s % QT + 1) * P
                                act.wait_ge(sem("b_max"), h * B_STEPS + (s + 1))
                                if s >= 3:
                                    act.wait_ge(sem("b_turned"), h * B_STEPS + (s - 2))
                                act.activation(pr[s % 3][:, 0:w], sc[s % 3][:, 0:w], ACT.Exp, bias=nmax[:, s:s + 1],
                                               scale=1.0, accum_out=ssum[:, s:s + 1]).then_inc(sem("b_exp"), 1)
                            if s >= 2:
                                b, i = (s - 2) // QT, (s - 2) % QT
                                act.wait_ge(sem("b_turned"), h * B_STEPS + (s - 1))
                                act.activation(prT[b][:, 0:i + 1, i * P:(i + 1) * P],
                                               tp[s % 2][:, 0:(i + 1) * P].rearrange("p (j q) -> p j q", q=P),
                                               ACT.Copy).then_inc(sem("b_prT"), 1)
                            if s == QT + 3:
                                out_head(h, 0)
                        out_head(h, 1)

                    with act.Fori(0, B_H - 1) as h:
                        head(h, False)
                    head(B_H - 1, True)
                    evac_transposed(act, 0, sem("b_turn2"), sem("b_xT"), ln2w, ln2b)

                @blk.vector
                def _(v):
                    own = Order(v, sem("v_own_b"))
                    half = P // 2

                    def rotate(h, n):
                        b, c = CHUNKS[n]
                        x, t = xb[n % 2], part[n % 2]
                        v.wait_ge(sem("b_proj"), h * 4 + (n + 1))
                        if n >= 2:
                            v.wait_ge(sem("b_qk"), h * 4 + (n - 1))
                        v.scalar_tensor_tensor(out=t[:, 0, :], in0=x[:, :], scalar=bqk[:, c, 0, ds(h, 1)],
                                               in1=rope[:, c, 0, :], op0=ALU.add,
                                               op1=ALU.mult).then_inc(sem("b_parts"), 1)
                        for lo, hi in ((0, half), (half, 0)):
                            v.scalar_tensor_tensor(out=t[lo:lo + half, 1, :], in0=x[hi:hi + half, :],
                                                   scalar=bqk[lo:lo + half, c, 1, ds(h, 1)],
                                                   in1=rope[lo:lo + half, c, 1, :], op0=ALU.add,
                                                   op1=ALU.mult).then_inc(sem("b_parts"), 1)

                    def head(h, last):
                        for s in range(B_STEPS + 1):
                            if s < B_STEPS:
                                w = (s % QT + 1) * P
                                v.wait_ge(sem("b_scores"), h * B_STEPS + (s + 1))
                                v.tensor_reduce(nmax[:, s:s + 1], sc[s % 3][:, 0:w], AX.X, ALU.max,
                                                negate=True).then_inc(sem("b_max"), 1)
                            if s >= 1:
                                w = ((s - 1) % QT + 1) * P
                                v.wait_ge(sem("b_exp"), h * B_STEPS + s)
                                v.reciprocal(rsum[:, s - 1:s], ssum[:, s - 1:s]).then_inc(sem("b_rsum"), 1)
                                v.wait_ge(sem("b_rsum"), h * B_STEPS + s)
                                p = pr[(s - 1) % 3][:, 0:w]
                                v.tensor_scalar(p, p, rsum[:, s - 1:s], None, ALU.mult).then_inc(sem("b_pr"), 1)
                        if not last:
                            for n in range(4):
                                rotate(h + 1, n)

                    v.wait_ge(sem("b_rope_in"), 32)
                    for n in range(4):
                        rotate(0, n)
                    with v.Fori(0, B_H - 1) as h:
                        head(h, False)
                    head(B_H - 1, True)
                    v.wait_ge(sem("b_hb"), NT)
                    for t in range(NT):
                        v.wait_ge(sem("b_oproj"), t + 1)
                        v.tensor_tensor(pre[:, t, :], bank[t % 4][:, 0:D], hb[:, t, :],
                                        ALU.add).then_inc(sem("b_h"), 1)
                        v.wait_ge(sem("b_h"), t + 1)
                        norm_stats(v, own, t, pre)
                    norm_apply(v, own, 3, pre, nrm, sem("b_nrm"))
                    evac_transposed(v, 1, sem("b_turn2"), sem("b_xT"), ln2w, ln2b)

                @blk.gpsimd
                def _(pool):
                    def add_up(h):
                        for n, (b, c) in enumerate(CHUNKS):
                            t = part[n % 2]
                            pool.wait_ge(sem("b_parts"), h * 12 + 3 * (n + 1))
                            pool.tensor_tensor(qk[b][c][:, :], t[:, 0, :], t[:, 1, :],
                                               ALU.add).then_inc(sem("b_qk"), 1)

                    add_up(0)
                    pool.wait_ge(sem("b_bo"), 16)
                    for t in range(NT):
                        pool.tensor_tensor(hb[:, t, :], res[:, t, :], bo[:, :], ALU.add).then_inc(sem("b_hb"), 1)
                    with pool.Fori(1, B_H) as h:
                        add_up(h)
                    pool_rstd(pool, 3)

        def mixture(tag, experts, gated, init, k_norm):
            name = f"{tag}_"
            pairs = experts // 2
            n_up = 2 if gated else 1
            lay = ExitStack()
            with lay:
                wr = sb(name + "wr", [P, KD, experts], ctx=lay)
                wup = [sb(f"{name}wup{k}", [P, n_up, KD, F], ctx=lay) for k in range(2)]
                wdn = [sb(f"{name}wdn{k}", [P, KF, D], ctx=lay) for k in range(2)]
                hid = [sb(f"{name}hid{k}", [P, KF, T], ctx=lay) for k in range(2)]
                acc = sb(name + "acc", [P, NT, D], ctx=lay)
                gate = [sb(f"{name}gate{i}", [P, S], ctx=lay) for i in range(2)]
                if not gated:
                    b1 = sb(name + "b1", [P, KF, experts], ctx=lay)
                    b2 = sb(name + "b2", [experts, D], ctx=lay)
                    combT = sb(name + "combT", [experts, T], ctx=lay)
                up, down = bank[0:4], bank[4:8]
                PARTS = [(mt, c) for mt in range(KF) for c in range(B)]
                deep = 2 if gated else 4
                per = 1 if gated else 2

                with nc.Block() as blk:
                    @blk.sync
                    def _(sp):
                        sp.dma_start(wr[:, :, :], a[name + "wr"].rearrange("(k p) e -> p k e", p=P)).then_inc(sem(name + "wr"), 16)
                        if not gated:
                            sp.dma_start(b1[:, :, :], a[name + "b1"]).then_inc(sem(name + "b1"), 16)
                            sp.dma_start(b2[:, :], a[name + "b2"]).then_inc(sem(name + "b2"), 16)
                        for k in range(2):
                            sp.dma_start(wup[k][:, :, :, :], a[name + "wup"][k]).then_inc(sem(f"{name}wup{k}"), 16)
                        for k in range(2):
                            sp.dma_start(wdn[k][:, :, :], a[name + "wdn"][k]).then_inc(sem(f"{name}wdn{k}"), 16)
                        with sp.Fori(1, pairs) as i:
                            for k in range(2):
                                src = a[name + "wup"][ds(i * 2 + k, 1), :, :, :, :].rearrange("a p c k n -> p (a c k) n")
                                sp.wait_ge(sem(name + "up"), i * (8 * n_up) + (4 * n_up * (k - 1)))
                                sp.dma_start(wup[k][:, :, :, :].rearrange("p c k n -> p (c k) n"),
                                             src).then_inc(sem(f"{name}wup{k}"), 16)
                            for k in range(2):
                                src = a[name + "wdn"][ds(i * 2 + k, 1), :, :, :].rearrange("a p k n -> p (a k) n")
                                sp.wait_ge(sem(name + "down"), i * (2 * NT) + NT * (k - 1))
                                sp.dma_start(wdn[k][:, :, :], src).then_inc(sem(f"{name}wdn{k}"), 16)

                    @blk.tensor
                    def _(pe):
                        pe.wait_ge(sem(name + "wr"), 16)
                        for t in range(NT):
                            for kt in range(KD):
                                ins = pe.matmul(bank[0][:, t * experts:(t + 1) * experts],
                                                xT[:, kt, t * P:(t + 1) * P], wr[:, kt, :],
                                                start=(kt == 0), stop=(kt == KD - 1))
                        ins.then_inc(sem(name + "logits"), 1)
                        pe.wait_ge(sem(name + "routed"), 1)
                        if not gated:
                            for t in range(NT):
                                ins = pe.transpose(bank[1 + t // 4][0:experts, t % 4 * P:(t % 4 + 1) * P],
                                                   comb[:, t, 0:experts], ident[:, :])
                            ins.then_inc(sem(name + "comb_turned"), 1)
                            pe.wait_ge(sem(name + "combT"), 1)
                            pe.wait_ge(sem(name + "b2"), 16)
                            for t in range(NT):
                                if t >= 4:
                                    pe.wait_ge(sem(name + "acc"), t - 3)
                                pe.matmul(down[t % 4][:, 0:D], combT[:, t * P:(t + 1) * P], b2[:, :],
                                          start=True, stop=True).then_inc(sem(name + "bias"), 1)

                        def pair(i):
                            for k in range(2):
                                pe.wait_ge(sem(f"{name}wup{k}"), i * 16 + 16)
                                for q, (mt, c) in enumerate(PARTS):
                                    n = 4 * k + q
                                    if n >= deep:
                                        pe.wait_ge(sem(name + "hid"), i * (8 // per) + ((n - deep) // per + 1))
                                    for g in range(n_up):
                                        for kt in range(KD):
                                            ins = pe.matmul(up[(q * n_up + g) % 4][:, :],
                                                            wup[k][:, g, kt, mt * P:(mt + 1) * P],
                                                            xT[:, kt, c * S:(c + 1) * S],
                                                            start=(kt == 0), stop=(kt == KD - 1))
                                        ins.then_inc(sem(name + "up"), 1)
                            for k in range(2):
                                pe.wait_ge(sem(f"{name}wdn{k}"), i * 16 + 16)
                                pe.wait_ge(sem(name + "hid"), i * (8 // per) + 4 // per * (k + 1))
                                for t in range(NT):
                                    pe.wait_ge(sem(name + "acc"), i * (2 * NT) + (NT * (k + 1) + t - 3))
                                    for kt in range(KF):
                                        ins = pe.matmul(down[t % 4][:, 0:D], hid[k][:, kt, t * P:(t + 1) * P],
                                                        wdn[k][:, kt, :], start=(kt == 0), stop=(kt == KF - 1))
                                    ins.then_inc(sem(name + "down"), 1)

                        with pe.Fori(0, pairs) as i:
                            pair(i)
                        if k_norm < 7:
                            pe.wait_ge(sem(name + "acc"), NT * (experts + 1))

                    @blk.scalar
                    def _(act):
                        act.wait_ge(sem(name + "shifted"), 1)
                        act.activation(probs8[:, :, 0:experts], probs8[:, :, 0:experts],
                                       ACT.Exp).then_inc(sem(name + "exp"), 1)
                        if not gated:
                            act.wait_ge(sem(name + "gap"), 1)
                            act.activation(row2[:, :], row1[:, :], ACT.Exp).then_inc(sem(name + "exp"), 1)
                            act.wait_ge(sem(name + "comb_turned"), 1)
                            for n in range(2):
                                ins = act.activation(combT[:, n * S:(n + 1) * S], bank[1 + n][0:experts, :], ACT.Copy)
                            ins.then_inc(sem(name + "combT"), 1)
                            act.wait_ge(sem(name + "b1"), 16)

                        def pair(i):
                            for k in range(2):
                                if gated:
                                    for q in range(4):
                                        act.wait_ge(sem(name + "up"), i * 16 + (8 * k + 2 * q + 1))
                                        act.activation(gate[q % 2][:, :], up[q % 2 * 2], ACT.Silu).then_inc(sem(name + "gate"), 1)
                                else:
                                    for mt in range(KF):
                                        act.wait_ge(sem(name + "up"), i * 8 + (4 * k + 2 * mt + 2))
                                        act.activation(hid[k][:, mt, :],
                                                       psum[:, 2 * mt:2 * mt + 2, :].rearrange("p b s -> p (b s)"), ACT.Gelu,
                                                       bias=b1[:, mt, ds(i * 2 + k, 1)]).then_inc(sem(name + "hid"), 1)

                        with act.Fori(0, pairs) as i:
                            pair(i)

                    @blk.vector
                    def _(v):
                        own = Order(v, sem("v_own_" + tag))
                        pe8 = probs8[:, :, 0:experts]

                        def wide(x, n=experts):
                            return x.unsqueeze(2).to_broadcast([P, NT, n])

                        own.mark(v.memset(probs8[:, :, :], -1.0))
                        v.wait_ge(sem(name + "logits"), 1)
                        logits = bank[0][:, 0:NT * experts].rearrange("p (t e) -> p t e", e=experts)
                        own.mark(v.tensor_reduce(row1[:, :], logits, AX.X, ALU.max))
                        own.sync()
                        v.tensor_tensor(pe8, logits, wide(row1[:, :]), ALU.subtract).then_inc(sem(name + "shifted"), 1)
                        v.wait_ge(sem(name + "exp"), 1)
                        own.mark(v.tensor_reduce(row1[:, :], pe8, AX.X, ALU.add))
                        own.sync()
                        own.mark(v.reciprocal(row2[:, :], row1[:, :]))
                        own.sync()
                        own.mark(v.tensor_tensor(pe8, pe8, wide(row2[:, :]), ALU.mult))
                        own.sync()
                        for t in range(NT):
                            own.mark(v.max(top8[:, t, :], probs8[:, t, :]))
                        own.sync()
                        for t in range(NT):
                            own.mark(v.max_index(idx8[:, t, :], top8[:, t, :], probs8[:, t, :]))
                        if gated:
                            own.mark(v.tensor_tensor(row1[:, :], top8[:, :, 0], top8[:, :, 1], ALU.add))
                            own.sync()
                            own.mark(v.reciprocal(row2[:, :], row1[:, :]))
                            own.sync()
                            own.mark(v.tensor_tensor(wts[:, :, :], top8[:, :, 0:2], wide(row2[:, :], 2), ALU.mult))
                        else:
                            v.tensor_tensor(row1[:, :], top8[:, :, 1], top8[:, :, 0],
                                            ALU.subtract).then_inc(sem(name + "gap"), 1)
                            v.wait_ge(sem(name + "exp"), 2)
                            own.mark(v.tensor_scalar(row1[:, :], row2[:, :], 1.0, None, ALU.add))
                            own.sync()
                            own.mark(v.reciprocal(wts[:, :, 0], row1[:, :]))
                            own.sync()
                            own.mark(v.tensor_tensor(wts[:, :, 1], wts[:, :, 0], row2[:, :], ALU.mult))
                        own.mark(v.tensor_copy(idxf[:, :, :], idx8[:, :, 0:2]))
                        own.sync()
                        experts_row = iota[:, 0:experts].unsqueeze(1).to_broadcast([P, NT, experts])
                        for r, dst in ((0, comb), (1, pick)):
                            x = dst[:, :, 0:experts]
                            own.mark(v.tensor_tensor(x, experts_row, wide(idxf[:, :, r]), ALU.is_equal))
                            own.sync()
                            own.mark(v.tensor_tensor(x, x, wide(wts[:, :, r]), ALU.mult))
                            own.sync()
                        v.tensor_tensor(comb[:, :, 0:experts], comb[:, :, 0:experts], pick[:, :, 0:experts],
                                        ALU.add).then_inc(sem(name + "routed"), 1)
                        v.wait_ge(sem(name + "routed"), 1)
                        init(v, own, acc, down, sem(name + "bias"), sem(name + "acc"))

                        def pair(i):
                            if gated:
                                for k in range(2):
                                    for q, (mt, c) in enumerate(PARTS):
                                        n = 4 * k + q
                                        v.wait_ge(sem(name + "gate"), i * 8 + (n + 1))
                                        v.wait_ge(sem(name + "up"), i * 16 + (2 * n + 2))
                                        v.tensor_tensor(hid[k][:, mt, c * S:(c + 1) * S], up[q % 2 * 2 + 1][:, :],
                                                        gate[q % 2][:, :], ALU.mult).then_inc(sem(name + "hid"), 1)
                            for k in range(2):
                                for t in range(NT):
                                    v.wait_ge(sem(name + "down"), i * (2 * NT) + (NT * k + t + 1))
                                    v.wait_ge(sem(name + "acc"), i * (2 * NT) + (NT * k + t + 1))
                                    v.scalar_tensor_tensor(out=acc[:, t, :], in0=down[t % 4][:, 0:D],
                                                           scalar=comb[:, t, ds(i * 2 + k, 1)], in1=acc[:, t, :],
                                                           op0=ALU.mult, op1=ALU.add).then_inc(sem(name + "acc"), 1)

                        with v.Fori(0, pairs) as i:
                            pair(i)
                        v.wait_ge(sem(name + "acc"), NT * (experts + 1))
                        for t in range(NT):
                            norm_stats(v, own, t, acc)
                        norm_apply(v, own, k_norm, acc, res, sem(name + "normed"))

                    @blk.gpsimd
                    def _(pool):
                        pool_rstd(pool, k_norm)
                        if k_norm == 7:
                            dst = out.rearrange("b s d -> (b s) d").rearrange("(t p) d -> p t d", p=P)
                            for half in range(2):
                                pool.wait_ge(sem(name + "normed"), 4 * (half + 1))
                                pool.dma_start(dst[:, 4 * half:4 * half + 4, :],
                                               res[:, 4 * half:4 * half + 4, :]).then_inc(sem("stored"), 16)
                            pool.wait_ge(sem("stored"), 32)

        def init_b(v, own, acc, down, bias, ready):
            for t in range(NT):
                own.mark(v.tensor_tensor(acc[:, t, :], res[:, t, :], pre[:, t, :], ALU.add))
            for t in range(NT):
                own.sync()
                v.wait_ge(bias, t + 1)
                v.tensor_tensor(acc[:, t, :], down[t % 4][:, 0:D], acc[:, t, :], ALU.add).then_inc(ready, 1)

        mixture("m", MOE_B, False, init_b, 4)

        lay = ExitStack()
        with lay:
            win = sb("c_win", [P, KD, 2 * DI], ctx=lay)
            wx = sb("c_wx", [P, KI, 2 * NS], ctx=lay)
            wdt = sb("c_wdt", [P, KI, P], ctx=lay)
            wout = sb("c_wout", [P, KI, D], ctx=lay)
            cw = sb("c_cw", [P, KI, TAPS], ctx=lay)
            cols = sb("c_cols", [P, 4, KI], ctx=lay)
            alog = sb("c_alog", [P, KI, NS], ctx=lay)
            nega = sb("c_nega", [P, KI, NS], ctx=lay)
            sel = sb("c_sel", [P, 2 * NS, P], BF16, ctx=lay)
            xin = sb("c_xin", [P, KI, B, S + TAPS - 1], ctx=lay)
            gz = sb("c_gz", [P, KI, T], ctx=lay)
            xc = sb("c_xc", [P, KI, T], ctx=lay)
            dt = sb("c_dt", [P, KI, T], ctx=lay)
            du = sb("c_du", [P, KI, T], ctx=lay)
            conv = sb("c_conv", [P, B, S], ctx=lay)
            tmp = sb("c_tmp", [P, T], ctx=lay)
            tmp2 = sb("c_tmp2", [P, T], ctx=lay)
            bc_f = sb("c_bc_f", [2 * NS, T], ctx=lay)
            bc_p = sb("c_bc_p", [2 * NS, T], BF16, ctx=lay)
            bcs = sb("c_bcs", [P, T], BF16, ctx=lay)
            dg = sb("c_dg", [P, KI, P], ctx=lay)
            bs = [sb(f"c_bs{u}", [P, S], ctx=lay) for u in range(2)]
            da = [sb(f"c_da{m}", [P, S], ctx=lay) for m in range(KI)]
            dbu = [sb(f"c_dbu{m}", [P, S], ctx=lay) for m in range(KI)]
            st = [sb(f"c_st{m}", [P, S], ctx=lay) for m in range(KI)]
            hc = [sb(f"c_hc{m}", [P, S], ctx=lay) for m in range(KI)]
            ssq = sb("c_ssq", [P, NT], ctx=lay)
            yacc, bb, cb = bank[0:4], bank[4:6], bank[6:8]
            CB, DTW, DTB, DP = range(4)

            with nc.Block() as blk:
                @blk.sync
                def _(sp):
                    sp.dma_start(win[:, :, :], a["c_win"].rearrange("(k p) n -> p k n", p=P)).then_inc(sem("c_win"), 16)
                    sp.dma_start(cw[:, :, :], a["c_cw"]).then_inc(sem("c_small"), 16)
                    sp.dma_start(cols[:, :, :], a["c_cols"]).then_inc(sem("c_small"), 16)
                    sp.dma_start(alog[:, :, :], a["c_alog"]).then_inc(sem("c_small"), 16)
                    sp.dma_start(wx[:, :, :], a["c_wx"].rearrange("(k p) n -> p k n", p=P)).then_inc(sem("c_wx"), 16)
                    sp.dma_start(wdt[:, :, :], a["c_wdt"].rearrange("(k p) n -> p k n", p=P)).then_inc(sem("c_wx"), 16)
                    sp.dma_start(sel[:, :, :], a["c_sel"]).then_inc(sem("c_sel"), 16)
                    sp.dma_start(wout[:, :, :], a["c_wout"].rearrange("(k p) n -> p k n", p=P)).then_inc(sem("c_wout"), 16)

                @blk.tensor
                def _(pe):
                    transpose_tokens(pe, nrm, sem("c_nrm"), sem("c_turn"), base=0)
                    pe.wait_ge(sem("c_win"), 16)
                    pe.wait_ge(sem("c_xT"), 4)
                    for n in range(16):
                        m, b = n // 2, n % 2
                        if n >= 4:
                            pe.wait_ge(sem("c_in_out"), n - 3)
                        for kt in range(KD):
                            ins = pe.matmul(bank[4 + n % 4][:, :], win[:, kt, m * P:(m + 1) * P],
                                            xT[:, kt, b * S:(b + 1) * S], start=(kt == 0), stop=(kt == KD - 1))
                        ins.then_inc(sem("c_in"), 1)
                    pe.wait_ge(sem("c_wx"), 32)
                    pe.wait_ge(sem("c_xc"), KI)
                    for b in range(B):
                        for kt in range(KI):
                            ins = pe.matmul(bank[b][0:2 * NS, :], wx[:, kt, :], xc[:, kt, b * S:(b + 1) * S],
                                            start=(kt == 0), stop=(kt == KI - 1))
                        ins.then_inc(sem("c_bc"), 1)
                        for kt in range(KI):
                            ins = pe.matmul(bank[2 + b][:, :], wdt[:, kt, :], xc[:, kt, b * S:(b + 1) * S],
                                            start=(kt == 0), stop=(kt == KI - 1))
                        ins.then_inc(sem("c_step"), 1)

                    def spread(b, n, u):
                        cols_b = bcs[:, b * S:(b + 1) * S]
                        pe.matmul(bb[u][:, :], sel[:, ds(n, 1), :].rearrange("p a m -> p (a m)"), cols_b,
                                  start=True, stop=True).then_inc(sem("c_bb"), 1)
                        pe.matmul(cb[u][:, :], sel[:, ds(n + NS, 1), :].rearrange("p a m -> p (a m)"), cols_b,
                                  start=True, stop=True).then_inc(sem("c_cb"), 1)

                    def total(b, n, stop=False):
                        for m in range(KI):
                            pe.wait_ge(sem("c_hc"), n * KI + (b * NS * KI + KI + m + 1))
                            pe.matmul(yacc[m][:, :], ident[:, :], hc[m][:, :], start=False,
                                      stop=stop).then_inc(sem("c_sum"), 1)

                    def two(b, j, last):
                        for u in range(2):
                            total(b, j * 2 + u, last and u == 1)
                            if not last:
                                pe.wait_ge(sem("c_bs"), j * 2 + (b * NS + u + 1))
                                spread(b, j * 2 + (u + 2), u)

                    pe.wait_ge(sem("c_split"), 1)
                    pe.wait_ge(sem("c_sel"), 16)
                    pe.wait_ge(sem("c_hc"), KI)
                    pe.wait_ge(sem("c_v"), 2 * KI)
                    for b in range(B):
                        if b:
                            pe.wait_ge(sem("c_y"), KI)
                        spread(b, 0, 0)
                        spread(b, 1, 1)
                        for m in range(KI):
                            pe.matmul(yacc[m][:, :], dg[:, m, :], xc[:, m, b * S:(b + 1) * S], start=True,
                                      stop=False).then_inc(sem("c_sum"), 1)
                        with pe.Fori(0, NS // 2 - 1) as j:
                            two(b, j, False)
                        two(b, NS // 2 - 1, True)
                    pe.wait_ge(sem("c_wout"), 16)
                    pe.wait_ge(sem("c_y"), 2 * KI)
                    for t in range(NT):
                        if t >= 4:
                            pe.wait_ge(sem("c_pre"), t - 3)
                        for kt in range(KI):
                            ins = pe.matmul(bank[t % 4][:, 0:D], gz[:, kt, t * P:(t + 1) * P], wout[:, kt, :],
                                            start=(kt == 0), stop=(kt == KI - 1))
                        ins.then_inc(sem("c_oproj"), 1)
                    pe.wait_ge(sem("c_pre"), NT)
                    transpose_tokens(pe, res, sem("c_res"), sem("c_turn2"))

                @blk.scalar
                def _(act):
                    for t in range(NT):
                        act.activation(pre[:, t, :], res[:, t, :], ACT.Square,
                                       accum_out=ssq[:, t:t + 1]).then_inc(sem("c_ssq"), 1)
                    evac_transposed(act, 0, sem("c_turn"), sem("c_xT"), rmsw, None)
                    for n in range(16):
                        m, b = n // 2, n % 2
                        act.wait_ge(sem("c_in"), n + 1)
                        if m < KI:
                            act.activation(xin[:, m, b, TAPS - 1:], bank[4 + n % 4][:, :],
                                           ACT.Copy).then_inc(sem("c_in_out"), 1)
                        else:
                            act.activation(gz[:, m - KI, b * S:(b + 1) * S], bank[4 + n % 4][:, :],
                                           ACT.Silu).then_inc(sem("c_in_out"), 1)
                    for m in range(KI):
                        act.wait_ge(sem("c_conv"), m + 1)
                        act.activation(xc[:, m, :], conv[:, :, :].rearrange("p b s -> p (b s)"),
                                       ACT.Silu).then_inc(sem("c_xc"), 1)
                    act.wait_ge(sem("c_small"), 48)
                    act.activation(nega[:, :, :], alog[:, :, :], ACT.Exp).then_inc(sem("c_ea"), 1)
                    for m in range(KI):
                        act.wait_ge(sem("c_nabs"), m + 1)
                        act.activation(tmp2[:, :], tmp[:, :], ACT.Exp).then_inc(sem("c_e"), 1)
                        act.wait_ge(sem("c_e"), m + 1)
                        act.activation(tmp2[:, :], tmp2[:, :], ACT.Ln, bias=1.0).then_inc(sem("c_l"), 1)

                    def copy_b(b, n, u):
                        act.wait_ge(sem("c_bb"), n + (b * NS + 1))
                        act.activation(bs[u][:, :], bb[u][:, :], ACT.Copy).then_inc(sem("c_bs"), 1)

                    def two(b, j, last):
                        for u in range(2):
                            if not (last and u == 1):
                                act.wait_ge(sem("c_dbu"), j * (2 * KI) + (b * NS * KI + KI * u))
                                copy_b(b, j * 2 + (u + 1), (u + 1) % 2)
                            for m in range(KI):
                                act.wait_ge(sem("c_scan"), j * (2 * KI) + (b * NS * KI + KI * u + m + 1))
                                act.wait_ge(sem("c_nega"), 1)
                                act.activation(da[m][:, :], dt[:, m, b * S:(b + 1) * S], ACT.Exp,
                                               scale=nega[:, m, ds(j * 2 + u, 1)]).then_inc(sem("c_da"), 1)

                    act.wait_ge(sem("c_dt"), KI)
                    for b in range(B):
                        if b:
                            act.wait_ge(sem("c_dbu"), NS * KI)
                        copy_b(b, 0, 0)
                        with act.Fori(0, NS // 2 - 1) as j:
                            two(b, j, False)
                        two(b, NS // 2 - 1, True)
                    evac_transposed(act, 0, sem("c_turn2"), sem("c_xT2"))

                @blk.vector
                def _(v):
                    own = Order(v, sem("v_own_c"))
                    own.mark(v.memset(xin[:, :, :, 0:TAPS - 1], 0.0))
                    own.mark(v.memset(bcs[:, :].bitcast(F32), 0.0))
                    v.wait_ge(sem("c_ssq"), NT)
                    v.tensor_scalar(var_eps[:, :], ssq[:, :], 1.0 / D, EPS, ALU.mult,
                                    ALU.add).then_inc(sem("var_ready"), 1)
                    v.wait_ge(sem("rstd_ready"), 5)
                    for t in range(NT):
                        v.tensor_scalar(nrm[:, t, :], res[:, t, :], rstd[:, t:t + 1], None,
                                        ALU.mult).then_inc(sem("c_nrm"), 1)
                    for half in range(2):
                        v.wait_ge(sem("c_turn"), half * KD + 2)
                        v.tensor_scalar(xT[:, 1, half * S:(half + 1) * S], bank[half * KD + 1][:, :],
                                        rmsw[:, 1:2], None, ALU.mult).then_inc(sem("c_xT"), 1)
                    v.wait_ge(sem("c_small"), 48)
                    for m in range(KI):
                        v.wait_ge(sem("c_in_out"), 2 * m + 2)
                        if m:
                            v.wait_ge(sem("c_xc"), m)
                        own.mark(v.tensor_scalar(conv[:, :, :], xin[:, m, :, 0:S], cw[:, m, 0:1], cols[:, CB, m:m + 1],
                                                 ALU.mult, ALU.add))
                        for k in range(1, TAPS):
                            own.sync()
                            ins = v.scalar_tensor_tensor(out=conv[:, :, :], in0=xin[:, m, :, k:k + S],
                                                         scalar=cw[:, m, k:k + 1], in1=conv[:, :, :],
                                                         op0=ALU.mult, op1=ALU.add)
                            if k < TAPS - 1:
                                own.mark(ins)
                            else:
                                ins.then_inc(sem("c_conv"), 1)
                    for m in range(KI):
                        v.tensor_scalar(dg[:, m, :], ident[:, :], cols[:, DP, m:m + 1], None,
                                        ALU.mult).then_inc(sem("c_hc"), 1)
                    v.wait_ge(sem("c_ea"), 1)
                    v.tensor_scalar(nega[:, :, :], nega[:, :, :], -1.0, None, ALU.mult).then_inc(sem("c_nega"), 1)
                    for b in range(B):
                        half = slice(b * S, (b + 1) * S)
                        v.wait_ge(sem("c_bc"), b + 1)
                        own.mark(v.tensor_copy(bcs[0:32, half], bank[b][0:32, :]))
                        own.sync()
                        own.mark(v.tensor_tensor(bc_f[:, half], bank[b][0:32, :], bcs[0:32, half], ALU.subtract))
                        own.sync()
                        own.mark(v.tensor_copy(bc_p[:, half], bc_f[:, half]))
                        own.sync()
                        own.mark(v.tensor_tensor(bc_f[:, half], bc_f[:, half], bc_p[:, half], ALU.subtract))
                        own.mark(v.tensor_copy(bcs[32:64, half], bc_p[:, half]))
                        own.sync()
                        own.mark(v.tensor_copy(bcs[64:96, half], bc_f[:, half]))
                    own.sync()
                    v.sem_inc(sem("c_split"), 1)
                    for m in range(KI):
                        for b in range(B):
                            v.wait_ge(sem("c_step"), b + 1)
                            v.tensor_scalar(dt[:, m, b * S:(b + 1) * S], bank[2 + b][:, :], cols[:, DTW, m:m + 1],
                                            cols[:, DTB, m:m + 1], ALU.mult, ALU.add).then_inc(sem("c_v"), 1)
                    for m in range(KI):
                        v.wait_ge(sem("c_v"), 2 * (m + 1))
                        if m:
                            v.wait_ge(sem("c_l"), m)
                        v.scalar_tensor_tensor(out=tmp[:, :], in0=dt[:, m, :], scalar=-1.0, in1=dt[:, m, :],
                                               op0=ALU.mult, op1=ALU.min).then_inc(sem("c_nabs"), 1)
                        v.wait_ge(sem("c_l"), m + 1)
                        v.scalar_tensor_tensor(out=dt[:, m, :], in0=dt[:, m, :], scalar=0.0, in1=tmp2[:, :],
                                               op0=ALU.max, op1=ALU.add).then_inc(sem("c_dt"), 1)
                        v.wait_ge(sem("c_dt"), m + 1)
                        v.tensor_tensor(du[:, m, :], dt[:, m, :], xc[:, m, :], ALU.mult).then_inc(sem("c_scan"), 1)

                    def scan(b, n, m):
                        done = b * NS * KI + m + 1
                        v.wait_ge(sem("c_da"), n * KI + done)
                        v.wait_ge(sem("c_dbu"), n * KI + done)
                        v.wait_ge(sem("c_hc"), n * KI + done)
                        v.tensor_tensor_scan(st[m][:, :], da[m][:, :], dbu[m][:, :], 0.0, ALU.mult,
                                             ALU.add).then_inc(sem("c_scan"), 1)

                    def times_c(b, n, m, u):
                        done = b * NS * KI + m + 1
                        v.wait_ge(sem("c_scan"), n * KI + (KI + done))
                        if m == 0:
                            v.wait_ge(sem("c_cb"), n + (b * NS + 1))
                        v.wait_ge(sem("c_sum"), n * KI + (b * (NS + 1) * KI + m + 1))
                        v.tensor_tensor(hc[m][:, :], st[m][:, :], cb[u][:, :], ALU.mult).then_inc(sem("c_hc"), 1)

                    def two(b, j):
                        for u in range(2):
                            n = j * 2 + u
                            scan(b, n, 0)
                            for m in range(1, KI):
                                scan(b, n, m)
                                times_c(b, n, m - 1, u)
                            times_c(b, n, KI - 1, u)

                    for b in range(B):
                        with v.Fori(0, NS // 2) as j:
                            two(b, j)
                        for m in range(KI):
                            v.wait_ge(sem("c_sum"), (NS + 1) * KI * (b + 1) - KI + m + 1)
                            z = gz[:, m, b * S:(b + 1) * S]
                            v.tensor_tensor(z, yacc[m][:, :], z, ALU.mult).then_inc(sem("c_y"), 1)
                    for t in range(NT):
                        v.wait_ge(sem("c_oproj"), t + 1)
                        v.scalar_tensor_tensor(out=pre[:, t, :], in0=res[:, t, :], scalar=2.0,
                                               in1=bank[t % 4][:, 0:D], op0=ALU.mult,
                                               op1=ALU.add).then_inc(sem("c_pre"), 1)
                        v.wait_ge(sem("c_pre"), t + 1)
                        norm_stats(v, own, t, pre)
                    norm_apply(v, own, 6, pre, res, sem("c_res"))
                    evac_transposed(v, 1, sem("c_turn2"), sem("c_xT2"))

                @blk.gpsimd
                def _(pool):
                    pool_rstd(pool, 5)

                    def inputs(b, n, u):
                        pool.wait_ge(sem("c_bs"), n + (b * NS + 1))
                        for m in range(KI):
                            pool.wait_ge(sem("c_scan"), n * KI + (b * NS * KI + m + 1))
                            pool.tensor_tensor(dbu[m][:, :], du[:, m, b * S:(b + 1) * S], bs[u][:, :],
                                               ALU.mult).then_inc(sem("c_dbu"), 1)

                    pool.wait_ge(sem("c_scan"), KI)
                    for b in range(B):
                        with pool.Fori(0, NS // 2) as j:
                            for u in range(2):
                                inputs(b, j * 2 + u, u)
                    pool_rstd(pool, 6)

        def init_d(v, own, acc, down, bias, ready):
            for t in range(NT):
                v.tensor_copy(acc[:, t, :], res[:, t, :]).then_inc(ready, 1)

        mixture("d", MOE_D, True, init_d, 7)


def kernel(**inputs):
    import numpy as np
    import concourse.bacc as bacc
    from concourse import mybir as _mybir
    from concourse.bass_utils import run_bass_kernel_spmd as run

    x = {k: np.asarray(v) for k, v in inputs.items()}
    bf16 = _mybir.dt.np(_mybir.dt.bfloat16) if hasattr(_mybir.dt, "np") else None
    import ml_dtypes
    bf16 = ml_dtypes.bfloat16
    f32 = np.float32
    arrays = {}

    def put(name, v):
        arrays["in_" + name] = np.ascontiguousarray(v)

    tok = x["L0_attn_hidden_states"].reshape(T, D)
    put("x", tok)
    put("xT", tok.T)

    def by_part(v):
        return v.reshape(-1, P).T

    put("ident", np.eye(P, dtype=f32))
    put("ident_bf", np.eye(P).astype(bf16))
    put("mask_bf", np.where(np.arange(P)[None, :] > np.arange(P)[:, None], -1e30, 0.0).astype(bf16))
    put("iota", np.broadcast_to(np.arange(8, dtype=f32), (P, 8)))
    sel = np.zeros((P, 2 * NS, P), f32)
    for n in range(2 * NS):
        sel[[n, 32 + n, 64 + n], n, :] = 1.0
    put("c_sel", sel.astype(bf16))
    inv = f32(1.0) / np.power(f32(10000.0), np.arange(0, B_HD, 2, dtype=f32) / f32(B_HD)).astype(f32)
    ang = np.arange(S, dtype=f32)[:, None] * inv[None, :]
    cos = np.concatenate([np.cos(ang), np.cos(ang)], 1).T.astype(f32)
    sin = np.concatenate([-np.sin(ang), np.sin(ang)], 1).T.astype(f32)
    sc = 1.0 / np.sqrt(float(B_HD))
    put("b_rope", np.stack([np.stack([cos * sc, sin * sc]), np.stack([cos, sin])]).transpose(2, 0, 1, 3).astype(f32))

    w = x["L0_attn_w_qkv"].reshape(3, A_GROUPS, A_G, A_HD, KD, P)
    wqk = np.zeros((A_GROUPS, P, 2, KD, A_G, 32), f32)
    wqk[..., 0:A_HD] = w[0:2].transpose(1, 5, 0, 4, 2, 3)
    put("a_wqk", wqk.reshape(A_GROUPS, P, 2, KD, P))
    put("a_wv", x["L0_attn_w_qkv"][2 * D:3 * D].T)
    put("a_wo", x["L0_attn_w_o"].T)
    for n, k in (("ln1w", "ln1_w"), ("ln1b", "ln1_b"), ("ln2w", "ln2_w"), ("ln2b", "ln2_b")):
        put(n, by_part(x["L0_ffn_" + k]))
    wq, wk, wv = (x["L0_ffn_" + n].reshape(KD, P, B_H, B_HD) for n in ("wq", "wk", "wv"))
    put("b_wqk", np.stack([wq, wk]).transpose(3, 2, 0, 1, 4))
    put("b_wv", wv.transpose(2, 1, 0, 3))
    bq, bk = (x["L0_ffn_" + n].reshape(B_H, 2, P // 2) for n in ("bq", "bk"))
    both = np.stack([bq, bk])
    put("b_bqk", np.stack([both, both[:, :, ::-1]], 1).reshape(2, 2, B_H, P).transpose(3, 0, 1, 2))
    put("b_bv", by_part(x["L0_ffn_bv"]))
    put("b_bo", x["L0_ffn_bo"])
    put("b_wo", x["L0_ffn_wo"])
    put("m_wr", x["L0_ffn_w_gate"])
    put("m_wup", x["L0_ffn_we1"].reshape(MOE_B, 1, KD, P, F).transpose(0, 3, 1, 2, 4))
    put("m_wdn", x["L0_ffn_we2"].reshape(MOE_B, KF, P, D).transpose(0, 2, 1, 3))
    put("m_b1", x["L0_ffn_be1"].reshape(MOE_B, KF, P).transpose(2, 1, 0))
    put("m_b2", x["L0_ffn_be2"])
    put("rmsw", by_part(x["L1_attn_norm_w"]))
    put("c_win", x["L1_attn_in_proj_w"].T)
    put("c_wx", x["L1_attn_x_proj_w"][0:2 * NS].T)
    put("c_wdt", np.broadcast_to(x["L1_attn_x_proj_w"][2 * NS][:, None], (DI, P)))
    put("c_wout", x["L1_attn_out_proj_w"].T)
    put("c_cw", x["L1_attn_conv_w"].reshape(KI, P, TAPS).transpose(1, 0, 2))
    put("c_cols", np.stack([by_part(x["L1_attn_conv_b"]), by_part(x["L1_attn_dt_w"].reshape(-1)),
                            by_part(x["L1_attn_dt_b"]), by_part(x["L1_attn_D_param"])], 1))
    put("c_alog", x["L1_attn_A_log"].reshape(KI, P, NS).transpose(1, 0, 2))
    put("d_wr", x["L1_ffn_Wr"])
    put("d_wup", np.stack([x["L1_ffn_Wg"], x["L1_ffn_Wu"]], 1).reshape(MOE_D, 2, KD, P, F).transpose(0, 3, 1, 2, 4))
    put("d_wdn", x["L1_ffn_Wd"].reshape(MOE_D, KF, P, D).transpose(0, 2, 1, 3))

    nc = bacc.Bacc("TRN2", target_bir_lowering=False, num_devices=1)
    aps = {n[3:]: nc.dram_tensor(n, v.shape, _mybir.dt.from_np(v.dtype), kind="ExternalInput").ap()
           for n, v in arrays.items()}
    out = nc.dram_tensor("out_0_dram", (B, S, D), _mybir.dt.float32, kind="ExternalOutput").ap()
    build_program(nc, aps, out)
    r = run(nc, [arrays], core_ids=[0])
    return r.results[0]["out_0_dram"]
```

```python
from contextlib import ExitStack

import concourse.bass as bass
from concourse import mybir

ALU = mybir.AluOpType
ACT = mybir.ActivationFunctionType
AX = mybir.AxisListType
F32 = mybir.dt.float32
F32R = mybir.dt.float32r
BF16 = mybir.dt.bfloat16
U32 = mybir.dt.uint32
ds = bass.ds

P = 128
D = 256
KD = D // P
T = 1024
NT = T // P
B = 2
S = T // B
QT = S // P
EPS = 1e-5

A_H, A_HD = 16, 16
A_G = 4
A_GROUPS = A_H // A_G
A_STEPS = B * A_G * QT
B_H, B_HD = 16, 128
B_STEPS = B * QT
MOE_B, MOE_D = 4, 8
F = 256
KF = F // P
DI = 512
KI = DI // P
NS = 16
TAPS = 4


class Order:

    def __init__(self, eng, sem, base=0):
        self.eng, self.sem, self.base, self.n = eng, sem, base, 0

    def mark(self, ins):
        ins.then_inc(self.sem, 1)
        self.n += 1

    def sync(self, behind=0):
        self.eng.wait_ge(self.sem, self.base + (self.n - behind))


def build_program(nc, a, out):
    top = ExitStack()
    with top:
        def sb(name, shape, dt=F32, ctx=top):
            return ctx.enter_context(nc.sbuf_tensor(name, shape, dt))

        sems = {}

        def sem(name):
            if name not in sems:
                sems[name] = top.enter_context(nc.semaphore(name))
            return sems[name]

        psum = top.enter_context(nc.psum_tensor("psum", [P, 8, 512], F32))
        bank = [psum[:, i, :] for i in range(8)]

        ident = sb("ident", [P, P])
        ident_bf = sb("ident_bf", [P, P], BF16)
        mask_bf = sb("mask_bf", [P, P], BF16)
        iota = sb("iota", [P, 8])
        power = sb("power", [P, NT])
        res = sb("res", [P, NT, D])
        pre = sb("pre", [P, NT, D])
        nrm = sb("nrm", [P, NT, D])
        xT = sb("xT", [P, KD, T])
        xh, xl = sb("xh", [P, KD, T], F32R), sb("xl", [P, KD, T], F32R)
        up_in = [sb(f"up_in{k}", [P, 2, KD, F]) for k in range(2)]
        dn_in = [sb(f"dn_in{k}", [P, KF, D]) for k in range(2)]
        stats = sb("stats", [P, NT, 6])
        mv = sb("mv", [P, NT, 2])
        var_eps = sb("var_eps", [P, NT])
        rstd = sb("rstd", [P, NT])
        ln1w, ln1b = sb("ln1w", [P, KD]), sb("ln1b", [P, KD])
        ln2w, ln2b = sb("ln2w", [P, KD]), sb("ln2b", [P, KD])
        rmsw = sb("rmsw", [P, KD])
        probs8 = sb("probs8", [P, NT, 8])
        top8 = sb("top8", [P, NT, 8])
        idx8 = sb("idx8", [P, NT, 8], U32)
        idxf = sb("idxf", [P, NT, 2])
        comb = sb("comb", [P, NT, 8])
        pick = sb("pick", [P, NT, 8])
        row1 = sb("row1", [P, NT])
        row2 = sb("row2", [P, NT])
        wts = sb("wts", [P, NT, 2])


        def load_first(tag, sp, gated):
            name = tag + "_"
            n_up = 2 if gated else 1
            for k in range(2):
                sp.dma_start(up_in[k][:, 0:n_up, :, :], a[name + "wup"][k]).then_inc(sem(f"{name}wup{k}"), 16)
            for k in range(2):
                sp.dma_start(dn_in[k][:, :, :], a[name + "wdn"][k]).then_inc(sem(f"{name}wdn{k}"), 16)

        def norm_stats(v, own, t, src):
            own.mark(v.bn_stats(stats[:, t, :], src[:, t, :]))
            own.sync()
            own.mark(v.bn_aggr(mv[:, t, :], stats[:, t, :]))

        def norm_apply(v, own, k, src, dst, ready=None):
            own.sync()
            v.tensor_scalar(var_eps[:, :], mv[:, :, 1], EPS, None, ALU.add).then_inc(sem("var_ready"), 1)
            v.wait_ge(sem("rstd_ready"), k)
            for t in range(NT):
                ins = v.tensor_scalar(dst[:, t, :], src[:, t, :], mv[:, t, 0:1], rstd[:, t:t + 1],
                                      ALU.subtract, ALU.mult)
                if ready is not None:
                    ins.then_inc(ready, 1)
                else:
                    own.mark(ins)

        def pool_rstd(pool, k):
            pool.wait_ge(sem("var_ready"), k)
            pool.tensor_tensor(rstd[:, :], var_eps[:, :], power[:, :], ALU.pow).then_inc(sem("rstd_ready"), 1)

        def transpose_tokens(pe, src, src_ready, done, kt_n=KD, base=0):
            for half in range(2):
                for kt in range(kt_n):
                    pe.wait_ge(src_ready, 4 * (half + 1))
                    for j in range(4):
                        ins = pe.transpose(bank[base + half * kt_n + kt][:, j * P:(j + 1) * P],
                                           src[:, 4 * half + j, kt * P:(kt + 1) * P], ident[:, :])
                    ins.then_inc(done, 1)

        def evac_transposed(eng, which, done, ready, scale=None, bias=None):
            for half in range(2):
                eng.wait_ge(done, half * KD + which + 1)
                src = bank[half * KD + which][:, :]
                dst = xT[:, which, half * S:(half + 1) * S]
                w = scale[:, which:which + 1] if scale is not None else 1.0
                b = bias[:, which:which + 1] if bias is not None else 0.0
                if which == 0:
                    ins = eng.activation(dst, src, ACT.Identity, bias=b, scale=w)
                elif scale is None:
                    ins = eng.tensor_copy(dst, src)
                else:
                    ins = eng.tensor_scalar(dst, src, w, b, ALU.mult, ALU.add)
                ins.then_inc(ready, 1)

        lay = ExitStack()
        with lay:
            wqkv = sb("a_wqkv", [P, 3, KD, P], ctx=lay)
            wo = sb("a_wo", [P, A_GROUPS, D], ctx=lay)
            qT = [sb(f"a_qT{b}", [P, S], ctx=lay) for b in range(B)]
            kT = [sb(f"a_kT{b}", [P, A_G, S], ctx=lay) for b in range(B)]
            val = [sb(f"a_val{b}", [P, QT, P], ctx=lay) for b in range(B)]
            attT = sb("a_attT", [P, A_GROUPS, T], ctx=lay)
            pr = [sb(f"a_pr{i}", [P, S], ctx=lay) for i in range(3)]
            prT = [sb(f"a_prT{i}", [P, S], ctx=lay) for i in range(2 * A_G)]
            nmax = sb("a_nmax", [P, A_STEPS], ctx=lay)
            ssum = sb("a_ssum", [P, A_STEPS], ctx=lay)
            rsum = sb("a_rsum", [P, A_STEPS], ctx=lay)
            rwide = [sb(f"a_rwide{b}", [P, QT * A_G, 32], ctx=lay) for b in range(B)]
            rT = sb("a_rT", [P, S], ctx=lay)
            sc, tp, ob, x0, x1 = bank[0:3], bank[3:5], bank[5], bank[6], bank[7]
            HALF = A_STEPS // B

            def step(s):
                return s // HALF, s // A_G % QT, s % A_G

            def on_act(s):
                return s % A_G == A_G - 1


            with nc.Block() as blk:
                @blk.sync
                def _(sp):
                    sp.dma_start(wqkv[:, :, :, :], a["a_wqkv"][0]).then_inc(sem("a_w"), 16)
                    for half in range(2):
                        for kt in range(KD):
                            sp.dma_start(xT[:, kt, half * S:(half + 1) * S],
                                         a["xT"][kt * P:(kt + 1) * P, half * S:(half + 1) * S]).then_inc(sem(f"a_x{half}"), 16)
                    for dst, name in ((ident_bf, "ident_bf"), (mask_bf, "mask_bf"), (ident, "ident")):
                        sp.dma_start(dst[:, :], a[name]).then_inc(sem("consts"), 16)
                    for dst, name in ((ln1w, "ln1w"), (ln1b, "ln1b"), (ln2w, "ln2w"), (ln2b, "ln2b"), (rmsw, "rmsw"),
                                      (iota, "iota")):
                        sp.dma_start(dst[:, :], a[name]).then_inc(sem("consts2"), 16)
                    sp.dma_start(wo[:, :, :], a["a_wo"].rearrange("(g p) n -> p g n", p=P)).then_inc(sem("a_wo"), 16)
                    sp.dma_start(res[:, :, :], a["x"].rearrange("(t p) d -> p t d", p=P)).then_inc(sem("a_res"), 16)
                    with sp.Fori(1, A_GROUPS) as g:
                        src = a["a_wqkv"][ds(g, 1), :, :, :, :].rearrange("a p c k n -> p (a c k) n")
                        sp.wait_ge(sem("a_x1_in"), g * 3)
                        sp.dma_start(wqkv[:, :, :, :].rearrange("p c k n -> p (c k) n"), src).then_inc(sem("a_w"), 16)

                @blk.tensor
                def _(pe):
                    def project(g, b, c):
                        for kt in range(KD):
                            ins = pe.matmul((x0, x1)[c], wqkv[:, c, kt, :], xT[:, kt, b * S:(b + 1) * S],
                                            start=(kt == 0), stop=(kt == KD - 1))
                        ins.then_inc(sem("a_x0_in" if c == 0 else "a_x1_in"), 1)

                    def values(g, b):
                        for j in range(QT):
                            for kt in range(KD):
                                ins = pe.matmul((x0, x1)[b][:, j * P:(j + 1) * P],
                                                xT[:, kt, (b * QT + j) * P:(b * QT + j + 1) * P], wqkv[:, 2, kt, :],
                                                start=(kt == 0), stop=(kt == KD - 1))
                        ins.then_inc(sem("a_x0_in" if b == 0 else "a_x1_in"), 1)

                    def inverse_sums(g, b):
                        pe.wait_ge(sem("a_rwide"), g * 2 + (b + 1))
                        for i in range(QT):
                            ins = pe.transpose(x0[:, i * P:(i + 1) * P],
                                               rwide[b][:, i * A_G:(i + 1) * A_G, :].rearrange("p h d -> p (h d)"),
                                               ident[:, :])
                        ins.then_inc(sem("a_x0_in"), 1)

                    def scores(g, s):
                        b, i, h = step(s)
                        if s == 0:
                            pe.wait_ge(sem("a_x0_out"), g * 5 + 1)
                            pe.wait_ge(sem("a_x1_out"), g * 3 + 1)
                        if s == HALF:
                            pe.wait_ge(sem("a_x0_out"), g * 5 + 3)
                            pe.wait_ge(sem("a_x1_out"), g * 3 + 2)
                        w = (i + 1) * P
                        pe.matmul(sc[s % 3][:, 0:w], qT[b][:, i * P:w], kT[b][:, h, 0:w], start=True, stop=False)
                        pe.matmul(sc[s % 3][:, i * P:w], ident_bf[:, :], mask_bf[:, :],
                                  start=False, stop=True).then_inc(sem("a_scores"), 1)

                    def wait_taken(g, s):
                        if on_act(s):
                            pe.wait_ge(sem("a_prT_act"), g * (A_STEPS // A_G) + (s // A_G + 1))
                        else:
                            pe.wait_ge(sem("a_prT_dve"), g * (A_STEPS - A_STEPS // A_G) + (s - s // A_G + 1))

                    def turn(g, s):
                        pe.wait_ge(sem("a_exp"), g * A_STEPS + (s + 1))
                        if s >= 2:
                            wait_taken(g, s - 2)
                        for j in range(step(s)[1] + 1):
                            ins = pe.transpose(tp[s % 2][:, j * P:(j + 1) * P], pr[s % 3][:, j * P:(j + 1) * P],
                                               ident[:, :])
                        ins.then_inc(sem("a_turned"), 1)

                    def weigh(g, e):
                        b, i = e // QT, e % QT
                        wait_taken(g, A_G * e + A_G - 2)
                        wait_taken(g, A_G * e + A_G - 1)
                        if i == 0:
                            pe.wait_ge(sem("a_x0_out"), g * 5 + 2)
                            pe.wait_ge(sem("a_x1_out"), g * 3 + 3)
                            pe.wait_ge(sem("a_out"), g * 2 + b)
                        for j in range(i + 1):
                            for h in range(A_G):
                                ins = pe.matmul(ob[32 * h:32 * h + 32, i * P:(i + 1) * P],
                                                val[b][:, j, 32 * h:32 * h + 32],
                                                prT[(A_G * e + h) % (2 * A_G)][:, j * P:(j + 1) * P],
                                                start=(j == 0), stop=(j == i))
                        ins.then_inc(sem("a_weighed"), 1)

                    def group(g, last):
                        for s in range(A_STEPS):
                            scores(g, s)
                            if s >= 2:
                                turn(g, s - 2)
                            if s == HALF + 3:
                                pe.wait_ge(sem("a_x0_out"), g * 5 + 3)
                                inverse_sums(g, 0)
                            if s % A_G == 2 and s > A_G and s != HALF + 6:
                                weigh(g, s // A_G - 1)
                            if s == HALF + 7:
                                weigh(g, QT)
                        if not last:
                            pe.wait_ge(sem("a_w"), g * 16 + 32)
                            pe.wait_ge(sem("a_x0_out"), g * 5 + 4)
                            project(g + 1, 0, 0)
                            project(g + 1, 0, 1)
                        turn(g, A_STEPS - 2)
                        if not last:
                            pe.wait_ge(sem("a_x0_out"), g * 5 + 5)
                            values(g + 1, 0)
                        turn(g, A_STEPS - 1)
                        if not last:
                            pe.wait_ge(sem("a_x1_out"), g * 3 + 4)
                            project(g + 1, 1, 1)
                            pe.wait_ge(sem("a_x0_out"), g * 5 + 6)
                            project(g + 1, 1, 0)
                        weigh(g, 2 * QT - 1)
                        if not last:
                            pe.wait_ge(sem("a_x1_out"), g * 3 + 5)
                            values(g + 1, 1)
                        pe.wait_ge(sem("a_x0_out"), g * 5 + (4 if last else 7))
                        inverse_sums(g, 1)

                    pe.wait_ge(sem("a_w"), 16)
                    pe.wait_ge(sem("a_x0"), 32)
                    project(0, 0, 0)
                    project(0, 0, 1)
                    pe.wait_ge(sem("a_x0_out"), 1)
                    values(0, 0)
                    pe.wait_ge(sem("a_x1"), 32)
                    pe.wait_ge(sem("a_x1_out"), 1)
                    project(0, 1, 1)
                    pe.wait_ge(sem("a_x0_out"), 2)
                    project(0, 1, 0)
                    pe.wait_ge(sem("a_x1_out"), 2)
                    values(0, 1)
                    pe.wait_ge(sem("consts"), 48)
                    with pe.Fori(0, A_GROUPS - 1) as g:
                        group(g, False)
                    group(A_GROUPS - 1, True)

                    pe.wait_ge(sem("a_wo"), 16)
                    pe.wait_ge(sem("a_out"), 2 * A_GROUPS - 1)
                    for t in range(NT):
                        if t == QT:
                            pe.wait_ge(sem("a_out"), 2 * A_GROUPS)
                        if t >= 4:
                            pe.wait_ge(sem("a_pre"), t - 3)
                        for g in range(A_GROUPS):
                            ins = pe.matmul(bank[t % 4][:, 0:D], attT[:, g, t * P:(t + 1) * P], wo[:, g, :],
                                            start=(g == 0), stop=(g == A_GROUPS - 1))
                        ins.then_inc(sem("a_oproj"), 1)
                    pe.wait_ge(sem("a_pre"), NT)
                    transpose_tokens(pe, nrm, sem("a_nrm"), sem("a_turn2"))

                @blk.scalar
                def _(act):
                    def take(dst, n, scale=1.0):
                        act.wait_ge(sem("a_x0_in"), n)
                        act.activation(dst, x0, ACT.Copy, scale=scale).then_inc(sem("a_x0_out"), 1)

                    q_scale = float(A_HD) ** -0.5

                    def group(g, last):
                        for s in range(A_STEPS + 2):
                            if s < A_STEPS:
                                w = (step(s)[1] + 1) * P
                                act.wait_ge(sem("a_max"), g * A_STEPS + (s + 1))
                                if s >= 3:
                                    act.wait_ge(sem("a_turned"), g * A_STEPS + (s - 2))
                                act.activation(pr[s % 3][:, 0:w], sc[s % 3][:, 0:w], ACT.Exp, bias=nmax[:, s:s + 1],
                                               scale=1.0, accum_out=ssum[:, s:s + 1]).then_inc(sem("a_exp"), 1)
                            if s == A_STEPS and not last:
                                take(qT[0][:, :], g * 5 + 5, q_scale)
                            if s >= 2 and on_act(s - 2):
                                w = (step(s - 2)[1] + 1) * P
                                act.wait_ge(sem("a_turned"), g * A_STEPS + (s - 1))
                                act.activation(prT[(s - 2) % (2 * A_G)][:, 0:w], tp[s % 2][:, 0:w],
                                               ACT.Copy).then_inc(sem("a_prT_act"), 1)
                            if s == HALF + 4:
                                take(rT[:, :], g * 5 + 4)
                            if s == A_STEPS and not last:
                                take(val[0][:, :, :].rearrange("p t d -> p (t d)"), g * 5 + 6)
                        if not last:
                            take(qT[1][:, :], g * 5 + 7, q_scale)
                        act.wait_ge(sem("a_out"), g * 2 + 1)
                        take(rT[:, :], g * 5 + (5 if last else 8))

                    take(qT[0][:, :], 1, q_scale)
                    take(val[0][:, :, :].rearrange("p t d -> p (t d)"), 2)
                    take(qT[1][:, :], 3, q_scale)
                    with act.Fori(0, A_GROUPS - 1) as g:
                        group(g, False)
                    group(A_GROUPS - 1, True)
                    act.wait_ge(sem("consts2"), 96)
                    evac_transposed(act, 0, sem("a_turn2"), sem("a_xT"), ln1w, ln1b)

                @blk.vector
                def _(v):
                    own = Order(v, sem("v_own"))

                    def take(dst, n):
                        v.wait_ge(sem("a_x1_in"), n)
                        v.tensor_copy(dst, x1).then_inc(sem("a_x1_out"), 1)

                    def take_keys(b, n):
                        v.wait_ge(sem("a_x1_in"), n)
                        for h in range(A_G):
                            rows = slice(32 * h, 32 * h + 32)
                            ins = v.tensor_copy(kT[b][rows, h, :], x1[rows, :])
                        ins.then_inc(sem("a_x1_out"), 1)

                    def widen(g, b):
                        cols = slice(b * HALF, (b + 1) * HALF)
                        v.wait_ge(sem("a_exp"), g * A_STEPS + HALF * (b + 1))
                        v.reciprocal(rsum[:, cols], ssum[:, cols]).then_inc(sem("a_rsum"), 1)
                        v.wait_ge(sem("a_rsum"), g * 2 + (b + 1))
                        v.tensor_copy(rwide[b][:, :, :], rsum[:, cols].unsqueeze(2).to_broadcast([P, HALF, 32])
                                      ).then_inc(sem("a_rwide"), 1)

                    def results(g, b, n):
                        v.wait_ge(sem("a_weighed"), g * (2 * QT) + QT * (b + 1))
                        v.wait_ge(sem("a_x0_out"), n)
                        v.tensor_tensor(attT[:, ds(g, 1), b * S:(b + 1) * S].rearrange("p a s -> p (a s)"), ob,
                                        rT[:, :], ALU.mult).then_inc(sem("a_out"), 1)

                    def group(g, last):
                        for s in range(A_STEPS + 2):
                            if s < A_STEPS:
                                w = (step(s)[1] + 1) * P
                                v.wait_ge(sem("a_scores"), g * A_STEPS + (s + 1))
                                v.tensor_reduce(nmax[:, s:s + 1], sc[s % 3][:, 0:w], AX.X, ALU.max,
                                                negate=True).then_inc(sem("a_max"), 1)
                            if s == A_STEPS and not last:
                                take_keys(0, g * 3 + 4)
                            if s >= 2 and not on_act(s - 2):
                                w = (step(s - 2)[1] + 1) * P
                                v.wait_ge(sem("a_turned"), g * A_STEPS + (s - 1))
                                v.tensor_copy(prT[(s - 2) % (2 * A_G)][:, 0:w],
                                              tp[s % 2][:, 0:w]).then_inc(sem("a_prT_dve"), 1)
                            if s == HALF + 1:
                                widen(g, 0)
                            if s == HALF + 5:
                                results(g, 0, g * 5 + 4)
                        widen(g, 1)
                        if not last:
                            take_keys(1, g * 3 + 5)
                            take(val[1][:, :, :].rearrange("p t d -> p (t d)"), g * 3 + 6)
                        results(g, 1, g * 5 + (5 if last else 8))

                    v.memset(power[:, :], -0.5).then_inc(sem("power"), 1)
                    v.wait_ge(sem("a_zeroed"), 2)
                    take_keys(0, 1)
                    take_keys(1, 2)
                    take(val[1][:, :, :].rearrange("p t d -> p (t d)"), 3)
                    with v.Fori(0, A_GROUPS - 1) as g:
                        group(g, False)
                    group(A_GROUPS - 1, True)
                    v.wait_ge(sem("a_res"), 16)
                    for t in range(NT):
                        v.wait_ge(sem("a_oproj"), t + 1)
                        v.tensor_tensor(pre[:, t, :], bank[t % 4][:, 0:D], res[:, t, :],
                                        ALU.add).then_inc(sem("a_pre"), 1)
                        v.wait_ge(sem("a_pre"), t + 1)
                        norm_stats(v, own, t, pre)
                    norm_apply(v, own, 1, pre, res)
                    own.sync()
                    for t in range(NT):
                        norm_stats(v, own, t, res)
                    norm_apply(v, own, 2, res, nrm, sem("a_nrm"))
                    v.wait_ge(sem("consts2"), 96)
                    evac_transposed(v, 1, sem("a_turn2"), sem("a_xT"), ln1w, ln1b)

                @blk.gpsimd
                def _(pool):
                    for b in range(B):
                        pool.memset(kT[b][:, :, :], 0.0).then_inc(sem("a_zeroed"), 1)
                    pool.wait_ge(sem("power"), 1)
                    pool_rstd(pool, 1)
                    pool_rstd(pool, 2)

        lay = ExitStack()
        with lay:
            wqk = sb("b_wqk", [P, 2, KD, P], ctx=lay)
            wv = sb("b_wv", [P, KD, P], ctx=lay)
            wo = sb("b_wo", [P, B_H, D], ctx=lay)
            rope = sb("b_rope", [P, 2, 2, S], ctx=lay)
            bqk = sb("b_bqk", [P, 2, 2, B_H], ctx=lay)
            bv = sb("b_bv", [P, B_H], ctx=lay)
            bo = sb("b_bo", [P, D], ctx=lay)
            part = [sb(f"b_part{i}", [P, 2, S], ctx=lay) for i in range(2)]
            qk = [[sb(f"b_qk{b}{c}", [P, S], ctx=lay) for c in range(2)] for b in range(B)]
            val = sb("b_val", [P, NT, B_HD], ctx=lay)
            pr = [sb(f"b_pr{i}", [P, S], ctx=lay) for i in range(3)]
            prT = [sb(f"b_prT{b}", [P, QT, S], ctx=lay) for b in range(B)]
            attT = sb("b_attT", [P, B_H, T], ctx=lay)
            nmax = sb("b_nmax", [P, B_STEPS], ctx=lay)
            ssum = sb("b_ssum", [P, B_STEPS], ctx=lay)
            rsum = sb("b_rsum", [P, B_STEPS], ctx=lay)
            sc, tp, ob, xb = bank[0:3], bank[3:5], bank[5], bank[6:8]
            CHUNKS = [(b, c) for b in range(B) for c in range(2)]

            with nc.Block() as blk:
                @blk.sync
                def _(sp):
                    sp.dma_start(wqk[:, :, :, :], a["b_wqk"][0]).then_inc(sem("b_wqk"), 16)
                    sp.dma_start(wv[:, :, :], a["b_wv"][0]).then_inc(sem("b_wv"), 16)
                    sp.dma_start(rope[:, :, :, :], a["b_rope"]).then_inc(sem("b_rope_in"), 16)
                    sp.dma_start(bqk[:, :, :, :], a["b_bqk"]).then_inc(sem("b_rope_in"), 16)
                    sp.dma_start(bv[:, :], a["b_bv"]).then_inc(sem("b_bv"), 16)
                    sp.dma_start(bo[:, :], a["b_bo"].partition_broadcast(P)).then_inc(sem("b_bo"), 16)
                    sp.dma_start(wo[:, :, :], a["b_wo"].rearrange("(h p) n -> p h n", p=P)).then_inc(sem("b_wo"), 16)
                    with sp.Fori(1, B_H) as h:
                        src_qk = a["b_wqk"][ds(h, 1), :, :, :, :].rearrange("a p c k n -> p (a c k) n")
                        src_v = a["b_wv"][ds(h, 1), :, :, :].rearrange("a p k n -> p (a k) n")
                        sp.wait_ge(sem("b_proj"), h * 4)
                        sp.dma_start(wqk[:, :, :, :].rearrange("p c k n -> p (c k) n"), src_qk).then_inc(sem("b_wqk"), 16)
                        sp.wait_ge(sem("b_vproj"), h * 2)
                        sp.dma_start(wv[:, :, :], src_v).then_inc(sem("b_wv"), 16)
                    load_first("m", sp, False)

                @blk.tensor
                def _(pe):
                    def project(h, n):
                        b, c = CHUNKS[n]
                        if n == 0:
                            pe.wait_ge(sem("b_wqk"), h * 16 + 16)
                        if n == 1:
                            pe.wait_ge(sem("b_val"), h * 2)
                        if n >= 2:
                            pe.wait_ge(sem("b_parts"), h * 12 + 3 * (n - 1))
                        for kt in range(KD):
                            ins = pe.matmul(xb[n % 2][:, :], wqk[:, c, kt, :], xT[:, kt, b * S:(b + 1) * S],
                                            start=(kt == 0), stop=(kt == KD - 1))
                        ins.then_inc(sem("b_proj"), 1)

                    def values(h, b):
                        if b == 0:
                            pe.wait_ge(sem("b_wv"), h * 16 + 16)
                        pe.wait_ge(sem("b_parts"), h * 12 + (9 + 3 * b))
                        for j in range(QT):
                            for kt in range(KD):
                                ins = pe.matmul(xb[b][:, j * P:(j + 1) * P],
                                                xT[:, kt, (b * QT + j) * P:(b * QT + j + 1) * P], wv[:, kt, :],
                                                start=(kt == 0), stop=(kt == KD - 1))
                        ins.then_inc(sem("b_vproj"), 1)

                    def scores(h, s):
                        b, i = s // QT, s % QT
                        if i == 0:
                            pe.wait_ge(sem("b_qk"), h * 4 + 2 * (b + 1))
                        w = (i + 1) * P
                        pe.matmul(sc[s % 3][:, 0:w], qk[b][0][:, i * P:w], qk[b][1][:, 0:w], start=True, stop=False)
                        pe.matmul(sc[s % 3][:, i * P:w], ident_bf[:, :], mask_bf[:, :],
                                  start=False, stop=True).then_inc(sem("b_scores"), 1)

                    def turn(h, s):
                        pe.wait_ge(sem("b_pr"), h * B_STEPS + (s + 1))
                        if s >= 2:
                            pe.wait_ge(sem("b_prT"), h * B_STEPS + (s - 1))
                        for j in range(s % QT + 1):
                            ins = pe.transpose(tp[s % 2][:, j * P:(j + 1) * P], pr[s % 3][:, j * P:(j + 1) * P],
                                               ident[:, :])
                        ins.then_inc(sem("b_turned"), 1)

                    def weigh(h, b):
                        pe.wait_ge(sem("b_prT"), h * B_STEPS + QT * (b + 1))
                        pe.wait_ge(sem("b_val"), h * 2 + (b + 1))
                        pe.wait_ge(sem("b_out"), h * 2 + b)
                        for j in range(QT):
                            ins = pe.matmul(ob[:, j * P:S], val[:, b * QT + j, :], prT[b][:, j, j * P:S],
                                            start=(j == 0), stop=(j == QT - 1))
                        ins.then_inc(sem("b_weighed"), 1)

                    def head(h, last):
                        values(h, 0)
                        values(h, 1)
                        for s in range(B_STEPS):
                            scores(h, s)
                            if s >= 2:
                                turn(h, s - 2)
                            if s == QT + 2:
                                weigh(h, 0)
                        for n in range(2):
                            if not last:
                                project(h + 1, n)
                            turn(h, B_STEPS - 2 + n)
                        if not last:
                            project(h + 1, 2)
                            project(h + 1, 3)
                        weigh(h, 1)

                    for n in range(4):
                        project(0, n)
                    with pe.Fori(0, B_H - 1) as h:
                        head(h, False)
                    head(B_H - 1, True)

                    pe.wait_ge(sem("b_wo"), 16)
                    pe.wait_ge(sem("b_out"), 2 * B_H)
                    for t in range(NT):
                        if t >= 4:
                            pe.wait_ge(sem("b_h"), t - 3)
                        for h in range(B_H):
                            ins = pe.matmul(bank[t % 4][:, 0:D], attT[:, h, t * P:(t + 1) * P], wo[:, h, :],
                                            start=(h == 0), stop=(h == B_H - 1))
                        ins.then_inc(sem("b_oproj"), 1)
                    pe.wait_ge(sem("b_h"), NT)
                    transpose_tokens(pe, nrm, sem("b_nrm"), sem("b_turn2"))

                @blk.scalar
                def _(act):
                    def out_head(h, b):
                        act.wait_ge(sem("b_weighed"), h * 2 + (b + 1))
                        act.wait_ge(sem("b_bv"), 16)
                        act.activation(attT[:, ds(h, 1), b * S:(b + 1) * S].rearrange("p a s -> p (a s)"), ob[:, :],
                                       ACT.Identity, bias=bv[:, ds(h, 1)]).then_inc(sem("b_out"), 1)

                    def head(h, last):
                        for b in range(B):
                            act.wait_ge(sem("b_vproj"), h * 2 + (b + 1))
                            act.activation(val[:, b * QT:(b + 1) * QT, :].rearrange("p t d -> p (t d)"), xb[b][:, :],
                                           ACT.Copy).then_inc(sem("b_val"), 1)
                        for s in range(B_STEPS + 2):
                            if s < B_STEPS:
                                w = (s % QT + 1) * P
                                act.wait_ge(sem("b_max"), h * B_STEPS + (s + 1))
                                if s >= 3:
                                    act.wait_ge(sem("b_turned"), h * B_STEPS + (s - 2))
                                act.activation(pr[s % 3][:, 0:w], sc[s % 3][:, 0:w], ACT.Exp, bias=nmax[:, s:s + 1],
                                               scale=1.0, accum_out=ssum[:, s:s + 1]).then_inc(sem("b_exp"), 1)
                            if s >= 2:
                                b, i = (s - 2) // QT, (s - 2) % QT
                                act.wait_ge(sem("b_turned"), h * B_STEPS + (s - 1))
                                act.activation(prT[b][:, 0:i + 1, i * P:(i + 1) * P],
                                               tp[s % 2][:, 0:(i + 1) * P].rearrange("p (j q) -> p j q", q=P),
                                               ACT.Copy).then_inc(sem("b_prT"), 1)
                            if s == QT + 3:
                                out_head(h, 0)
                        out_head(h, 1)

                    with act.Fori(0, B_H - 1) as h:
                        head(h, False)
                    head(B_H - 1, True)
                    evac_transposed(act, 0, sem("b_turn2"), sem("b_xT"), ln2w, ln2b)

                @blk.vector
                def _(v):
                    own = Order(v, sem("v_own_b"))
                    half = P // 2

                    def rotate(h, n):
                        b, c = CHUNKS[n]
                        x, t = xb[n % 2], part[n % 2]
                        v.wait_ge(sem("b_proj"), h * 4 + (n + 1))
                        if n >= 2:
                            v.wait_ge(sem("b_qk"), h * 4 + (n - 1))
                        v.scalar_tensor_tensor(out=t[:, 0, :], in0=x[:, :], scalar=bqk[:, c, 0, ds(h, 1)],
                                               in1=rope[:, c, 0, :], op0=ALU.add,
                                               op1=ALU.mult).then_inc(sem("b_parts"), 1)
                        for lo, hi in ((0, half), (half, 0)):
                            v.scalar_tensor_tensor(out=t[lo:lo + half, 1, :], in0=x[hi:hi + half, :],
                                                   scalar=bqk[lo:lo + half, c, 1, ds(h, 1)],
                                                   in1=rope[lo:lo + half, c, 1, :], op0=ALU.add,
                                                   op1=ALU.mult).then_inc(sem("b_parts"), 1)

                    def head(h, last):
                        for s in range(B_STEPS + 1):
                            if s < B_STEPS:
                                w = (s % QT + 1) * P
                                v.wait_ge(sem("b_scores"), h * B_STEPS + (s + 1))
                                v.tensor_reduce(nmax[:, s:s + 1], sc[s % 3][:, 0:w], AX.X, ALU.max,
                                                negate=True).then_inc(sem("b_max"), 1)
                            if s >= 1:
                                w = ((s - 1) % QT + 1) * P
                                v.wait_ge(sem("b_exp"), h * B_STEPS + s)
                                v.reciprocal(rsum[:, s - 1:s], ssum[:, s - 1:s]).then_inc(sem("b_rsum"), 1)
                                v.wait_ge(sem("b_rsum"), h * B_STEPS + s)
                                p = pr[(s - 1) % 3][:, 0:w]
                                v.tensor_scalar(p, p, rsum[:, s - 1:s], None, ALU.mult).then_inc(sem("b_pr"), 1)
                        if not last:
                            for n in range(4):
                                rotate(h + 1, n)

                    v.wait_ge(sem("b_rope_in"), 32)
                    for n in range(4):
                        rotate(0, n)
                    with v.Fori(0, B_H - 1) as h:
                        head(h, False)
                    head(B_H - 1, True)
                    v.wait_ge(sem("b_hb"), NT)
                    for t in range(NT):
                        v.wait_ge(sem("b_oproj"), t + 1)
                        v.tensor_tensor(pre[:, t, :], bank[t % 4][:, 0:D], pre[:, t, :],
                                        ALU.add).then_inc(sem("b_h"), 1)
                        v.wait_ge(sem("b_h"), t + 1)
                        norm_stats(v, own, t, pre)
                    norm_apply(v, own, 3, pre, nrm, sem("b_nrm"))
                    evac_transposed(v, 1, sem("b_turn2"), sem("b_xT"), ln2w, ln2b)

                @blk.gpsimd
                def _(pool):
                    def add_up(h):
                        for n, (b, c) in enumerate(CHUNKS):
                            t = part[n % 2]
                            pool.wait_ge(sem("b_parts"), h * 12 + 3 * (n + 1))
                            pool.tensor_tensor(qk[b][c][:, :], t[:, 0, :], t[:, 1, :],
                                               ALU.add).then_inc(sem("b_qk"), 1)

                    add_up(0)
                    pool.wait_ge(sem("b_bo"), 16)
                    for t in range(NT):
                        pool.tensor_tensor(pre[:, t, :], res[:, t, :], bo[:, :], ALU.add).then_inc(sem("b_hb"), 1)
                    with pool.Fori(1, B_H) as h:
                        add_up(h)
                    pool_rstd(pool, 3)

        def mixture(tag, experts, gated, init, k_norm):
            name = f"{tag}_"
            pairs = experts // 2
            n_up = 2 if gated else 1
            lay = ExitStack()
            with lay:
                wr = sb(name + "wr", [P, KD, experts], ctx=lay)
                wup_h = [sb(f"{name}wup_h{k}", [P, n_up, KD, F], F32R, ctx=lay) for k in range(2)]
                wup_l = [sb(f"{name}wup_l{k}", [P, n_up, KD, F], F32R, ctx=lay) for k in range(2)]
                wdn_h = [sb(f"{name}wdn_h{k}", [P, KF, D], F32R, ctx=lay) for k in range(2)]
                wdn_l = [sb(f"{name}wdn_l{k}", [P, KF, D], F32R, ctx=lay) for k in range(2)]
                hid_h = [sb(f"{name}hid_h{k}", [P, KF, T], F32R, ctx=lay) for k in range(2)]
                hid_l = [sb(f"{name}hid_l{k}", [P, KF, T], F32R, ctx=lay) for k in range(2)]
                hid = [sb(f"{name}hid{i}", [P, T], ctx=lay) for i in range(2)]
                acc = sb(name + "acc", [P, NT, D], ctx=lay)
                gate = [sb(f"{name}gate{i}", [P, S], ctx=lay) for i in range(2)]
                if not gated:
                    b1 = sb(name + "b1", [P, KF, experts], ctx=lay)
                    b2 = sb(name + "b2", [experts, D], ctx=lay)
                    combT = sb(name + "combT", [experts, T], ctx=lay)
                up, down = bank[0:4], bank[4:8]
                PARTS = [(mt, c) for mt in range(KF) for c in range(B)]
                deep = 2 if gated else 4
                per = 1 if gated else 2

                with nc.Block() as blk:
                    @blk.sync
                    def _(sp):
                        sp.dma_start(wr[:, :, :], a[name + "wr"].rearrange("(k p) e -> p k e", p=P)).then_inc(sem(name + "wr"), 16)
                        if not gated:
                            sp.dma_start(b1[:, :, :], a[name + "b1"]).then_inc(sem(name + "b1"), 16)
                            sp.dma_start(b2[:, :], a[name + "b2"]).then_inc(sem(name + "b2"), 16)
                        with sp.Fori(1, pairs) as i:
                            for k in range(2):
                                src = a[name + "wup"][ds(i * 2 + k, 1), :, :, :, :].rearrange("a p c k n -> p (a c k) n")
                                sp.wait_ge(sem(name + "w_lo"), i * 4 + (k - 3))
                                sp.dma_start(up_in[k][:, 0:n_up, :, :].rearrange("p c k n -> p (c k) n"),
                                             src).then_inc(sem(f"{name}wup{k}"), 16)
                            for k in range(2):
                                src = a[name + "wdn"][ds(i * 2 + k, 1), :, :, :].rearrange("a p k n -> p (a k) n")
                                sp.wait_ge(sem(name + "w_lo"), i * 4 + (k - 1))
                                sp.dma_start(dn_in[k][:, :, :], src).then_inc(sem(f"{name}wdn{k}"), 16)

                    @blk.tensor
                    def _(pe):
                        pe.wait_ge(sem(name + "wr"), 16)
                        for t in range(NT):
                            for kt in range(KD):
                                ins = pe.matmul(bank[7][:, t * experts:(t + 1) * experts],
                                                xT[:, kt, t * P:(t + 1) * P], wr[:, kt, :],
                                                start=(kt == 0), stop=(kt == KD - 1))
                        ins.then_inc(sem(name + "logits"), 1)

                        def second_biases():
                            pe.wait_ge(sem(name + "routed"), 1)
                            for t in range(NT):
                                ins = pe.transpose(bank[4 + t // 4][0:experts, t % 4 * P:(t % 4 + 1) * P],
                                                   comb[:, t, 0:experts], ident[:, :])
                            ins.then_inc(sem(name + "comb_turned"), 1)
                            pe.wait_ge(sem(name + "combT"), 1)
                            pe.wait_ge(sem(name + "b2"), 16)
                            for t in range(NT):
                                if t >= 4:
                                    pe.wait_ge(sem(name + "acc"), t - 3)
                                pe.matmul(down[t % 4][:, 0:D], combT[:, t * P:(t + 1) * P], b2[:, :],
                                          start=True, stop=True).then_inc(sem(name + "bias"), 1)

                        def pair(i, first=False):
                            for k in range(2):
                                if first and k == 0:
                                    pe.wait_ge(sem("x_lo_" + tag), 1)
                                pe.wait_ge(sem(name + "w_lo"), i * 4 + (1 + k))
                                for q, (mt, c) in enumerate(PARTS):
                                    n = 4 * k + q
                                    if first and n == 1:
                                        pe.wait_ge(sem("x_lo_" + tag), 2)
                                    if n >= deep:
                                        pe.wait_ge(sem(name + "hid"), i * (8 // per) + ((n - deep) // per + 1))
                                    for g in range(n_up):
                                        for kt in range(KD):
                                            wh, wl = (w[k][:, g, kt, mt * P:(mt + 1) * P] for w in (wup_h, wup_l))
                                            x_h, x_l = (x[:, kt, c * S:(c + 1) * S] for x in (xh, xl))
                                            dst = up[(q * n_up + g) % 4][:, :]
                                            pe.matmul(dst, wh, x_h, start=(kt == 0), stop=False)
                                            pe.matmul(dst, wh, x_l, start=False, stop=False)
                                            ins = pe.matmul(dst, wl, x_h, start=False, stop=(kt == KD - 1))
                                        ins.then_inc(sem(name + "up"), 1)
                            if first and not gated:
                                second_biases()
                            for k in range(2):
                                pe.wait_ge(sem(name + "w_lo"), i * 4 + (3 + k))
                                for t in range(NT):
                                    if t in (0, 4):
                                        pe.wait_ge(sem(name + "hid_lo"), i * 8 + 4 * k + (3 if t == 0 else 4))
                                    pe.wait_ge(sem(name + "acc"), i * (2 * NT) + (NT * (k + 1) + t - 3))
                                    for kt in range(KF):
                                        h_h, h_l = (h[k][:, kt, t * P:(t + 1) * P] for h in (hid_h, hid_l))
                                        dst = down[t % 4][:, 0:D]
                                        pe.matmul(dst, h_h, wdn_h[k][:, kt, :], start=(kt == 0), stop=False)
                                        pe.matmul(dst, h_h, wdn_l[k][:, kt, :], start=False, stop=False)
                                        ins = pe.matmul(dst, h_l, wdn_h[k][:, kt, :], start=False, stop=(kt == KF - 1))
                                    ins.then_inc(sem(name + "down"), 1)

                        pair(0, True)
                        with pe.Fori(1, pairs) as i:
                            pair(i)

                    @blk.scalar
                    def _(act):
                        def split_up(i, k):
                            act.wait_ge(sem(f"{name}wup{k}"), i * 16 + 16)
                            act.activation(wup_h[k][:, :, :, :], up_in[k][:, 0:n_up, :, :],
                                           ACT.Copy).then_inc(sem(name + "w_hi"), 1)

                        def split_down(i, k):
                            act.wait_ge(sem(f"{name}wdn{k}"), i * 16 + 16)
                            act.activation(wdn_h[k][:, :, :], dn_in[k][:, :, :], ACT.Copy).then_inc(sem(name + "w_hi"), 1)

                        split_up(0, 0)
                        for c in range(B):
                            half = slice(c * S, (c + 1) * S)
                            act.activation(xh[:, :, half], xT[:, :, half], ACT.Copy).then_inc(sem("x_hi_" + tag), 1)
                        act.wait_ge(sem(name + "shifted"), 1)
                        act.activation(probs8[:, :, 0:experts], probs8[:, :, 0:experts],
                                       ACT.Exp).then_inc(sem(name + "exp"), 1)
                        split_up(0, 1)
                        if not gated:
                            act.wait_ge(sem(name + "b1"), 16)

                        def pair(i, first=False, last=False):
                            for k in range(2):
                                if gated:
                                    for q in range(4):
                                        act.wait_ge(sem(name + "up"), i * 16 + (8 * k + 2 * q + 1))
                                        if not first or k or q >= 2:
                                            act.wait_ge(sem(name + "hid"), i * 8 + (4 * k + q - 1))
                                        act.activation(gate[q % 2][:, :], up[q % 2 * 2], ACT.Silu).then_inc(sem(name + "gate"), 1)
                                        if k == 0 and q in (0, 2):
                                            split_down(i, q // 2)
                                        if k == 1 and q == 1 and not last:
                                            split_up(i + 1, 0)
                                else:
                                    for mt in range(KF):
                                        act.wait_ge(sem(name + "up"), i * 8 + (4 * k + 2 * mt + 2))
                                        if not first or k:
                                            act.wait_ge(sem(name + "hid_lo"), i * 8 + (4 * k + 2 * mt - 2))
                                        act.activation(hid[mt][:, :],
                                                       psum[:, 2 * mt:2 * mt + 2, :].rearrange("p b s -> p (b s)"), ACT.Gelu,
                                                       bias=b1[:, mt, ds(i * 2 + k, 1)]).then_inc(sem(name + "hid"), 1)
                                        if k == 0:
                                            split_down(i, mt)
                                        if k == 1 and mt == 0 and not last:
                                            split_up(i + 1, 0)
                                    if first and k == 0:
                                        act.wait_ge(sem(name + "gap"), 1)
                                        act.activation(row2[:, :], row1[:, :], ACT.Exp).then_inc(sem(name + "exp"), 1)
                            if first and not gated:
                                act.wait_ge(sem(name + "comb_turned"), 1)
                                for n in range(2):
                                    ins = act.activation(combT[:, n * S:(n + 1) * S], bank[4 + n][0:experts, :], ACT.Copy)
                                ins.then_inc(sem(name + "combT"), 1)
                            if not last:
                                act.wait_ge(sem(name + "up"), (i + 1) * (8 * n_up))
                                split_up(i + 1, 1)

                        pair(0, first=True, last=(pairs == 1))
                        if pairs > 2:
                            with act.Fori(1, pairs - 1) as i:
                                pair(i)
                        pair(pairs - 1, last=True)

                    @blk.vector
                    def _(v):
                        own = Order(v, sem("v_own_" + tag))
                        pe8 = probs8[:, :, 0:experts]

                        def wide(x, n=experts):
                            return x.unsqueeze(2).to_broadcast([P, NT, n])

                        def route_shift():
                            own.mark(v.memset(probs8[:, :, :], -1.0))
                            v.wait_ge(sem(name + "logits"), 1)
                            logits = bank[7][:, 0:NT * experts].rearrange("p (t e) -> p t e", e=experts)
                            own.mark(v.tensor_reduce(row1[:, :], logits, AX.X, ALU.max))
                            own.sync()
                            v.tensor_tensor(pe8, logits, wide(row1[:, :]), ALU.subtract).then_inc(sem(name + "shifted"), 1)

                        def route_softmax():
                            v.wait_ge(sem(name + "exp"), 1)
                            own.mark(v.tensor_reduce(row1[:, :], pe8, AX.X, ALU.add))
                            own.sync()
                            own.mark(v.reciprocal(row2[:, :], row1[:, :]))
                            own.sync()
                            own.mark(v.tensor_tensor(pe8, pe8, wide(row2[:, :]), ALU.mult))
                            own.sync()

                        def route_top():
                            for t in range(NT):
                                own.mark(v.max(top8[:, t, :], probs8[:, t, :]))
                            own.sync()
                            for t in range(NT):
                                own.mark(v.max_index(idx8[:, t, :], top8[:, t, :], probs8[:, t, :]))
                            if gated:
                                own.mark(v.tensor_tensor(row1[:, :], top8[:, :, 0], top8[:, :, 1], ALU.add))
                                own.sync()
                                own.mark(v.reciprocal(row2[:, :], row1[:, :]))
                                own.sync()
                                own.mark(v.tensor_tensor(wts[:, :, :], top8[:, :, 0:2], wide(row2[:, :], 2), ALU.mult))
                            else:
                                v.tensor_tensor(row1[:, :], top8[:, :, 1], top8[:, :, 0],
                                                ALU.subtract).then_inc(sem(name + "gap"), 1)
                            own.sync()
                            own.mark(v.tensor_copy(idxf[:, :, :], idx8[:, :, 0:2]))
                            own.sync()

                        def route_weights():
                            if not gated:
                                v.wait_ge(sem(name + "exp"), 2)
                                own.mark(v.tensor_scalar(row1[:, :], row2[:, :], 1.0, None, ALU.add))
                                own.sync()
                                own.mark(v.reciprocal(wts[:, :, 0], row1[:, :]))
                                own.sync()
                                own.mark(v.tensor_tensor(wts[:, :, 1], wts[:, :, 0], row2[:, :], ALU.mult))
                                own.sync()
                            experts_row = iota[:, 0:experts].unsqueeze(1).to_broadcast([P, NT, experts])
                            for r, dst in ((0, comb), (1, pick)):
                                own.mark(v.tensor_tensor(dst[:, :, 0:experts], experts_row, wide(idxf[:, :, r]), ALU.is_equal))
                            for r, dst in ((0, comb), (1, pick)):
                                own.sync(behind=1)
                                x = dst[:, :, 0:experts]
                                own.mark(v.tensor_tensor(x, x, wide(wts[:, :, r]), ALU.mult))
                            own.sync()
                            v.tensor_tensor(comb[:, :, 0:experts], comb[:, :, 0:experts], pick[:, :, 0:experts],
                                            ALU.add).then_inc(sem(name + "routed"), 1)
                            v.wait_ge(sem(name + "routed"), 1)

                        def product(i, n):
                            v.wait_ge(sem(name + "gate"), i * 8 + (n + 1))
                            v.wait_ge(sem(name + "up"), i * 16 + (2 * n + 2))
                            if n >= 2:
                                v.wait_ge(sem(name + "hid_lo"), i * 8 + (n - 1))
                            v.tensor_tensor(hid[n % 2][:, 0:S], up[n % 2 * 2 + 1][:, :],
                                            gate[n % 2][:, :], ALU.mult).then_inc(sem(name + "hid"), 1)

                        def split(i, n, src):
                            k, (mt, c) = n // 4, PARTS[n % 4]
                            hi = hid_h[k][:, mt, c * S:(c + 1) * S]
                            v.wait_ge(sem(name + "hid"), i * (8 // per) + (n // per + 1))
                            v.tensor_copy(hi, src).then_inc(sem(name + "hid_hi"), 1)
                            v.wait_ge(sem(name + "hid_hi"), i * 8 + (n + 1))
                            v.tensor_tensor(hid_l[k][:, mt, c * S:(c + 1) * S], src, hi.bitcast(F32),
                                            ALU.subtract).then_inc(sem(name + "hid_lo"), 1)

                        route_shift()
                        for c in range(B):
                            half = slice(c * S, (c + 1) * S)
                            v.wait_ge(sem("x_hi_" + tag), c + 1)
                            v.tensor_tensor(xl[:, :, half], xT[:, :, half], xh[:, :, half].bitcast(F32),
                                            ALU.subtract).then_inc(sem("x_lo_" + tag), 1)

                        def pair(i, first=False):
                            if gated:
                                for n in range(8):
                                    product(i, n)
                                    split(i, n, hid[n % 2][:, 0:S])
                                    if first and n == 0:
                                        route_softmax()
                                    if first and n == 1:
                                        route_top()
                                    if first and n == 2:
                                        route_weights()
                                    if first and n == 3:
                                        init(v, own, acc, down, sem(name + "bias"), sem(name + "acc"))
                            else:
                                if first:
                                    route_softmax()
                                    route_top()
                                for n in range(8):
                                    split(i, n, hid[n // 2 % 2][:, n % 2 * S:(n % 2 + 1) * S])
                                    if first and n == 5:
                                        route_weights()
                                if first:
                                    init(v, own, acc, down, sem(name + "bias"), sem(name + "acc"))
                            for k in range(2):
                                for t in range(NT):
                                    v.wait_ge(sem(name + "down"), i * (2 * NT) + (NT * k + t + 1))
                                    v.wait_ge(sem(name + "acc"), i * (2 * NT) + (NT * k + t + 1))
                                    v.scalar_tensor_tensor(out=acc[:, t, :], in0=down[t % 4][:, 0:D],
                                                           scalar=comb[:, t, ds(i * 2 + k, 1)], in1=acc[:, t, :],
                                                           op0=ALU.mult, op1=ALU.add).then_inc(sem(name + "acc"), 1)

                        pair(0, True)
                        with v.Fori(1, pairs) as i:
                            pair(i)
                        v.wait_ge(sem(name + "acc"), NT * (experts + 1))
                        for t in range(NT):
                            norm_stats(v, own, t, acc)
                        norm_apply(v, own, k_norm, acc, res, sem(name + "normed"))

                    @blk.gpsimd
                    def _(pool):
                        def split_up(i, k):
                            pool.wait_ge(sem(name + "w_hi"), i * 4 + (1 + k))
                            pool.tensor_tensor(wup_l[k][:, :, :, :], up_in[k][:, 0:n_up, :, :],
                                               wup_h[k][:, :, :, :].bitcast(F32),
                                               ALU.subtract).then_inc(sem(name + "w_lo"), 1)

                        def split_down(i, k):
                            pool.wait_ge(sem(name + "w_hi"), i * 4 + (3 + k))
                            pool.tensor_tensor(wdn_l[k][:, :, :], dn_in[k][:, :, :],
                                               wdn_h[k][:, :, :].bitcast(F32),
                                               ALU.subtract).then_inc(sem(name + "w_lo"), 1)

                        def pair(i, last=False):
                            for k in range(2):
                                split_down(i, k)
                            if not last:
                                for k in range(2):
                                    split_up(i + 1, k)

                        for k in range(2):
                            split_up(0, k)
                        with pool.Fori(0, pairs - 1) as i:
                            pair(i)
                        pair(pairs - 1, last=True)
                        pool_rstd(pool, k_norm)
                        if k_norm == 7:
                            dst = out.rearrange("b s d -> (b s) d").rearrange("(t p) d -> p t d", p=P)
                            for half in range(2):
                                pool.wait_ge(sem(name + "normed"), 4 * (half + 1))
                                pool.dma_start(dst[:, 4 * half:4 * half + 4, :],
                                               res[:, 4 * half:4 * half + 4, :]).then_inc(sem("stored"), 16)
                            pool.wait_ge(sem("stored"), 32)

        def init_b(v, own, acc, down, bias, ready):
            for t in range(NT):
                own.mark(v.tensor_tensor(acc[:, t, :], res[:, t, :], pre[:, t, :], ALU.add))
            for t in range(NT):
                own.sync()
                v.wait_ge(bias, t + 1)
                v.tensor_tensor(acc[:, t, :], down[t % 4][:, 0:D], acc[:, t, :], ALU.add).then_inc(ready, 1)

        mixture("m", MOE_B, False, init_b, 4)

        lay = ExitStack()
        with lay:
            win = sb("c_win", [P, KD, 2 * DI], ctx=lay)
            wx = sb("c_wx", [P, KI, 2 * NS], ctx=lay)
            wdt = sb("c_wdt", [P, KI, P], ctx=lay)
            wout = sb("c_wout", [P, KI, D], ctx=lay)
            cw = sb("c_cw", [P, KI, TAPS], ctx=lay)
            cols = sb("c_cols", [P, 4, KI], ctx=lay)
            alog = sb("c_alog", [P, KI, NS], ctx=lay)
            nega = sb("c_nega", [P, KI, NS], ctx=lay)
            sel = sb("c_sel", [P, 2 * NS, P], BF16, ctx=lay)
            xin = sb("c_xin", [P, KI, B, S + TAPS - 1], ctx=lay)
            gz = sb("c_gz", [P, KI, T], ctx=lay)
            xc = sb("c_xc", [P, KI, T], ctx=lay)
            dt = xin
            du = sb("c_du", [P, KI, T], ctx=lay)
            conv = [sb(f"c_conv{i}", [P, B, S], ctx=lay) for i in range(2)]
            bc_f = sb("c_bc_f", [2 * NS, T], ctx=lay)
            bc_p = sb("c_bc_p", [2 * NS, T], BF16, ctx=lay)
            bcs = sb("c_bcs", [P, T], BF16, ctx=lay)
            dg = sb("c_dg", [P, KI, P], ctx=lay)
            bs = [sb(f"c_bs{u}", [P, S], ctx=lay) for u in range(2)]
            da = [sb(f"c_da{m}", [P, S], ctx=lay) for m in range(KI)]
            dbu = [sb(f"c_dbu{m}", [P, S], ctx=lay) for m in range(KI)]
            st = [sb(f"c_st{m}", [P, S], ctx=lay) for m in range(KI)]
            hc = [sb(f"c_hc{m}", [P, S], ctx=lay) for m in range(KI)]
            ssq = sb("c_ssq", [P, NT], ctx=lay)
            yacc, bb, cb = bank[0:4], bank[4:6], bank[6:8]
            CB, DTW, DTB, DP = range(4)

            def by_b(x):
                return x.rearrange("p (b s) -> p b s", b=B)

            with nc.Block() as blk:
                @blk.sync
                def _(sp):
                    sp.dma_start(win[:, :, :], a["c_win"].rearrange("(k p) n -> p k n", p=P)).then_inc(sem("c_win"), 16)
                    sp.dma_start(cw[:, :, :], a["c_cw"]).then_inc(sem("c_small"), 16)
                    sp.dma_start(cols[:, :, :], a["c_cols"]).then_inc(sem("c_small"), 16)
                    sp.dma_start(alog[:, :, :], a["c_alog"]).then_inc(sem("c_small"), 16)
                    sp.dma_start(wx[:, :, :], a["c_wx"].rearrange("(k p) n -> p k n", p=P)).then_inc(sem("c_wx"), 16)
                    sp.dma_start(wdt[:, :, :], a["c_wdt"].rearrange("(k p) n -> p k n", p=P)).then_inc(sem("c_wx"), 16)
                    sp.dma_start(sel[:, :, :], a["c_sel"]).then_inc(sem("c_sel"), 16)
                    sp.dma_start(wout[:, :, :], a["c_wout"].rearrange("(k p) n -> p k n", p=P)).then_inc(sem("c_wout"), 16)
                    load_first("d", sp, True)

                @blk.tensor
                def _(pe):
                    transpose_tokens(pe, nrm, sem("c_nrm"), sem("c_turn"), base=0)
                    pe.wait_ge(sem("c_win"), 16)
                    pe.wait_ge(sem("c_xT"), 4)
                    for n in range(16):
                        m, b = n // 2, n % 2
                        if n >= 4:
                            pe.wait_ge(sem("c_in_out"), n - 3)
                        for kt in range(KD):
                            ins = pe.matmul(bank[4 + n % 4][:, :], win[:, kt, m * P:(m + 1) * P],
                                            xT[:, kt, b * S:(b + 1) * S], start=(kt == 0), stop=(kt == KD - 1))
                        ins.then_inc(sem("c_in"), 1)
                    pe.wait_ge(sem("c_wx"), 32)
                    pe.wait_ge(sem("c_xc"), KI)
                    for b in range(B):
                        for kt in range(KI):
                            ins = pe.matmul(bank[b][0:2 * NS, :], wx[:, kt, :], xc[:, kt, b * S:(b + 1) * S],
                                            start=(kt == 0), stop=(kt == KI - 1))
                        ins.then_inc(sem("c_bc"), 1)
                        for kt in range(KI):
                            ins = pe.matmul(bank[2 + b][:, :], wdt[:, kt, :], xc[:, kt, b * S:(b + 1) * S],
                                            start=(kt == 0), stop=(kt == KI - 1))
                        ins.then_inc(sem("c_step"), 1)

                    def spread(b, n, u):
                        cols_b = bcs[:, b * S:(b + 1) * S]
                        pe.matmul(bb[u][:, :], sel[:, ds(n, 1), :].rearrange("p a m -> p (a m)"), cols_b,
                                  start=True, stop=True).then_inc(sem("c_bb"), 1)
                        pe.matmul(cb[u][:, :], sel[:, ds(n + NS, 1), :].rearrange("p a m -> p (a m)"), cols_b,
                                  start=True, stop=True).then_inc(sem("c_cb"), 1)

                    def total(b, n, stop=False):
                        for m in range(KI):
                            pe.wait_ge(sem("c_hc"), n * KI + (b * NS * KI + KI + m + 1))
                            pe.matmul(yacc[m][:, :], ident[:, :], hc[m][:, :], start=False,
                                      stop=stop).then_inc(sem("c_sum"), 1)

                    def two(b, j, last):
                        for u in range(2):
                            total(b, j * 2 + u, last and u == 1)
                            if not last:
                                pe.wait_ge(sem("c_bs"), j * 2 + (b * NS + u + 1))
                                spread(b, j * 2 + (u + 2), u)

                    pe.wait_ge(sem("c_split"), 1)
                    pe.wait_ge(sem("c_sel"), 16)
                    pe.wait_ge(sem("c_hc"), KI)
                    pe.wait_ge(sem("c_v"), 2 * KI)
                    for b in range(B):
                        if b:
                            pe.wait_ge(sem("c_y"), KI)
                        spread(b, 0, 0)
                        spread(b, 1, 1)
                        for m in range(KI):
                            pe.matmul(yacc[m][:, :], dg[:, m, :], xc[:, m, b * S:(b + 1) * S], start=True,
                                      stop=False).then_inc(sem("c_sum"), 1)
                        with pe.Fori(0, NS // 2 - 1) as j:
                            two(b, j, False)
                        two(b, NS // 2 - 1, True)
                    pe.wait_ge(sem("c_wout"), 16)
                    pe.wait_ge(sem("c_y"), 2 * KI)
                    for t in range(NT):
                        if t >= 4:
                            pe.wait_ge(sem("c_pre"), t - 3)
                        for kt in range(KI):
                            ins = pe.matmul(bank[t % 4][:, 0:D], gz[:, kt, t * P:(t + 1) * P], wout[:, kt, :],
                                            start=(kt == 0), stop=(kt == KI - 1))
                        ins.then_inc(sem("c_oproj"), 1)
                    pe.wait_ge(sem("c_pre"), NT)
                    transpose_tokens(pe, res, sem("c_res"), sem("c_turn2"))

                @blk.scalar
                def _(act):
                    for t in range(NT):
                        act.activation(pre[:, t, :], res[:, t, :], ACT.Square,
                                       accum_out=ssq[:, t:t + 1]).then_inc(sem("c_ssq"), 1)
                    evac_transposed(act, 0, sem("c_turn"), sem("c_xT"), rmsw, None)
                    for n in range(16):
                        m, b = n // 2, n % 2
                        act.wait_ge(sem("c_in"), n + 1)
                        if m < KI:
                            act.activation(xin[:, m, b, TAPS - 1:], bank[4 + n % 4][:, :],
                                           ACT.Copy).then_inc(sem("c_in_out"), 1)
                        else:
                            act.activation(gz[:, m - KI, b * S:(b + 1) * S], bank[4 + n % 4][:, :],
                                           ACT.Silu).then_inc(sem("c_in_out"), 1)
                    for m in range(KI):
                        act.wait_ge(sem("c_conv"), m + 1)
                        act.activation(xc[:, m, :], conv[m % 2][:, :, :].rearrange("p b s -> p (b s)"),
                                       ACT.Silu).then_inc(sem("c_xc"), 1)
                    act.wait_ge(sem("c_small"), 48)
                    act.activation(nega[:, :, :], alog[:, :, :], ACT.Exp).then_inc(sem("c_ea"), 1)
                    for m in range(KI):
                        act.wait_ge(sem("c_nabs"), m + 1)
                        act.activation(du[:, m, :], du[:, m, :], ACT.Exp).then_inc(sem("c_e"), 1)
                    for m in range(KI):
                        act.wait_ge(sem("c_e"), m + 1)
                        act.activation(du[:, m, :], du[:, m, :], ACT.Ln, bias=1.0).then_inc(sem("c_l"), 1)

                    def copy_b(b, n, u):
                        act.wait_ge(sem("c_bb"), n + (b * NS + 1))
                        act.activation(bs[u][:, :], bb[u][:, :], ACT.Copy).then_inc(sem("c_bs"), 1)

                    def two(b, j, last):
                        for u in range(2):
                            for m in range(KI):
                                act.wait_ge(sem("c_scan"), j * (2 * KI) + (b * NS * KI + KI * u + m + 1))
                                act.wait_ge(sem("c_nega"), 1)
                                act.activation(da[m][:, :], dt[:, m, b, 0:S], ACT.Exp,
                                               scale=nega[:, m, ds(j * 2 + u, 1)]).then_inc(sem("c_da"), 1)
                            if not (last and u == 1):
                                act.wait_ge(sem("c_dbu"), j * (2 * KI) + (b * NS * KI + KI * u))
                                copy_b(b, j * 2 + (u + 1), (u + 1) % 2)

                    act.wait_ge(sem("c_dt"), KI)
                    for b in range(B):
                        if b:
                            act.wait_ge(sem("c_dbu"), NS * KI)
                        copy_b(b, 0, 0)
                        with act.Fori(0, NS // 2 - 1) as j:
                            two(b, j, False)
                        two(b, NS // 2 - 1, True)
                    evac_transposed(act, 0, sem("c_turn2"), sem("c_xT2"))

                @blk.vector
                def _(v):
                    own = Order(v, sem("v_own_c"))
                    own.mark(v.memset(xin[:, :, :, 0:TAPS - 1], 0.0))
                    own.mark(v.memset(bcs[:, :].bitcast(F32), 0.0))
                    v.wait_ge(sem("c_ssq"), NT)
                    v.tensor_scalar(var_eps[:, :], ssq[:, :], 1.0 / D, EPS, ALU.mult,
                                    ALU.add).then_inc(sem("var_ready"), 1)
                    v.wait_ge(sem("rstd_ready"), 5)
                    for t in range(NT):
                        v.tensor_scalar(nrm[:, t, :], res[:, t, :], rstd[:, t:t + 1], None,
                                        ALU.mult).then_inc(sem("c_nrm"), 1)
                    for half in range(2):
                        v.wait_ge(sem("c_turn"), half * KD + 2)
                        v.tensor_scalar(xT[:, 1, half * S:(half + 1) * S], bank[half * KD + 1][:, :],
                                        rmsw[:, 1:2], None, ALU.mult).then_inc(sem("c_xT"), 1)
                    v.wait_ge(sem("c_small"), 48)
                    for m in range(KI):
                        v.wait_ge(sem("c_in_out"), 2 * m + 2)
                        if m >= 2:
                            v.wait_ge(sem("c_xc"), m - 1)
                        own.mark(v.tensor_scalar(conv[m % 2][:, :, :], xin[:, m, :, 0:S], cw[:, m, 0:1], cols[:, CB, m:m + 1],
                                                 ALU.mult, ALU.add))
                        for k in range(1, TAPS):
                            own.sync()
                            ins = v.scalar_tensor_tensor(out=conv[m % 2][:, :, :], in0=xin[:, m, :, k:k + S],
                                                         scalar=cw[:, m, k:k + 1], in1=conv[m % 2][:, :, :],
                                                         op0=ALU.mult, op1=ALU.add)
                            if k < TAPS - 1:
                                own.mark(ins)
                            else:
                                ins.then_inc(sem("c_conv"), 1)
                    for m in range(KI):
                        v.tensor_scalar(dg[:, m, :], ident[:, :], cols[:, DP, m:m + 1], None,
                                        ALU.mult).then_inc(sem("c_hc"), 1)
                    v.wait_ge(sem("c_ea"), 1)
                    v.tensor_scalar(nega[:, :, :], nega[:, :, :], -1.0, None, ALU.mult).then_inc(sem("c_nega"), 1)
                    for b in range(B):
                        half = slice(b * S, (b + 1) * S)
                        v.wait_ge(sem("c_bc"), b + 1)
                        own.mark(v.tensor_copy(bcs[0:32, half], bank[b][0:32, :]))
                        own.sync()
                        own.mark(v.tensor_tensor(bc_f[:, half], bank[b][0:32, :], bcs[0:32, half], ALU.subtract))
                        own.sync()
                        own.mark(v.tensor_copy(bc_p[:, half], bc_f[:, half]))
                        own.sync()
                        own.mark(v.tensor_tensor(bc_f[:, half], bc_f[:, half], bc_p[:, half], ALU.subtract))
                        own.mark(v.tensor_copy(bcs[32:64, half], bc_p[:, half]))
                        own.sync()
                        own.mark(v.tensor_copy(bcs[64:96, half], bc_f[:, half]))
                    own.sync()
                    v.sem_inc(sem("c_split"), 1)
                    for m in range(KI):
                        for b in range(B):
                            v.wait_ge(sem("c_step"), b + 1)
                            v.tensor_scalar(dt[:, m, b, 0:S], bank[2 + b][:, :], cols[:, DTW, m:m + 1],
                                            cols[:, DTB, m:m + 1], ALU.mult, ALU.add).then_inc(sem("c_v"), 1)
                    for m in range(KI):
                        v.wait_ge(sem("c_v"), 2 * (m + 1))
                        v.scalar_tensor_tensor(out=by_b(du[:, m, :]), in0=dt[:, m, :, 0:S], scalar=-1.0,
                                               in1=dt[:, m, :, 0:S],
                                               op0=ALU.mult, op1=ALU.min).then_inc(sem("c_nabs"), 1)
                    for m in range(KI):
                        v.wait_ge(sem("c_l"), m + 1)
                        v.scalar_tensor_tensor(out=dt[:, m, :, 0:S], in0=dt[:, m, :, 0:S], scalar=0.0,
                                               in1=by_b(du[:, m, :]),
                                               op0=ALU.max, op1=ALU.add).then_inc(sem("c_dt"), 1)
                        v.wait_ge(sem("c_dt"), m + 1)
                        v.tensor_tensor(by_b(du[:, m, :]), dt[:, m, :, 0:S], by_b(xc[:, m, :]), ALU.mult).then_inc(sem("c_scan"), 1)

                    def scan(b, n, m):
                        done = b * NS * KI + m + 1
                        v.wait_ge(sem("c_da"), n * KI + done)
                        v.wait_ge(sem("c_dbu"), n * KI + done)
                        v.wait_ge(sem("c_hc"), n * KI + done)
                        v.tensor_tensor_scan(st[m][:, :], da[m][:, :], dbu[m][:, :], 0.0, ALU.mult,
                                             ALU.add).then_inc(sem("c_scan"), 1)

                    def times_c(b, n, m, u):
                        done = b * NS * KI + m + 1
                        v.wait_ge(sem("c_scan"), n * KI + (KI + done))
                        if m == 0:
                            v.wait_ge(sem("c_cb"), n + (b * NS + 1))
                        v.wait_ge(sem("c_sum"), n * KI + (b * (NS + 1) * KI + m + 1))
                        v.tensor_tensor(hc[m][:, :], st[m][:, :], cb[u][:, :], ALU.mult).then_inc(sem("c_hc"), 1)

                    def two(b, j):
                        for u in range(2):
                            n = j * 2 + u
                            scan(b, n, 0)
                            for m in range(1, KI):
                                scan(b, n, m)
                                times_c(b, n, m - 1, u)
                            times_c(b, n, KI - 1, u)

                    for b in range(B):
                        with v.Fori(0, NS // 2) as j:
                            two(b, j)
                        for m in range(KI):
                            v.wait_ge(sem("c_sum"), (NS + 1) * KI * (b + 1) - KI + m + 1)
                            z = gz[:, m, b * S:(b + 1) * S]
                            v.tensor_tensor(z, yacc[m][:, :], z, ALU.mult).then_inc(sem("c_y"), 1)
                    for t in range(NT):
                        v.wait_ge(sem("c_oproj"), t + 1)
                        v.scalar_tensor_tensor(out=pre[:, t, :], in0=res[:, t, :], scalar=2.0,
                                               in1=bank[t % 4][:, 0:D], op0=ALU.mult,
                                               op1=ALU.add).then_inc(sem("c_pre"), 1)
                        v.wait_ge(sem("c_pre"), t + 1)
                        norm_stats(v, own, t, pre)
                    norm_apply(v, own, 6, pre, res, sem("c_res"))
                    evac_transposed(v, 1, sem("c_turn2"), sem("c_xT2"))

                @blk.gpsimd
                def _(pool):
                    pool_rstd(pool, 5)

                    def inputs(b, n, u):
                        pool.wait_ge(sem("c_bs"), n + (b * NS + 1))
                        for m in range(KI):
                            pool.wait_ge(sem("c_scan"), n * KI + (b * NS * KI + m + 1))
                            pool.tensor_tensor(dbu[m][:, :], du[:, m, b * S:(b + 1) * S], bs[u][:, :],
                                               ALU.mult).then_inc(sem("c_dbu"), 1)

                    pool.wait_ge(sem("c_scan"), KI)
                    for b in range(B):
                        with pool.Fori(0, NS // 2) as j:
                            for u in range(2):
                                inputs(b, j * 2 + u, u)
                    pool_rstd(pool, 6)

        def init_d(v, own, acc, down, bias, ready):
            for t in range(NT):
                v.tensor_copy(acc[:, t, :], res[:, t, :]).then_inc(ready, 1)

        mixture("d", MOE_D, True, init_d, 7)


def kernel(**inputs):
    import numpy as np
    import concourse.bacc as bacc
    from concourse import mybir as _mybir
    from concourse.bass_utils import run_bass_kernel_spmd as run

    x = {k: np.asarray(v) for k, v in inputs.items()}
    bf16 = _mybir.dt.np(_mybir.dt.bfloat16) if hasattr(_mybir.dt, "np") else None
    import ml_dtypes
    bf16 = ml_dtypes.bfloat16
    f32 = np.float32
    arrays = {}

    def put(name, v):
        arrays["in_" + name] = np.ascontiguousarray(v)

    tok = x["L0_attn_hidden_states"].reshape(T, D)
    put("x", tok)
    put("xT", tok.T)

    def by_part(v):
        return v.reshape(-1, P).T

    put("ident", np.eye(P, dtype=f32))
    put("ident_bf", np.eye(P).astype(bf16))
    put("mask_bf", np.where(np.arange(P)[None, :] > np.arange(P)[:, None], -1e30, 0.0).astype(bf16))
    put("iota", np.broadcast_to(np.arange(8, dtype=f32), (P, 8)))
    sel = np.zeros((P, 2 * NS, P), f32)
    for n in range(2 * NS):
        sel[[n, 32 + n, 64 + n], n, :] = 1.0
    put("c_sel", sel.astype(bf16))
    inv = f32(1.0) / np.power(f32(10000.0), np.arange(0, B_HD, 2, dtype=f32) / f32(B_HD)).astype(f32)
    ang = np.arange(S, dtype=f32)[:, None] * inv[None, :]
    cos = np.concatenate([np.cos(ang), np.cos(ang)], 1).T.astype(f32)
    sin = np.concatenate([-np.sin(ang), np.sin(ang)], 1).T.astype(f32)
    sc = 1.0 / np.sqrt(float(B_HD))
    put("b_rope", np.stack([np.stack([cos * sc, sin * sc]), np.stack([cos, sin])]).transpose(2, 0, 1, 3).astype(f32))

    w = x["L0_attn_w_qkv"].reshape(3, A_GROUPS, A_G, A_HD, KD, P)
    wqkv = np.zeros((A_GROUPS, P, 3, KD, A_G, 32), f32)
    wqkv[..., 0:A_HD] = w.transpose(1, 5, 0, 4, 2, 3)
    put("a_wqkv", wqkv.reshape(A_GROUPS, P, 3, KD, P))
    wo = np.zeros((A_GROUPS, A_G, 32, D), f32)
    wo[:, :, 0:A_HD] = x["L0_attn_w_o"].T.reshape(A_GROUPS, A_G, A_HD, D)
    put("a_wo", wo.reshape(A_GROUPS * P, D))
    for n, k in (("ln1w", "ln1_w"), ("ln1b", "ln1_b"), ("ln2w", "ln2_w"), ("ln2b", "ln2_b")):
        put(n, by_part(x["L0_ffn_" + k]))
    wq, wk, wv = (x["L0_ffn_" + n].reshape(KD, P, B_H, B_HD) for n in ("wq", "wk", "wv"))
    put("b_wqk", np.stack([wq, wk]).transpose(3, 2, 0, 1, 4))
    put("b_wv", wv.transpose(2, 1, 0, 3))
    bq, bk = (x["L0_ffn_" + n].reshape(B_H, 2, P // 2) for n in ("bq", "bk"))
    both = np.stack([bq, bk])
    put("b_bqk", np.stack([both, both[:, :, ::-1]], 1).reshape(2, 2, B_H, P).transpose(3, 0, 1, 2))
    put("b_bv", by_part(x["L0_ffn_bv"]))
    put("b_bo", x["L0_ffn_bo"])
    put("b_wo", x["L0_ffn_wo"])
    put("m_wr", x["L0_ffn_w_gate"])
    put("m_wup", x["L0_ffn_we1"].reshape(MOE_B, 1, KD, P, F).transpose(0, 3, 1, 2, 4))
    put("m_wdn", x["L0_ffn_we2"].reshape(MOE_B, KF, P, D).transpose(0, 2, 1, 3))
    put("m_b1", x["L0_ffn_be1"].reshape(MOE_B, KF, P).transpose(2, 1, 0))
    put("m_b2", x["L0_ffn_be2"])
    put("rmsw", by_part(x["L1_attn_norm_w"]))
    put("c_win", x["L1_attn_in_proj_w"].T)
    put("c_wx", x["L1_attn_x_proj_w"][0:2 * NS].T)
    put("c_wdt", np.broadcast_to(x["L1_attn_x_proj_w"][2 * NS][:, None], (DI, P)))
    put("c_wout", x["L1_attn_out_proj_w"].T)
    put("c_cw", x["L1_attn_conv_w"].reshape(KI, P, TAPS).transpose(1, 0, 2))
    put("c_cols", np.stack([by_part(x["L1_attn_conv_b"]), by_part(x["L1_attn_dt_w"].reshape(-1)),
                            by_part(x["L1_attn_dt_b"]), by_part(x["L1_attn_D_param"])], 1))
    put("c_alog", x["L1_attn_A_log"].reshape(KI, P, NS).transpose(1, 0, 2))
    put("d_wr", x["L1_ffn_Wr"])
    put("d_wup", np.stack([x["L1_ffn_Wg"], x["L1_ffn_Wu"]], 1).reshape(MOE_D, 2, KD, P, F).transpose(0, 3, 1, 2, 4))
    put("d_wdn", x["L1_ffn_Wd"].reshape(MOE_D, KF, P, D).transpose(0, 2, 1, 3))

    nc = bacc.Bacc("TRN2", target_bir_lowering=False, num_devices=1)
    aps = {n[3:]: nc.dram_tensor(n, v.shape, _mybir.dt.from_np(v.dtype), kind="ExternalInput").ap()
           for n, v in arrays.items()}
    out = nc.dram_tensor("out_0_dram", (B, S, D), _mybir.dt.float32, kind="ExternalOutput").ap()
    build_program(nc, aps, out)
    r = run(nc, [arrays], core_ids=[0])
    return r.results[0]["out_0_dram"]
```

```python
from contextlib import ExitStack

import concourse.bass as bass
from concourse import mybir

ALU = mybir.AluOpType
ACT = mybir.ActivationFunctionType
AX = mybir.AxisListType
F32 = mybir.dt.float32
F32R = mybir.dt.float32r
BF16 = mybir.dt.bfloat16
U32 = mybir.dt.uint32
ds = bass.ds

P = 128
D = 256
KD = D // P
T = 1024
NT = T // P
B = 2
S = T // B
QT = S // P
EPS = 1e-5

A_H, A_HD = 16, 16
A_G = 4
A_GROUPS = A_H // A_G
A_STEPS = B * A_G * QT
B_H, B_HD = 16, 128
B_STEPS = B * QT
MOE_B, MOE_D = 4, 8
F = 256
KF = F // P
DI = 512
KI = DI // P
NS = 16
TAPS = 4


class Order:

    def __init__(self, eng, sem, base=0):
        self.eng, self.sem, self.base, self.n = eng, sem, base, 0

    def mark(self, ins):
        ins.then_inc(self.sem, 1)
        self.n += 1

    def sync(self, behind=0):
        self.eng.wait_ge(self.sem, self.base + (self.n - behind))


def build_program(nc, a, out):
    top = ExitStack()
    with top:
        def sb(name, shape, dt=F32, ctx=top):
            return ctx.enter_context(nc.sbuf_tensor(name, shape, dt))

        sems = {}

        def sem(name):
            if name not in sems:
                sems[name] = top.enter_context(nc.semaphore(name))
            return sems[name]

        psum = top.enter_context(nc.psum_tensor("psum", [P, 8, 512], F32))
        bank = [psum[:, i, :] for i in range(8)]

        ident = sb("ident", [P, P])
        ident_bf = sb("ident_bf", [P, P], BF16)
        mask_bf = sb("mask_bf", [P, P], BF16)
        iota = sb("iota", [P, 8])
        power = sb("power", [P, NT])
        res = sb("res", [P, NT, D])
        pre = sb("pre", [P, NT, D])
        nrm = sb("nrm", [P, NT, D])
        xT = sb("xT", [P, KD, T])
        xh, xl = sb("xh", [P, KD, T], F32R), sb("xl", [P, KD, T], F32R)
        routers = {"m": sb("m_wr", [P, KD, MOE_B]), "d": sb("d_wr", [P, KD, MOE_D])}
        b1, b2 = sb("m_b1", [P, KF, MOE_B]), sb("m_b2", [MOE_B, D])
        up_in = [sb(f"up_in{k}", [P, 2, KD, F]) for k in range(2)]
        dn_in = [sb(f"dn_in{k}", [P, KF, D]) for k in range(2)]
        stats = sb("stats", [P, NT, 6])
        mv = sb("mv", [P, NT, 2])
        var_eps = sb("var_eps", [P, NT])
        rstd = sb("rstd", [P, NT])
        ln1w, ln1b = sb("ln1w", [P, KD]), sb("ln1b", [P, KD])
        ln2w, ln2b = sb("ln2w", [P, KD]), sb("ln2b", [P, KD])
        rmsw = sb("rmsw", [P, KD])
        probs8 = sb("probs8", [P, NT, 8])
        top8 = sb("top8", [P, NT, 8])
        idx8 = sb("idx8", [P, NT, 8], U32)
        idxf = sb("idxf", [P, NT, 2])
        comb = sb("comb", [P, NT, 8])
        pick = sb("pick", [P, NT, 8])
        row1 = sb("row1", [P, NT])
        row2 = sb("row2", [P, NT])
        wts = sb("wts", [P, NT, 2])


        def load_first(tag, sp, gated):
            name = tag + "_"
            n_up = 2 if gated else 1
            sp.dma_start(routers[tag][:, :, :], a[name + "wr"].rearrange("(k p) e -> p k e", p=P)).then_inc(sem(name + "small"), 16)
            if not gated:
                sp.dma_start(b1[:, :, :], a[name + "b1"]).then_inc(sem(name + "small"), 16)
                sp.dma_start(b2[:, :], a[name + "b2"]).then_inc(sem(name + "small"), 16)
            for k in range(2):
                sp.dma_start(up_in[k][:, 0:n_up, :, :], a[name + "wup"][k]).then_inc(sem(f"{name}wup{k}"), 16)
            for k in range(2):
                sp.dma_start(dn_in[k][:, :, :], a[name + "wdn"][k]).then_inc(sem(f"{name}wdn{k}"), 16)

        HT = NT // 2

        def norm_var(v, own, half, var, scale=None):
            own.sync()
            dst = var_eps[:, half * HT:(half + 1) * HT]
            if scale is None:
                ins = v.tensor_scalar(dst, var, EPS, None, ALU.add)
            else:
                ins = v.tensor_scalar(dst, var, scale, EPS, ALU.mult, ALU.add)
            ins.then_inc(sem("var_ready"), 1)

        def norm_stats(v, own, t, src):
            own.mark(v.bn_stats(stats[:, t, :], src[:, t, :]))
            own.sync()
            own.mark(v.bn_aggr(mv[:, t, :], stats[:, t, :]))
            if t % HT == HT - 1:
                norm_var(v, own, t // HT, mv[:, t - HT + 1:t + 1, 1])

        def norm_apply(v, own, k, src, dst, ready=None):
            for t in range(NT):
                if t % HT == 0:
                    v.wait_ge(sem("rstd_ready"), 2 * k - 1 + t // HT)
                ins = v.tensor_scalar(dst[:, t, :], src[:, t, :], mv[:, t, 0:1], rstd[:, t:t + 1],
                                      ALU.subtract, ALU.mult)
                if ready is not None:
                    ins.then_inc(ready, 1)
                else:
                    own.mark(ins)

        def pool_rstd(pool, k):
            for half in range(2):
                part_t = slice(half * HT, (half + 1) * HT)
                pool.wait_ge(sem("var_ready"), 2 * k - 1 + half)
                pool.tensor_tensor(rstd[:, part_t], var_eps[:, part_t], power[:, part_t],
                                   ALU.pow).then_inc(sem("rstd_ready"), 1)

        def transpose_tokens(pe, src, src_ready, done, kt_n=KD, base=0):
            for half in range(2):
                for kt in range(kt_n):
                    pe.wait_ge(src_ready, 4 * (half + 1))
                    for j in range(4):
                        ins = pe.transpose(bank[base + half * kt_n + kt][:, j * P:(j + 1) * P],
                                           src[:, 4 * half + j, kt * P:(kt + 1) * P], ident[:, :])
                    ins.then_inc(done, 1)

        def evac_act(act, k, done, scale=None, bias=None):
            for half in range(B):
                cols_x = slice(half * S, (half + 1) * S)
                act.wait_ge(done, half * KD + 1)
                act.activation(xT[:, 0, cols_x], bank[half * KD][:, :], ACT.Identity,
                               bias=bias[:, 0:1] if bias is not None else 0.0,
                               scale=scale[:, 0:1] if scale is not None else 1.0).then_inc(sem("x0_whole"), 1)
                act.wait_ge(sem("x0_whole"), 2 * k + half + 1)
                act.activation(xh[:, 0, cols_x], xT[:, 0, cols_x], ACT.Copy).then_inc(sem("x0_hi"), 1)

        def evac_dve(v, own, k, done, ready, scale=None, bias=None):
            for half in range(B):
                cols_x = slice(half * S, (half + 1) * S)
                src, dst = bank[half * KD + 1][:, :], xT[:, 1, cols_x]
                v.wait_ge(done, half * KD + 2)
                if scale is None:
                    own.mark(v.tensor_copy(dst, src))
                elif bias is None:
                    own.mark(v.tensor_scalar(dst, src, scale[:, 1:2], None, ALU.mult))
                else:
                    own.mark(v.tensor_scalar(dst, src, scale[:, 1:2], bias[:, 1:2], ALU.mult, ALU.add))
                own.sync()
                own.mark(v.tensor_copy(xh[:, 1, cols_x], xT[:, 1, cols_x]))
                own.sync()
                for kt in (1, 0):
                    if kt == 0:
                        v.wait_ge(sem("x0_hi"), 2 * k + half + 1)
                    v.tensor_tensor(xl[:, kt, cols_x], xT[:, kt, cols_x], xh[:, kt, cols_x].bitcast(F32),
                                    ALU.subtract).then_inc(ready, 1)

        ahead_b = ExitStack()
        wqk = sb("b_wqk", [P, 2, KD, P], ctx=ahead_b)
        wv = sb("b_wv", [P, KD, 2 * P], ctx=ahead_b)
        rope = sb("b_rope", [P, 2, 2, S], ctx=ahead_b)
        bqk = sb("b_bqk", [P, 2, 2, B_H], ctx=ahead_b)
        bv = sb("b_bv", [P, B_H], ctx=ahead_b)
        bo = sb("b_bo", [P, D], ctx=ahead_b)
        wqk_h = sb("b_wqk_h", [P, 2, KD, P], F32R, ctx=ahead_b)
        wqk_l = sb("b_wqk_l", [P, 2, KD, P], F32R, ctx=ahead_b)
        wv_h = sb("b_wv_h", [P, KD, 2 * P], F32R, ctx=ahead_b)
        wv_l = sb("b_wv_l", [P, KD, 2 * P], F32R, ctx=ahead_b)

        def load_rotary(sp):
            sp.dma_start(wqk[:, :, :, :], a["b_wqk"][0]).then_inc(sem("b_wqk"), 16)
            sp.dma_start(wv[:, :, :], a["b_wv"][0]).then_inc(sem("b_wv"), 16)
            sp.dma_start(rope[:, :, :, :], a["b_rope"]).then_inc(sem("b_small"), 16)
            sp.dma_start(bqk[:, :, :, :], a["b_bqk"]).then_inc(sem("b_small"), 16)
            sp.dma_start(bv[:, :], a["b_bv"]).then_inc(sem("b_small"), 16)
            sp.dma_start(bo[:, :], a["b_bo"].partition_broadcast(P)).then_inc(sem("b_small"), 16)

        lay = ExitStack()
        with lay:
            wqkv = sb("a_wqkv", [P, 3, KD, P], ctx=lay)
            wo = sb("a_wo", [P, A_GROUPS, D], ctx=lay)
            qT = [sb(f"a_qT{b}", [P, S], F32R, ctx=lay) for b in range(B)]
            q_h = [sb(f"a_q_h{b}", [P, S], F32R, ctx=lay) for b in range(B)]
            q_second = [sb(f"a_q_second{b}", [P, S], ctx=lay) for b in range(B)]
            kf = [sb(f"a_kf{b}", [P, S], ctx=lay) for b in range(B)]
            k_h = [sb(f"a_k_h{b}", [P, A_G, S], F32R, ctx=lay) for b in range(B)]
            k_l = [sb(f"a_k_l{b}", [P, A_G, S], F32R, ctx=lay) for b in range(B)]
            halves = sb("a_halves", [P, 2], ctx=lay)
            val = [sb(f"a_val{b}", [P, QT, P], ctx=lay) for b in range(B)]
            attT = sb("a_attT", [P, A_GROUPS, T], ctx=lay)
            pr = [sb(f"a_pr{i}", [P, S], ctx=lay) for i in range(3)]
            prT = [sb(f"a_prT{i}", [P, S], ctx=lay) for i in range(2 * A_G)]
            nmax = sb("a_nmax", [P, A_STEPS], ctx=lay)
            ssum = sb("a_ssum", [P, A_STEPS], ctx=lay)
            rsum = sb("a_rsum", [P, A_STEPS], ctx=lay)
            rwide = [sb(f"a_rwide{b}", [P, QT * A_G, 32], ctx=lay) for b in range(B)]
            rT = sb("a_rT", [P, S], ctx=lay)
            sc, tp, ob, x0, x1 = bank[0:3], bank[3:5], bank[5], bank[6], bank[7]
            HALF = A_STEPS // B

            def step(s):
                return s // HALF, s // A_G % QT, s % A_G

            def on_act(s):
                return s % A_G == A_G - 1


            with nc.Block() as blk:
                @blk.sync
                def _(sp):
                    sp.dma_start(wqkv[:, :, :, :], a["a_wqkv"][0]).then_inc(sem("a_w"), 16)
                    sp.dma_start(halves[:, :], a["a_halves"]).then_inc(sem("a_x0"), 16)
                    for half in range(2):
                        for kt in range(KD):
                            sp.dma_start(xT[:, kt, half * S:(half + 1) * S],
                                         a["xT"][kt * P:(kt + 1) * P, half * S:(half + 1) * S]).then_inc(sem(f"a_x{half}"), 16)
                    for dst, name in ((ident_bf, "ident_bf"), (mask_bf, "mask_bf"), (ident, "ident")):
                        sp.dma_start(dst[:, :], a[name]).then_inc(sem("a_x1"), 16)
                    for dst, name in ((ln1w, "ln1w"), (ln1b, "ln1b"), (ln2w, "ln2w"), (ln2b, "ln2b"), (rmsw, "rmsw"),
                                      (iota, "iota")):
                        sp.dma_start(dst[:, :], a[name]).then_inc(sem("a_late"), 16)
                    sp.dma_start(wo[:, :, :], a["a_wo"].rearrange("(g p) n -> p g n", p=P)).then_inc(sem("a_late"), 16)
                    sp.dma_start(res[:, :, :], a["x"].rearrange("(t p) d -> p t d", p=P)).then_inc(sem("a_late"), 16)
                    with sp.Fori(1, A_GROUPS) as g:
                        src = a["a_wqkv"][ds(g, 1), :, :, :, :].rearrange("a p c k n -> p (a c k) n")
                        sp.wait_ge(sem("a_x1_in"), g * 3)
                        sp.dma_start(wqkv[:, :, :, :].rearrange("p c k n -> p (c k) n"), src).then_inc(sem("a_w"), 16)
                    load_rotary(sp)

                @blk.tensor
                def _(pe):
                    def project(g, b, c):
                        for kt in range(KD):
                            ins = pe.matmul((x0, x1)[c], wqkv[:, c, kt, :], xT[:, kt, b * S:(b + 1) * S],
                                            start=(kt == 0), stop=(kt == KD - 1))
                        ins.then_inc(sem("a_x0_in" if c == 0 else "a_x1_in"), 1)

                    def values(g, b):
                        for j in range(QT):
                            for kt in range(KD):
                                ins = pe.matmul((x0, x1)[b][:, j * P:(j + 1) * P],
                                                xT[:, kt, (b * QT + j) * P:(b * QT + j + 1) * P], wqkv[:, 2, kt, :],
                                                start=(kt == 0), stop=(kt == KD - 1))
                        ins.then_inc(sem("a_x0_in" if b == 0 else "a_x1_in"), 1)

                    def inverse_sums(g, b):
                        pe.wait_ge(sem("a_rwide"), g * 2 + (b + 1))
                        for i in range(QT):
                            ins = pe.transpose(x0[:, i * P:(i + 1) * P],
                                               rwide[b][:, i * A_G:(i + 1) * A_G, :].rearrange("p h d -> p (h d)"),
                                               ident[:, :])
                        ins.then_inc(sem("a_x0_in"), 1)

                    def scores(g, s):
                        b, i, h = step(s)
                        if s % HALF == 0:
                            pe.wait_ge(sem("a_q"), g * 2 + (b + 1))
                            pe.wait_ge(sem("a_k_lo"), g * 4 + 2 * (b + 1))
                            pe.wait_ge(sem("a_k_lo_pool"), g * 4 + 2 * (b + 1))
                        w = (i + 1) * P
                        pe.matmul(sc[s % 3][:, 0:w], qT[b][:, i * P:w], k_h[b][:, h, 0:w], start=True, stop=False)
                        pe.matmul(sc[s % 3][:, 0:w], qT[b][:, i * P:w], k_l[b][:, h, 0:w], start=False, stop=False)
                        pe.matmul(sc[s % 3][:, i * P:w], ident_bf[:, :], mask_bf[:, :],
                                  start=False, stop=True).then_inc(sem("a_scores"), 1)

                    def wait_taken(g, s):
                        if on_act(s):
                            pe.wait_ge(sem("a_prT_act"), g * (A_STEPS // A_G) + (s // A_G + 1))
                        else:
                            pe.wait_ge(sem("a_prT_dve"), g * (A_STEPS - A_STEPS // A_G) + (s - s // A_G + 1))

                    def turn(g, s):
                        pe.wait_ge(sem("a_exp"), g * A_STEPS + (s + 1))
                        if s >= 2:
                            wait_taken(g, s - 2)
                        for j in range(step(s)[1] + 1):
                            ins = pe.transpose(tp[s % 2][:, j * P:(j + 1) * P], pr[s % 3][:, j * P:(j + 1) * P],
                                               ident[:, :])
                        ins.then_inc(sem("a_turned"), 1)

                    def weigh(g, e):
                        b, i = e // QT, e % QT
                        wait_taken(g, A_G * e + A_G - 2)
                        wait_taken(g, A_G * e + A_G - 1)
                        if i == 0:
                            pe.wait_ge(sem("a_x0_out"), g * 5 + 2)
                            pe.wait_ge(sem("a_x1_out"), g * 3 + 3)
                            pe.wait_ge(sem("a_out"), g * 2 + (b + 1))
                        for j in range(i + 1):
                            for h in range(A_G):
                                ins = pe.matmul(ob[32 * h:32 * h + 32, i * P:(i + 1) * P],
                                                val[b][:, j, 32 * h:32 * h + 32],
                                                prT[(A_G * e + h) % (2 * A_G)][:, j * P:(j + 1) * P],
                                                start=(j == 0), stop=(j == i))
                        ins.then_inc(sem("a_weighed"), 1)

                    def group(g, last):
                        for s in range(A_STEPS):
                            scores(g, s)
                            if s >= 2:
                                turn(g, s - 2)
                            if s == HALF + 3:
                                pe.wait_ge(sem("a_x0_out"), g * 5 + 3)
                                inverse_sums(g, 0)
                            if s % A_G == 3 and s > A_G:
                                weigh(g, s // A_G - 1)
                        if not last:
                            pe.wait_ge(sem("a_w"), g * 16 + 32)
                            pe.wait_ge(sem("a_x0_out"), g * 5 + 4)
                            project(g + 1, 0, 0)
                            project(g + 1, 0, 1)
                        turn(g, A_STEPS - 2)
                        if not last:
                            pe.wait_ge(sem("a_x0_out"), g * 5 + 5)
                            values(g + 1, 0)
                        turn(g, A_STEPS - 1)
                        if not last:
                            pe.wait_ge(sem("a_x1_out"), g * 3 + 4)
                            project(g + 1, 1, 1)
                            pe.wait_ge(sem("a_x0_out"), g * 5 + 6)
                            project(g + 1, 1, 0)
                        weigh(g, 2 * QT - 1)
                        if not last:
                            pe.wait_ge(sem("a_x1_out"), g * 3 + 5)
                            values(g + 1, 1)
                        pe.wait_ge(sem("a_x0_out"), g * 5 + (4 if last else 7))
                        inverse_sums(g, 1)

                    pe.wait_ge(sem("a_w"), 16)
                    pe.wait_ge(sem("a_x0"), 48)
                    project(0, 0, 0)
                    project(0, 0, 1)
                    pe.wait_ge(sem("a_x0_out"), 1)
                    values(0, 0)
                    pe.wait_ge(sem("a_x1"), 80)
                    pe.wait_ge(sem("a_x1_out"), 1)
                    project(0, 1, 1)
                    pe.wait_ge(sem("a_x0_out"), 2)
                    project(0, 1, 0)
                    pe.wait_ge(sem("a_x1_out"), 2)
                    values(0, 1)
                    pe.wait_ge(sem("a_x1"), 80)
                    with pe.Fori(0, A_GROUPS - 1) as g:
                        group(g, False)
                    group(A_GROUPS - 1, True)

                    pe.wait_ge(sem("a_late"), 128)
                    pe.wait_ge(sem("a_out"), 2 * A_GROUPS)
                    for t in range(NT):
                        if t == QT:
                            pe.wait_ge(sem("a_out"), 2 * A_GROUPS + 1)
                        if t >= 4:
                            pe.wait_ge(sem("a_pre"), t - 3)
                        for g in range(A_GROUPS):
                            ins = pe.matmul(bank[t % 4][:, 0:D], attT[:, g, t * P:(t + 1) * P], wo[:, g, :],
                                            start=(g == 0), stop=(g == A_GROUPS - 1))
                        ins.then_inc(sem("a_oproj"), 1)
                    pe.wait_ge(sem("a_pre"), NT)
                    transpose_tokens(pe, nrm, sem("a_nrm"), sem("a_turn2"))

                @blk.scalar
                def _(act):
                    def take(dst, n, scale=1.0):
                        act.wait_ge(sem("a_x0_in"), n)
                        act.activation(dst, x0, ACT.Copy, scale=scale).then_inc(sem("a_x0_out"), 1)

                    q_scale = float(A_HD) ** -0.5

                    def take_queries(b, n):
                        act.wait_ge(sem("a_x0_in"), n)
                        act.activation(q_h[b][:, :], x0, ACT.Copy, scale=q_scale)
                        act.activation(q_second[b][:, :], x0, ACT.Identity,
                                       scale=halves[:, 1:2]).then_inc(sem("a_x0_out"), 1)

                    def group(g, last):
                        for s in range(A_STEPS + 2):
                            if s < A_STEPS:
                                w = (step(s)[1] + 1) * P
                                act.wait_ge(sem("a_max"), g * A_STEPS + (s + 1))
                                if s >= 3:
                                    act.wait_ge(sem("a_turned"), g * A_STEPS + (s - 2))
                                act.activation(pr[s % 3][:, 0:w], sc[s % 3][:, 0:w], ACT.Exp, bias=nmax[:, s:s + 1],
                                               scale=1.0, accum_out=ssum[:, s:s + 1]).then_inc(sem("a_exp"), 1)
                            if s == A_STEPS and not last:
                                take_queries(0, g * 5 + 5)
                            if s >= 2 and on_act(s - 2):
                                w = (step(s - 2)[1] + 1) * P
                                act.wait_ge(sem("a_turned"), g * A_STEPS + (s - 1))
                                act.activation(prT[(s - 2) % (2 * A_G)][:, 0:w], tp[s % 2][:, 0:w],
                                               ACT.Copy).then_inc(sem("a_prT_act"), 1)
                            if s == HALF + 4:
                                take(rT[:, :], g * 5 + 4)
                            if s == A_STEPS and not last:
                                take(val[0][:, :, :].rearrange("p t d -> p (t d)"), g * 5 + 6)
                        if not last:
                            take_queries(1, g * 5 + 7)
                        act.wait_ge(sem("a_out"), g * 2 + 2)
                        take(rT[:, :], g * 5 + (5 if last else 8))

                    act.wait_ge(sem("a_x0"), 48)
                    take_queries(0, 1)
                    take(val[0][:, :, :].rearrange("p t d -> p (t d)"), 2)
                    take_queries(1, 3)
                    with act.Fori(0, A_GROUPS - 1) as g:
                        group(g, False)
                    group(A_GROUPS - 1, True)
                    act.wait_ge(sem("b_wqk"), 16)
                    act.activation(wqk_h[:, :, :, :], wqk[:, :, :, :], ACT.Copy).then_inc(sem("b_wqk_hi"), 1)
                    act.wait_ge(sem("b_wv"), 16)
                    act.activation(wv_h[:, :, :], wv[:, :, :], ACT.Copy).then_inc(sem("b_wv_hi"), 1)
                    act.wait_ge(sem("a_late"), 128)
                    evac_act(act, 0, sem("a_turn2"), ln1w, ln1b)

                @blk.vector
                def _(v):
                    own = Order(v, sem("v_own"))

                    def take(dst, n):
                        v.wait_ge(sem("a_x1_in"), n)
                        v.tensor_copy(dst, x1).then_inc(sem("a_x1_out"), 1)

                    def take_keys(g, b, n):
                        take(kf[b][:, :], n)
                        v.wait_ge(sem("a_x1_out"), n)
                        for h in range(A_G):
                            rows = slice(32 * h, 32 * h + 32)
                            v.tensor_copy(k_h[b][rows, h, :], kf[b][rows, :]).then_inc(sem("a_k_hi"), 1)
                        for h in range(2):
                            rows = slice(32 * h, 32 * h + 32)
                            v.wait_ge(sem("a_k_hi"), g * 8 + (4 * b + 1 + h))
                            v.tensor_tensor(k_l[b][rows, h, :], kf[b][rows, :], k_h[b][rows, h, :].bitcast(F32),
                                            ALU.subtract).then_inc(sem("a_k_lo"), 1)

                    def join_queries(b, n):
                        v.wait_ge(sem("a_x0_out"), n)
                        v.scalar_tensor_tensor(out=qT[b][:, :], in0=q_h[b][:, :].bitcast(F32), scalar=halves[:, 0:1],
                                               in1=q_second[b][:, :], op0=ALU.mult,
                                               op1=ALU.add).then_inc(sem("a_q"), 1)

                    def widen(g, b):
                        cols = slice(b * HALF, (b + 1) * HALF)
                        v.wait_ge(sem("a_exp"), g * A_STEPS + HALF * (b + 1))
                        v.reciprocal(rsum[:, cols], ssum[:, cols]).then_inc(sem("a_rsum"), 1)
                        v.wait_ge(sem("a_rsum"), g * 2 + (b + 1))
                        v.tensor_copy(rwide[b][:, :, :], rsum[:, cols].unsqueeze(2).to_broadcast([P, HALF, 32])
                                      ).then_inc(sem("a_rwide"), 1)

                    def results(g, b, n):
                        v.wait_ge(sem("a_weighed"), g * (2 * QT) + QT * (b + 1))
                        v.wait_ge(sem("a_x0_out"), n)
                        v.tensor_tensor(attT[:, ds(g, 1), b * S:(b + 1) * S].rearrange("p a s -> p (a s)"), ob,
                                        rT[:, :], ALU.mult).then_inc(sem("a_out"), 1)

                    def group(g, last):
                        for s in range(A_STEPS + 2):
                            if s < A_STEPS:
                                w = (step(s)[1] + 1) * P
                                v.wait_ge(sem("a_scores"), g * A_STEPS + (s + 1))
                                v.tensor_reduce(nmax[:, s:s + 1], sc[s % 3][:, 0:w], AX.X, ALU.max,
                                                negate=True).then_inc(sem("a_max"), 1)
                            if s == A_STEPS and not last:
                                take_keys(g + 1, 0, g * 3 + 4)
                                join_queries(0, g * 5 + 5)
                            if s >= 2 and not on_act(s - 2):
                                w = (step(s - 2)[1] + 1) * P
                                v.wait_ge(sem("a_turned"), g * A_STEPS + (s - 1))
                                v.tensor_copy(prT[(s - 2) % (2 * A_G)][:, 0:w],
                                              tp[s % 2][:, 0:w]).then_inc(sem("a_prT_dve"), 1)
                            if s == HALF + 1:
                                widen(g, 0)
                            if s == HALF + 5:
                                results(g, 0, g * 5 + 4)
                        widen(g, 1)
                        if not last:
                            take_keys(g + 1, 1, g * 3 + 5)
                            join_queries(1, g * 5 + 7)
                            take(val[1][:, :, :].rearrange("p t d -> p (t d)"), g * 3 + 6)
                        results(g, 1, g * 5 + (5 if last else 8))

                    v.sem_inc(sem("a_out"), 1)
                    v.wait_ge(sem("a_zeroed"), 5)
                    take_keys(0, 0, 1)
                    join_queries(0, 1)
                    take_keys(0, 1, 2)
                    join_queries(1, 3)
                    take(val[1][:, :, :].rearrange("p t d -> p (t d)"), 3)
                    with v.Fori(0, A_GROUPS - 1) as g:
                        group(g, False)
                    group(A_GROUPS - 1, True)
                    v.wait_ge(sem("a_late"), 128)
                    for t in range(NT):
                        v.wait_ge(sem("a_oproj"), t + 1)
                        v.tensor_tensor(pre[:, t, :], bank[t % 4][:, 0:D], res[:, t, :],
                                        ALU.add).then_inc(sem("a_pre"), 1)
                        v.wait_ge(sem("a_pre"), t + 1)
                        norm_stats(v, own, t, pre)
                    norm_apply(v, own, 1, pre, res)
                    own.sync()
                    for t in range(NT):
                        norm_stats(v, own, t, res)
                    norm_apply(v, own, 2, res, nrm, sem("a_nrm"))
                    v.wait_ge(sem("a_late"), 128)
                    evac_dve(v, own, 0, sem("a_turn2"), sem("x_lo"), ln1w, ln1b)

                @blk.gpsimd
                def _(pool):
                    for b in range(B):
                        pool.memset(k_h[b][:, :, :].bitcast(F32), 0.0).then_inc(sem("a_zeroed"), 1)
                        pool.memset(k_l[b][:, :, :].bitcast(F32), 0.0).then_inc(sem("a_zeroed"), 1)
                    pool.memset(power[:, :], -0.5).then_inc(sem("a_zeroed"), 1)

                    def low_keys(g, b):
                        for h in range(2, A_G):
                            rows = slice(32 * h, 32 * h + 32)
                            pool.wait_ge(sem("a_k_hi"), g * 8 + (4 * b + 1 + h))
                            pool.tensor_tensor(k_l[b][rows, h, :], kf[b][rows, :], k_h[b][rows, h, :].bitcast(F32),
                                               ALU.subtract).then_inc(sem("a_k_lo_pool"), 1)

                    pool.wait_ge(sem("a_zeroed"), 5)
                    with pool.Fori(0, A_GROUPS) as g:
                        low_keys(g, 0)
                        low_keys(g, 1)
                    pool.wait_ge(sem("b_wqk_hi"), 1)
                    pool.tensor_tensor(wqk_l[:, :, :, :], wqk[:, :, :, :], wqk_h[:, :, :, :].bitcast(F32),
                                       ALU.subtract).then_inc(sem("b_wqk_lo"), 1)
                    pool.wait_ge(sem("b_wv_hi"), 1)
                    pool.tensor_tensor(wv_l[:, :, :], wv[:, :, :], wv_h[:, :, :].bitcast(F32),
                                       ALU.subtract).then_inc(sem("b_wv_lo"), 1)
                    pool_rstd(pool, 1)
                    pool_rstd(pool, 2)

        lay = ExitStack()
        with lay:
            wo = sb("b_wo", [P, B_H, D], ctx=lay)
            part = [sb(f"b_part{i}", [P, 2, S], ctx=lay) for i in range(2)]
            qk = [[sb(f"b_qk{b}{c}", [P, S], ctx=lay) for c in range(2)] for b in range(B)]
            val = sb("b_val", [P, NT, 2 * B_HD], ctx=lay)
            pr = [sb(f"b_pr{i}", [P, S], ctx=lay) for i in range(3)]
            prT = [sb("b_prT0", [P, QT, S], ctx=lay)[:, :, :],
                   nrm[:, :, :].rearrange("p (j x) d -> p j (x d)", x=NT // QT)]
            attT = sb("b_attT", [P, B_H, T], ctx=lay)
            nmax = sb("b_nmax", [P, B_STEPS], ctx=lay)
            ssum = sb("b_ssum", [P, B_STEPS], ctx=lay)
            rsum = sb("b_rsum", [P, B_STEPS], ctx=lay)
            sc, tp, ob, xb = bank[0:3], bank[3:5], bank[5], bank[6:8]
            CHUNKS = [(b, c) for b in range(B) for c in range(2)]
            pb = [sc[2], sc[0], xb[0], xb[1]]
            PAIRS = B_H // 2

            def at(h, n, k):
                i, j = h
                return i * (2 * n) + (j * n + k)

            def after(h):
                return h[0], h[1] + 1

            def head_no(h):
                return h[0] * 2 + h[1]

            with nc.Block() as blk:
                @blk.sync
                def _(sp):
                    sp.dma_start(wo[:, :, :], a["b_wo"].rearrange("(h p) n -> p h n", p=P)).then_inc(sem("b_wo"), 16)
                    def load_qk(i, j):
                        src = a["b_wqk"][ds(head_no((i, j)), 1), :, :, :, :].rearrange("a p c k n -> p (a c k) n")
                        sp.wait_ge(sem("b_wqk_lo"), at((i, j), 1, 0))
                        sp.dma_start(wqk[:, :, :, :].rearrange("p c k n -> p (c k) n"), src).then_inc(sem("b_wqk"), 16)

                    load_qk(0, 1)
                    with sp.Fori(1, PAIRS) as i:
                        load_qk(i, 0)
                        src_v = a["b_wv"][ds(i, 1), :, :, :].rearrange("a p k n -> p (a k) n")
                        sp.wait_ge(sem("b_wv_lo"), i)
                        sp.dma_start(wv[:, :, :], src_v).then_inc(sem("b_wv"), 16)
                        load_qk(i, 1)
                    load_first("m", sp, False)

                @blk.tensor
                def _(pe):
                    def project(h, n):
                        b, c = CHUNKS[n]
                        if n == 0:
                            pe.wait_ge(sem("b_wqk_lo"), at(h, 1, 1))
                        for kt in range(KD):
                            wh, wl = (w[:, c, kt, :] for w in (wqk_h, wqk_l))
                            x_h, x_l = (x[:, kt, b * S:(b + 1) * S] for x in (xh, xl))
                            pe.matmul(pb[n][:, :], wh, x_h, start=(kt == 0), stop=False)
                            pe.matmul(pb[n][:, :], wl, x_h, start=False, stop=False)
                            ins = pe.matmul(pb[n][:, :], wh, x_l, start=False, stop=(kt == KD - 1))
                        ins.then_inc(sem("b_proj"), 1)

                    def values(i, c):
                        if c == 0:
                            pe.wait_ge(sem("b_wv_lo"), i + 1)
                        if c < 2:
                            pe.wait_ge(sem("b_parts"), at((i, 0), 12, 9 + 3 * c))
                        else:
                            pe.wait_ge(sem("b_val"), i * 4 + (c - 1))
                        for t in (2 * c, 2 * c + 1):
                            dst = xb[c % 2][:, t % 2 * 2 * P:(t % 2 + 1) * 2 * P]
                            for kt in range(KD):
                                x_h, x_l = (x[:, kt, t * P:(t + 1) * P] for x in (xh, xl))
                                pe.matmul(dst, x_h, wv_h[:, kt, :], start=(kt == 0), stop=False)
                                pe.matmul(dst, x_h, wv_l[:, kt, :], start=False, stop=False)
                                ins = pe.matmul(dst, x_l, wv_h[:, kt, :], start=False, stop=(kt == KD - 1))
                        ins.then_inc(sem("b_vproj"), 1)

                    def scores(h, s):
                        b, i = s // QT, s % QT
                        if i == 0:
                            pe.wait_ge(sem("b_qk"), at(h, 4, 2 * (b + 1)))
                        w = (i + 1) * P
                        pe.matmul(sc[s % 3][:, 0:w], qk[b][0][:, i * P:w], qk[b][1][:, 0:w], start=True, stop=False)
                        pe.matmul(sc[s % 3][:, i * P:w], ident_bf[:, :], mask_bf[:, :],
                                  start=False, stop=True).then_inc(sem("b_scores"), 1)

                    def turn(h, s):
                        pe.wait_ge(sem("b_pr"), at(h, B_STEPS, s + 1))
                        if s >= 2:
                            pe.wait_ge(sem("b_prT"), at(h, B_STEPS, s - 1))
                        for j in range(s % QT + 1):
                            ins = pe.transpose(tp[s % 2][:, j * P:(j + 1) * P], pr[s % 3][:, j * P:(j + 1) * P],
                                               ident[:, :])
                        ins.then_inc(sem("b_turned"), 1)

                    def weigh(h, b):
                        pe.wait_ge(sem("b_prT"), at(h, B_STEPS, QT * (b + 1)))
                        pe.wait_ge(sem("b_val"), h[0] * 4 + 4)
                        pe.wait_ge(sem("b_out"), at(h, 2, b + 1))
                        for j in range(QT):
                            ins = pe.matmul(ob[:, j * P:S], val[:, b * QT + j, h[1] * P:(h[1] + 1) * P], prT[b][:, j, j * P:S],
                                            start=(j == 0), stop=(j == QT - 1))
                        ins.then_inc(sem("b_weighed"), 1)

                    def head(h, last):
                        if h[1] == 0:
                            values(h[0], 0)
                            values(h[0], 1)
                        for s in range(B_STEPS):
                            scores(h, s)
                            if h[1] == 0 and s < 2:
                                values(h[0], 2 + s)
                            if s >= 2:
                                turn(h, s - 2)
                            if s == QT + 2:
                                weigh(h, 0)
                        for n in range(2):
                            if not last:
                                project(after(h), n)
                            turn(h, B_STEPS - 2 + n)
                        if not last:
                            project(after(h), 2)
                            project(after(h), 3)
                        weigh(h, 1)

                    for n in range(4):
                        project((0, 0), n)
                    with pe.Fori(0, PAIRS - 1) as i:
                        head((i, 0), False)
                        head((i, 1), False)
                    head((PAIRS - 1, 0), False)
                    head((PAIRS - 1, 1), True)

                    pe.wait_ge(sem("b_wo"), 16)
                    pe.wait_ge(sem("b_out"), 2 * B_H + 1)
                    for t in range(NT):
                        if t >= 4:
                            pe.wait_ge(sem("b_h"), t - 3)
                        for h in range(B_H):
                            ins = pe.matmul(bank[t % 4][:, 0:D], attT[:, h, t * P:(t + 1) * P], wo[:, h, :],
                                            start=(h == 0), stop=(h == B_H - 1))
                        ins.then_inc(sem("b_oproj"), 1)
                    pe.wait_ge(sem("b_h"), NT)
                    transpose_tokens(pe, nrm, sem("b_nrm"), sem("b_turn2"))

                @blk.scalar
                def _(act):
                    def split_qk(h):
                        act.wait_ge(sem("b_wqk"), at(h, 16, 16))
                        act.activation(wqk_h[:, :, :, :], wqk[:, :, :, :], ACT.Copy).then_inc(sem("b_wqk_hi"), 1)

                    def split_v(i):
                        act.wait_ge(sem("b_wv"), i * 16 + 16)
                        act.activation(wv_h[:, :, :], wv[:, :, :], ACT.Copy).then_inc(sem("b_wv_hi"), 1)

                    def take_values(i, c):
                        act.wait_ge(sem("b_vproj"), i * 4 + (c + 1))
                        act.activation(val[:, 2 * c:2 * c + 2, :].rearrange("p t d -> p (t d)"), xb[c % 2][:, :],
                                       ACT.Copy).then_inc(sem("b_val"), 1)


                    def out_head(h, b):
                        act.wait_ge(sem("b_weighed"), at(h, 2, b + 1))
                        act.wait_ge(sem("b_small"), 64)
                        act.activation(attT[:, ds(head_no(h), 1), b * S:(b + 1) * S].rearrange("p a s -> p (a s)"), ob[:, :],
                                       ACT.Identity, bias=bv[:, ds(head_no(h), 1)]).then_inc(sem("b_out"), 1)

                    def head(h, last):
                        if h[1] == 0:
                            take_values(h[0], 0)
                            take_values(h[0], 1)
                        for s in range(B_STEPS + 2):
                            if h[1] == 0 and s in (1, 2):
                                take_values(h[0], 1 + s)
                            if s == 3 and not last:
                                split_qk(after(h))
                            if s == 7 and not last and h[1] == 1:
                                split_v(h[0] + 1)
                            if s < B_STEPS:
                                w = (s % QT + 1) * P
                                act.wait_ge(sem("b_max"), at(h, B_STEPS, s + 1))
                                if s >= 3:
                                    act.wait_ge(sem("b_turned"), at(h, B_STEPS, s - 2))
                                act.activation(pr[s % 3][:, 0:w], sc[s % 3][:, 0:w], ACT.Exp, bias=nmax[:, s:s + 1],
                                               scale=1.0, accum_out=ssum[:, s:s + 1]).then_inc(sem("b_exp"), 1)
                            if s >= 2:
                                b, i = (s - 2) // QT, (s - 2) % QT
                                act.wait_ge(sem("b_turned"), at(h, B_STEPS, s - 1))
                                act.activation(prT[b][:, 0:i + 1, i * P:(i + 1) * P],
                                               tp[s % 2][:, 0:(i + 1) * P].rearrange("p (j q) -> p j q", q=P),
                                               ACT.Copy).then_inc(sem("b_prT"), 1)
                            if s == QT + 3:
                                out_head(h, 0)
                        out_head(h, 1)

                    act.sem_inc(sem("b_out"), 1)
                    with act.Fori(0, PAIRS - 1) as i:
                        head((i, 0), False)
                        head((i, 1), False)
                    head((PAIRS - 1, 0), False)
                    head((PAIRS - 1, 1), True)
                    evac_act(act, 1, sem("b_turn2"), ln2w, ln2b)

                @blk.vector
                def _(v):
                    own = Order(v, sem("v_own_b"))
                    half = P // 2

                    def rotate(h, n):
                        b, c = CHUNKS[n]
                        x, t = pb[n], part[n % 2]
                        v.wait_ge(sem("b_proj"), at(h, 4, n + 1))
                        if n >= 2:
                            v.wait_ge(sem("b_qk"), at(h, 4, n - 1))
                        v.scalar_tensor_tensor(out=t[:, 0, :], in0=x[:, :], scalar=bqk[:, c, 0, ds(head_no(h), 1)],
                                               in1=rope[:, c, 0, :], op0=ALU.add,
                                               op1=ALU.mult).then_inc(sem("b_parts"), 1)
                        for lo, hi in ((0, half), (half, 0)):
                            v.scalar_tensor_tensor(out=t[lo:lo + half, 1, :], in0=x[hi:hi + half, :],
                                                   scalar=bqk[lo:lo + half, c, 1, ds(head_no(h), 1)],
                                                   in1=rope[lo:lo + half, c, 1, :], op0=ALU.add,
                                                   op1=ALU.mult).then_inc(sem("b_parts"), 1)

                    def head(h, last):
                        for s in range(B_STEPS + 1):
                            if s < B_STEPS:
                                w = (s % QT + 1) * P
                                v.wait_ge(sem("b_scores"), at(h, B_STEPS, s + 1))
                                v.tensor_reduce(nmax[:, s:s + 1], sc[s % 3][:, 0:w], AX.X, ALU.max,
                                                negate=True).then_inc(sem("b_max"), 1)
                            if s >= 1:
                                w = ((s - 1) % QT + 1) * P
                                v.wait_ge(sem("b_exp"), at(h, B_STEPS, s))
                                v.reciprocal(rsum[:, s - 1:s], ssum[:, s - 1:s]).then_inc(sem("b_rsum"), 1)
                                v.wait_ge(sem("b_rsum"), at(h, B_STEPS, s))
                                p = pr[(s - 1) % 3][:, 0:w]
                                v.tensor_scalar(p, p, rsum[:, s - 1:s], None, ALU.mult).then_inc(sem("b_pr"), 1)
                            if s == 1 and h[1] == 1:
                                rotate(h, 3)
                        if not last:
                            for n in range(4 if h[1] == 1 else 3):
                                rotate(after(h), n)

                    v.wait_ge(sem("b_small"), 64)
                    for n in range(4):
                        rotate((0, 0), n)
                    with v.Fori(0, PAIRS - 1) as i:
                        head((i, 0), False)
                        head((i, 1), False)
                    head((PAIRS - 1, 0), False)
                    head((PAIRS - 1, 1), True)
                    v.wait_ge(sem("b_hb"), NT)
                    for t in range(NT):
                        v.wait_ge(sem("b_oproj"), t + 1)
                        v.tensor_tensor(pre[:, t, :], bank[t % 4][:, 0:D], pre[:, t, :],
                                        ALU.add).then_inc(sem("b_h"), 1)
                        v.wait_ge(sem("b_h"), t + 1)
                        norm_stats(v, own, t, pre)
                    norm_apply(v, own, 3, pre, nrm, sem("b_nrm"))
                    evac_dve(v, own, 1, sem("b_turn2"), sem("x_lo"), ln2w, ln2b)

                @blk.gpsimd
                def _(pool):
                    def add_up(h):
                        for n, (b, c) in enumerate(CHUNKS):
                            t = part[n % 2]
                            pool.wait_ge(sem("b_parts"), at(h, 12, 3 * (n + 1)))
                            pool.tensor_tensor(qk[b][c][:, :], t[:, 0, :], t[:, 1, :],
                                               ALU.add).then_inc(sem("b_qk"), 1)

                    def split_qk(h):
                        pool.wait_ge(sem("b_wqk_hi"), at(h, 1, 1))
                        pool.tensor_tensor(wqk_l[:, :, :, :], wqk[:, :, :, :], wqk_h[:, :, :, :].bitcast(F32),
                                           ALU.subtract).then_inc(sem("b_wqk_lo"), 1)

                    def split_v(i):
                        pool.wait_ge(sem("b_wv_hi"), i + 1)
                        pool.tensor_tensor(wv_l[:, :, :], wv[:, :, :], wv_h[:, :, :].bitcast(F32),
                                           ALU.subtract).then_inc(sem("b_wv_lo"), 1)

                    add_up((0, 0))
                    pool.wait_ge(sem("b_small"), 64)
                    for t in range(NT):
                        pool.tensor_tensor(pre[:, t, :], res[:, t, :], bo[:, :], ALU.add).then_inc(sem("b_hb"), 1)
                    split_qk((0, 1))
                    add_up((0, 1))
                    with pool.Fori(1, PAIRS) as i:
                        split_qk((i, 0))
                        split_v(i)
                        add_up((i, 0))
                        split_qk((i, 1))
                        add_up((i, 1))
                    pool_rstd(pool, 3)

        ahead_b.close()

        def mixture(tag, experts, gated, init, k_norm):
            name = f"{tag}_"
            pairs = experts // 2
            n_up = 2 if gated else 1
            lay = ExitStack()
            with lay:
                wr = routers[tag]
                wup_h = [sb(f"{name}wup_h{k}", [P, n_up, KD, F], F32R, ctx=lay) for k in range(2)]
                wup_l = [sb(f"{name}wup_l{k}", [P, n_up, KD, F], F32R, ctx=lay) for k in range(2)]
                wdn_h = [sb(f"{name}wdn_h{k}", [P, KF, D], F32R, ctx=lay) for k in range(2)]
                wdn_l = [sb(f"{name}wdn_l{k}", [P, KF, D], F32R, ctx=lay) for k in range(2)]
                hid_h = [sb(f"{name}hid_h{k}", [P, KF, T], F32R, ctx=lay) for k in range(2)]
                hid_l = [sb(f"{name}hid_l{k}", [P, KF, T], F32R, ctx=lay) for k in range(2)]
                hid = [sb(f"{name}hid{i}", [P, T], ctx=lay) for i in range(2)]
                acc = sb(name + "acc", [P, NT, D], ctx=lay)
                gate = [sb(f"{name}gate{i}", [P, S], ctx=lay) for i in range(2)]
                if not gated:
                    combT = sb(name + "combT", [experts, T], ctx=lay)
                up, down = bank[0:4], bank[4:8]
                PARTS = [(mt, c) for mt in range(KF) for c in range(B)]
                SMALL = 16 if gated else 48
                deep = 2 if gated else 4
                per = 1 if gated else 2

                with nc.Block() as blk:
                    @blk.sync
                    def _(sp):
                        if tag == "m":
                            load_state_space(sp)
                        with sp.Fori(1, pairs) as i:
                            for k in range(2):
                                src = a[name + "wup"][ds(i * 2 + k, 1), :, :, :, :].rearrange("a p c k n -> p (a c k) n")
                                sp.wait_ge(sem(name + "w_lo"), i * 4 + (k - 3))
                                sp.dma_start(up_in[k][:, 0:n_up, :, :].rearrange("p c k n -> p (c k) n"),
                                             src).then_inc(sem(f"{name}wup{k}"), 16)
                            for k in range(2):
                                src = a[name + "wdn"][ds(i * 2 + k, 1), :, :, :].rearrange("a p k n -> p (a k) n")
                                sp.wait_ge(sem(name + "w_lo"), i * 4 + (k - 1))
                                sp.dma_start(dn_in[k][:, :, :], src).then_inc(sem(f"{name}wdn{k}"), 16)
                        if k_norm == 7:
                            dst = out.rearrange("b s d -> (b s) d").rearrange("(t p) d -> p t d", p=P)
                            for t in range(0, NT, 2):
                                sp.wait_ge(sem(name + "normed"), t + 2)
                                sp.dma_start(dst[:, t:t + 2, :], res[:, t:t + 2, :]).then_inc(sem("stored"), 16)
                            sp.wait_ge(sem("stored"), 16 * NT // 2)

                    @blk.tensor
                    def _(pe):
                        def router(tiles):
                            for t in tiles:
                                for kt in range(KD):
                                    ins = pe.matmul(bank[7][:, t * experts:(t + 1) * experts],
                                                    xT[:, kt, t * P:(t + 1) * P], wr[:, kt, :],
                                                    start=(kt == 0), stop=(kt == KD - 1))
                            ins.then_inc(sem(name + "logits"), 1)

                        pe.wait_ge(sem(name + "small"), SMALL)
                        router(range(NT // 2))

                        def second_biases():
                            pe.wait_ge(sem(name + "routed"), 1)
                            for t in range(NT):
                                ins = pe.transpose(bank[4 + t // 4][0:experts, t % 4 * P:(t % 4 + 1) * P],
                                                   comb[:, t, 0:experts], ident[:, :])
                            ins.then_inc(sem(name + "comb_turned"), 1)
                            pe.wait_ge(sem(name + "combT"), 1)
                            pe.wait_ge(sem(name + "small"), SMALL)
                            for t in range(NT):
                                if t >= 4:
                                    pe.wait_ge(sem(name + "acc"), t - 3)
                                pe.matmul(down[t % 4][:, 0:D], combT[:, t * P:(t + 1) * P], b2[:, :],
                                          start=True, stop=True).then_inc(sem(name + "bias"), 1)

                        def pair(i, first=False):
                            for k in range(2):
                                pe.wait_ge(sem(name + "w_lo"), i * 4 + (1 + k))
                                for q, (mt, c) in enumerate(PARTS):
                                    n = 4 * k + q
                                    if n >= deep:
                                        pe.wait_ge(sem(name + "hid"), i * (8 // per) + ((n - deep) // per + 1))
                                    for g in range(n_up):
                                        for kt in range(KD):
                                            wh, wl = (w[k][:, g, kt, mt * P:(mt + 1) * P] for w in (wup_h, wup_l))
                                            x_h, x_l = (x[:, kt, c * S:(c + 1) * S] for x in (xh, xl))
                                            dst = up[(q * n_up + g) % 4][:, :]
                                            pe.matmul(dst, wh, x_h, start=(kt == 0), stop=False)
                                            pe.matmul(dst, wh, x_l, start=False, stop=False)
                                            ins = pe.matmul(dst, wl, x_h, start=False, stop=(kt == KD - 1))
                                        ins.then_inc(sem(name + "up"), 1)
                                    if first and n == 0:
                                        router(range(NT // 2, NT))
                            if first and not gated:
                                second_biases()
                            for k in range(2):
                                pe.wait_ge(sem(name + "w_lo"), i * 4 + (3 + k))
                                for t in range(NT):
                                    if t in (0, 4):
                                        pe.wait_ge(sem(name + "hid_lo"), i * 8 + 4 * k + (3 if t == 0 else 4))
                                    pe.wait_ge(sem(name + "acc"), i * (2 * NT) + (NT * (k + 1) + t - 3))
                                    for kt in range(KF):
                                        h_h, h_l = (h[k][:, kt, t * P:(t + 1) * P] for h in (hid_h, hid_l))
                                        dst = down[t % 4][:, 0:D]
                                        pe.matmul(dst, h_h, wdn_h[k][:, kt, :], start=(kt == 0), stop=False)
                                        pe.matmul(dst, h_h, wdn_l[k][:, kt, :], start=False, stop=False)
                                        ins = pe.matmul(dst, h_l, wdn_h[k][:, kt, :], start=False, stop=(kt == KF - 1))
                                    ins.then_inc(sem(name + "down"), 1)

                        pair(0, True)
                        with pe.Fori(1, pairs) as i:
                            pair(i)

                    @blk.scalar
                    def _(act):
                        def split_up(i, k):
                            act.wait_ge(sem(f"{name}wup{k}"), i * 16 + 16)
                            act.activation(wup_h[k][:, :, :, :], up_in[k][:, 0:n_up, :, :],
                                           ACT.Copy).then_inc(sem(name + "w_hi"), 1)

                        def split_down(i, k):
                            act.wait_ge(sem(f"{name}wdn{k}"), i * 16 + 16)
                            act.activation(wdn_h[k][:, :, :], dn_in[k][:, :, :], ACT.Copy).then_inc(sem(name + "w_hi"), 1)

                        split_up(0, 0)
                        act.wait_ge(sem(name + "shifted"), 1)
                        act.activation(probs8[:, :, 0:experts], probs8[:, :, 0:experts],
                                       ACT.Exp).then_inc(sem(name + "exp"), 1)
                        split_up(0, 1)
                        if not gated:
                            act.wait_ge(sem(name + "small"), SMALL)

                        def pair(i, first=False, last=False):
                            for k in range(2):
                                if gated:
                                    for q in range(4):
                                        act.wait_ge(sem(name + "up"), i * 16 + (8 * k + 2 * q + 1))
                                        if not first or k or q >= 2:
                                            act.wait_ge(sem(name + "hid"), i * 8 + (4 * k + q - 1))
                                        act.activation(gate[q % 2][:, :], up[q % 2 * 2], ACT.Silu).then_inc(sem(name + "gate"), 1)
                                        if k == 0 and q in (0, 2):
                                            split_down(i, q // 2)
                                        if k == 1 and q == 1 and not last:
                                            split_up(i + 1, 0)
                                else:
                                    for mt in range(KF):
                                        act.wait_ge(sem(name + "up"), i * 8 + (4 * k + 2 * mt + 2))
                                        if not first or k:
                                            act.wait_ge(sem(name + "hid_lo"), i * 8 + (4 * k + 2 * mt - 2))
                                        act.activation(hid[mt][:, :],
                                                       psum[:, 2 * mt:2 * mt + 2, :].rearrange("p b s -> p (b s)"), ACT.Gelu,
                                                       bias=b1[:, mt, ds(i * 2 + k, 1)]).then_inc(sem(name + "hid"), 1)
                                        if k == 0:
                                            split_down(i, mt)
                                        if k == 1 and mt == 0 and not last:
                                            split_up(i + 1, 0)
                                    if first and k == 0:
                                        act.wait_ge(sem(name + "gap"), 1)
                                        act.activation(row2[:, :], row1[:, :], ACT.Exp).then_inc(sem(name + "exp"), 1)
                            if first and not gated:
                                act.wait_ge(sem(name + "comb_turned"), 1)
                                for n in range(2):
                                    ins = act.activation(combT[:, n * S:(n + 1) * S], bank[4 + n][0:experts, :], ACT.Copy)
                                ins.then_inc(sem(name + "combT"), 1)
                            if not last:
                                act.wait_ge(sem(name + "up"), (i + 1) * (8 * n_up))
                                split_up(i + 1, 1)

                        pair(0, first=True, last=(pairs == 1))
                        if pairs > 2:
                            with act.Fori(1, pairs - 1) as i:
                                pair(i)
                        pair(pairs - 1, last=True)
                        if tag == "m":
                            for t in range(NT):
                                act.wait_ge(sem(name + "normed"), t + 1)
                                act.activation(pre[:, t, :], res[:, t, :], ACT.Square,
                                               accum_out=ssq[:, t:t + 1]).then_inc(sem("c_ssq"), 1)

                    @blk.vector
                    def _(v):
                        own = Order(v, sem("v_own_" + tag))
                        pe8 = probs8[:, :, 0:experts]

                        def wide(x, n=experts):
                            return x.unsqueeze(2).to_broadcast([P, NT, n])

                        def route_shift():
                            own.mark(v.memset(probs8[:, :, :], -1.0))
                            v.wait_ge(sem(name + "logits"), 2)
                            logits = bank[7][:, 0:NT * experts].rearrange("p (t e) -> p t e", e=experts)
                            own.mark(v.tensor_reduce(row1[:, :], logits, AX.X, ALU.max))
                            own.sync()
                            v.tensor_tensor(pe8, logits, wide(row1[:, :]), ALU.subtract).then_inc(sem(name + "shifted"), 1)

                        def route_softmax():
                            v.wait_ge(sem(name + "exp"), 1)
                            own.mark(v.tensor_reduce(row1[:, :], pe8, AX.X, ALU.add))
                            own.sync()
                            own.mark(v.reciprocal(row2[:, :], row1[:, :]))
                            own.sync()
                            own.mark(v.tensor_tensor(pe8, pe8, wide(row2[:, :]), ALU.mult))
                            own.sync()

                        def route_top():
                            for t in range(NT):
                                own.mark(v.max(top8[:, t, :], probs8[:, t, :]))
                            own.sync()
                            for t in range(NT):
                                own.mark(v.max_index(idx8[:, t, :], top8[:, t, :], probs8[:, t, :]))
                            if gated:
                                own.mark(v.tensor_tensor(row1[:, :], top8[:, :, 0], top8[:, :, 1], ALU.add))
                                own.sync()
                                own.mark(v.reciprocal(row2[:, :], row1[:, :]))
                                own.sync()
                                own.mark(v.tensor_tensor(wts[:, :, :], top8[:, :, 0:2], wide(row2[:, :], 2), ALU.mult))
                            else:
                                v.tensor_tensor(row1[:, :], top8[:, :, 1], top8[:, :, 0],
                                                ALU.subtract).then_inc(sem(name + "gap"), 1)
                            own.sync()
                            own.mark(v.tensor_copy(idxf[:, :, :], idx8[:, :, 0:2]))
                            own.sync()

                        def route_weights():
                            if not gated:
                                v.wait_ge(sem(name + "exp"), 2)
                                own.mark(v.tensor_scalar(row1[:, :], row2[:, :], 1.0, None, ALU.add))
                                own.sync()
                                own.mark(v.reciprocal(wts[:, :, 0], row1[:, :]))
                                own.sync()
                                own.mark(v.tensor_tensor(wts[:, :, 1], wts[:, :, 0], row2[:, :], ALU.mult))
                                own.sync()
                            experts_row = iota[:, 0:experts].unsqueeze(1).to_broadcast([P, NT, experts])
                            for r, dst in ((0, comb), (1, pick)):
                                own.mark(v.tensor_tensor(dst[:, :, 0:experts], experts_row, wide(idxf[:, :, r]), ALU.is_equal))
                            for r, dst in ((0, comb), (1, pick)):
                                own.sync(behind=1)
                                x = dst[:, :, 0:experts]
                                own.mark(v.tensor_tensor(x, x, wide(wts[:, :, r]), ALU.mult))
                            own.sync()
                            v.tensor_tensor(comb[:, :, 0:experts], comb[:, :, 0:experts], pick[:, :, 0:experts],
                                            ALU.add).then_inc(sem(name + "routed"), 1)
                            v.wait_ge(sem(name + "routed"), 1)

                        def product(i, n):
                            v.wait_ge(sem(name + "gate"), i * 8 + (n + 1))
                            v.wait_ge(sem(name + "up"), i * 16 + (2 * n + 2))
                            if n >= 2:
                                v.wait_ge(sem(name + "hid_lo"), i * 8 + (n - 1))
                            v.tensor_tensor(hid[n % 2][:, 0:S], up[n % 2 * 2 + 1][:, :],
                                            gate[n % 2][:, :], ALU.mult).then_inc(sem(name + "hid"), 1)

                        def split(i, n, src):
                            k, (mt, c) = n // 4, PARTS[n % 4]
                            hi = hid_h[k][:, mt, c * S:(c + 1) * S]
                            v.wait_ge(sem(name + "hid"), i * (8 // per) + (n // per + 1))
                            v.tensor_copy(hi, src).then_inc(sem(name + "hid_hi"), 1)
                            v.wait_ge(sem(name + "hid_hi"), i * 8 + (n + 1))
                            v.tensor_tensor(hid_l[k][:, mt, c * S:(c + 1) * S], src, hi.bitcast(F32),
                                            ALU.subtract).then_inc(sem(name + "hid_lo"), 1)

                        route_shift()

                        def pair(i, first=False, last=False):
                            if gated:
                                for n in range(8):
                                    product(i, n)
                                    split(i, n, hid[n % 2][:, 0:S])
                                    if first and n == 0:
                                        route_softmax()
                                    if first and n == 1:
                                        route_top()
                                    if first and n == 2:
                                        route_weights()
                                    if first and n == 3:
                                        init(v, own, acc, down, sem(name + "bias"), sem(name + "acc"))
                            else:
                                if first:
                                    route_softmax()
                                    route_top()
                                for n in range(8):
                                    split(i, n, hid[n // 2 % 2][:, n % 2 * S:(n % 2 + 1) * S])
                                    if first and n == 5:
                                        route_weights()
                                if first:
                                    init(v, own, acc, down, sem(name + "bias"), sem(name + "acc"))
                            for k in range(2):
                                for t in range(NT):
                                    v.wait_ge(sem(name + "down"), i * (2 * NT) + (NT * k + t + 1))
                                    v.wait_ge(sem(name + "acc"), i * (2 * NT) + (NT * k + t + 1))
                                    v.scalar_tensor_tensor(out=acc[:, t, :], in0=down[t % 4][:, 0:D],
                                                           scalar=comb[:, t, ds(i * 2 + k, 1)], in1=acc[:, t, :],
                                                           op0=ALU.mult, op1=ALU.add).then_inc(sem(name + "acc"), 1)
                                    if last and k == 1:
                                        v.wait_ge(sem(name + "acc"), i * (2 * NT) + (NT * (k + 1) + t + 1))
                                        norm_stats(v, own, t, acc)

                        pair(0, True)
                        if pairs > 2:
                            with v.Fori(1, pairs - 1) as i:
                                pair(i)
                        pair(pairs - 1, last=True)
                        norm_apply(v, own, k_norm, acc, res, sem(name + "normed"))

                    @blk.gpsimd
                    def _(pool):
                        def split_up(i, k):
                            pool.wait_ge(sem(name + "w_hi"), i * 4 + (1 + k))
                            pool.tensor_tensor(wup_l[k][:, :, :, :], up_in[k][:, 0:n_up, :, :],
                                               wup_h[k][:, :, :, :].bitcast(F32),
                                               ALU.subtract).then_inc(sem(name + "w_lo"), 1)

                        def split_down(i, k):
                            pool.wait_ge(sem(name + "w_hi"), i * 4 + (3 + k))
                            pool.tensor_tensor(wdn_l[k][:, :, :], dn_in[k][:, :, :],
                                               wdn_h[k][:, :, :].bitcast(F32),
                                               ALU.subtract).then_inc(sem(name + "w_lo"), 1)

                        def pair(i, last=False):
                            for k in range(2):
                                split_down(i, k)
                            if not last:
                                for k in range(2):
                                    split_up(i + 1, k)

                        for k in range(2):
                            split_up(0, k)
                        with pool.Fori(0, pairs - 1) as i:
                            pair(i)
                        pair(pairs - 1, last=True)
                        pool_rstd(pool, k_norm)

        def init_b(v, own, acc, down, bias, ready):
            for t in range(NT):
                own.mark(v.tensor_tensor(acc[:, t, :], res[:, t, :], pre[:, t, :], ALU.add))
            for t in range(NT):
                own.sync()
                v.wait_ge(bias, t + 1)
                v.tensor_tensor(acc[:, t, :], down[t % 4][:, 0:D], acc[:, t, :], ALU.add).then_inc(ready, 1)

        ssq = sb("ssq", [P, NT])
        ahead = top.enter_context(ExitStack())
        win = sb("c_win", [P, KD, 2 * DI], ctx=ahead)
        wx = sb("c_wx", [P, KI, 2 * NS + 1], ctx=ahead)
        wout = sb("c_wout", [P, KI, D], ctx=ahead)
        cw = sb("c_cw", [P, KI, TAPS], ctx=ahead)
        cols = sb("c_cols", [P, 4, KI], ctx=ahead)
        alog = sb("c_alog", [P, KI, NS], ctx=ahead)
        sel = sb("c_sel", [P, 2 * NS, P], BF16, ctx=ahead)
        sel_step = sb("c_sel_step", [P, P], ctx=ahead)

        def load_state_space(sp):
            sp.dma_start(win[:, :, :], a["c_win"].rearrange("(k p) n -> p k n", p=P)).then_inc(sem("c_loaded"), 16)
            sp.dma_start(cw[:, :, :], a["c_cw"]).then_inc(sem("c_loaded"), 16)
            sp.dma_start(cols[:, :, :], a["c_cols"]).then_inc(sem("c_loaded"), 16)
            sp.dma_start(alog[:, :, :], a["c_alog"]).then_inc(sem("c_loaded"), 16)
            sp.dma_start(wx[:, :, :], a["c_wx"].rearrange("(k p) n -> p k n", p=P)).then_inc(sem("c_loaded"), 16)
            sp.dma_start(sel_step[:, :], a["c_sel_step"]).then_inc(sem("c_loaded"), 16)
            sp.dma_start(sel[:, :, :], a["c_sel"]).then_inc(sem("c_loaded"), 16)
            sp.dma_start(wout[:, :, :], a["c_wout"].rearrange("(k p) n -> p k n", p=P)).then_inc(sem("c_loaded"), 16)

        mixture("m", MOE_B, False, init_b, 4)

        lay = ExitStack()
        with lay:
            nega = sb("c_nega", [P, KI, NS], ctx=lay)
            xin = sb("c_xin", [P, KI, B, S + TAPS - 1], ctx=lay)
            gz = sb("c_gz", [P, KI, T], ctx=lay)
            xc = sb("c_xc", [P, KI, T], ctx=lay)
            dt = xin
            du = sb("c_du", [P, KI, T], ctx=lay)
            conv = [sb(f"c_conv{i}", [P, B, S], ctx=lay) for i in range(2)]
            bc_f = sb("c_bc_f", [2 * NS, T], ctx=lay)
            bc_p = sb("c_bc_p", [2 * NS, T], BF16, ctx=lay)
            bcs = sb("c_bcs", [P, T], BF16, ctx=lay)
            dg = sb("c_dg", [P, KI, P], ctx=lay)
            dtap = sb("c_dtap", [P, TAPS, P], ctx=lay)
            bs = [sb(f"c_bs{u}", [P, S], ctx=lay) for u in range(2)]
            da = [sb(f"c_da{m}", [P, S], ctx=lay) for m in range(KI)]
            dbu = [sb(f"c_dbu{m}", [P, S], ctx=lay) for m in range(KI)]
            with ExitStack() as early:
                win_h = sb("c_win_h", [P, KD, 2 * DI], F32R, ctx=early)
                win_l = sb("c_win_l", [P, KD, 2 * DI], F32R, ctx=early)
            st = [sb(f"c_st{m}", [P, S], ctx=lay) for m in range(KI)]
            hc = [sb(f"c_hc{m}", [P, S], ctx=lay) for m in range(KI)]
            yacc, bb, cb = bank[0:4], bank[4:6], bank[6:8]
            bconv, bproj, bstep = bank[0:2], bank[2:4], bank[4:6]
            bz = [bank[i] for i in (6, 7, 0, 1)]
            row = 2 * NS
            CH = [(b, m) for b in range(B) for m in range(KI)]

            def halved(b):
                return slice(b * S, (b + 1) * S)

            def split_rows(eng, own, b):
                rest = bc_f[:, halved(b)]
                part = bc_p[:, halved(b)]
                own.mark(eng.tensor_copy(bcs[0:32, halved(b)], bs[b][0:32, :]))
                own.sync()
                own.mark(eng.tensor_tensor(rest, bs[b][0:32, :], bcs[0:32, halved(b)], ALU.subtract))
                own.sync()
                own.mark(eng.tensor_copy(part, rest))
                own.sync()
                own.mark(eng.tensor_tensor(rest, rest, part, ALU.subtract))
                own.mark(eng.tensor_copy(bcs[32:64, halved(b)], part))
                own.sync()
                eng.tensor_copy(bcs[64:96, halved(b)], rest).then_inc(sem("c_split"), 1)
            CB, DTW, DTB, DP = range(4)

            def by_b(x):
                return x.rearrange("p (b s) -> p b s", b=B)

            with nc.Block() as blk:
                @blk.sync
                def _(sp):
                    load_first("d", sp, True)

                @blk.tensor
                def _(pe):
                    transpose_tokens(pe, nrm, sem("c_nrm"), sem("c_turn"), base=0)

                    def in_proj(n, dst):
                        m, b = n // 2, n % 2
                        for kt in range(KD):
                            wh, wl = (w[:, kt, m * P:(m + 1) * P] for w in (win_h, win_l))
                            x_h, x_l = (x[:, kt, b * S:(b + 1) * S] for x in (xh, xl))
                            pe.matmul(dst[:, :], wh, x_h, start=(kt == 0), stop=False)
                            pe.matmul(dst[:, :], wl, x_h, start=False, stop=False)
                            ins = pe.matmul(dst[:, :], wh, x_l, start=False, stop=(kt == KD - 1))
                        ins.then_inc(sem("c_in"), 1)

                    pe.wait_ge(sem("c_win_lo"), 1)
                    for n in range(8):
                        if n < 2:
                            pe.wait_ge(sem("c_x_lo"), 2 * n + 2)
                        if n >= 4:
                            pe.wait_ge(sem("c_in_out"), n - 3)
                        in_proj(n, bank[4 + n % 4])
                    pe.wait_ge(sem("c_dtap"), TAPS)
                    pe.wait_ge(sem("c_zero"), 2)
                    for b in range(B):
                        pe.wait_ge(sem("c_in_out"), 7 + b)
                        for k in range(TAPS):
                            ins = pe.matmul(bconv[b][:, :], dtap[:, k, :], xin[:, KI - 1, b, k:k + S],
                                            start=(k == 0), stop=(k == TAPS - 1))
                        ins.then_inc(sem("c_conv_pe"), 1)
                    pe.wait_ge(sem("c_loaded"), 128)
                    pe.wait_ge(sem("c_xc"), KI + 1)
                    for b in range(B):
                        for kt in range(KI):
                            ins = pe.matmul(bproj[b][0:row + 1, :], wx[:, kt, :], xc[:, kt, b * S:(b + 1) * S],
                                            start=(kt == 0), stop=(kt == KI - 1))
                        ins.then_inc(sem("c_bc"), 1)
                    for b in range(B):
                        pe.wait_ge(sem("c_rows"), b + 1)
                        pe.matmul(bstep[b][:, :], sel_step[:, :], bs[b][:, :], start=True,
                                  stop=True).then_inc(sem("c_step"), 1)
                    for n in range(8):
                        if n >= 4:
                            pe.wait_ge(sem("c_z"), n - 3)
                        in_proj(8 + n, bz[n % 4])

                    def spread(b, n, u):
                        cols_b = bcs[:, b * S:(b + 1) * S]
                        pe.matmul(bb[u][:, :], sel[:, ds(n, 1), :].rearrange("p a m -> p (a m)"), cols_b,
                                  start=True, stop=True).then_inc(sem("c_bb"), 1)
                        pe.matmul(cb[u][:, :], sel[:, ds(n + NS, 1), :].rearrange("p a m -> p (a m)"), cols_b,
                                  start=True, stop=True).then_inc(sem("c_cb"), 1)

                    def total(b, n, stop=False):
                        for m in range(KI):
                            pe.wait_ge(sem("c_hc"), n * KI + (b * NS * KI + KI + m + 1))
                            pe.matmul(yacc[m][:, :], ident[:, :], hc[m][:, :], start=False,
                                      stop=stop).then_inc(sem("c_sum"), 1)

                    def two(b, j, last):
                        for u in range(2):
                            total(b, j * 2 + u, last and u == 1)
                            if not last:
                                pe.wait_ge(sem("c_bs"), j * 2 + (b * NS + u + 1))
                                spread(b, j * 2 + (u + 2), u)

                    pe.wait_ge(sem("c_split"), 2)
                    pe.wait_ge(sem("c_loaded"), 128)
                    pe.wait_ge(sem("c_hc"), KI)
                    pe.wait_ge(sem("c_v"), 2 * KI)
                    pe.wait_ge(sem("c_z"), 8)
                    for b in range(B):
                        if b:
                            pe.wait_ge(sem("c_bs"), NS)
                        spread(b, 0, 0)
                        spread(b, 1, 1)
                        if b:
                            pe.wait_ge(sem("c_y"), KI)
                        for m in range(KI):
                            pe.matmul(yacc[m][:, :], dg[:, m, :], xc[:, m, b * S:(b + 1) * S], start=True,
                                      stop=False).then_inc(sem("c_sum"), 1)
                        with pe.Fori(0, NS // 2 - 1) as j:
                            two(b, j, False)
                        two(b, NS // 2 - 1, True)
                    pe.wait_ge(sem("c_loaded"), 128)
                    pe.wait_ge(sem("c_y"), 2 * KI)
                    for t in range(NT):
                        if t >= 4:
                            pe.wait_ge(sem("c_pre"), t - 3)
                        for kt in range(KI):
                            ins = pe.matmul(bank[t % 4][:, 0:D], gz[:, kt, t * P:(t + 1) * P], wout[:, kt, :],
                                            start=(kt == 0), stop=(kt == KI - 1))
                        ins.then_inc(sem("c_oproj"), 1)
                    pe.wait_ge(sem("c_pre"), NT)
                    transpose_tokens(pe, res, sem("c_res"), sem("c_turn2"))

                @blk.scalar
                def _(act):
                    act.wait_ge(sem("c_loaded"), 128)
                    act.activation(win_h[:, :, :], win[:, :, :], ACT.Copy).then_inc(sem("c_win_hi"), 1)
                    evac_act(act, 2, sem("c_turn"), rmsw)
                    for n in range(8):
                        act.wait_ge(sem("c_in"), n + 1)
                        act.activation(xin[:, n // 2, n % 2, TAPS - 1:], bank[4 + n % 4][:, :],
                                       ACT.Copy).then_inc(sem("c_in_out"), 1)

                    def silu_conv(m):
                        act.wait_ge(sem("c_conv"), m + 1)
                        act.activation(xc[:, m, :], conv[m % 2][:, :, :].rearrange("p b s -> p (b s)"),
                                       ACT.Silu).then_inc(sem("c_xc"), 1)

                    silu_conv(0)
                    silu_conv(1)
                    act.wait_ge(sem("c_loaded"), 128)
                    for b in range(B):
                        act.wait_ge(sem("c_conv_pe"), b + 1)
                        act.activation(xc[:, KI - 1, b * S:(b + 1) * S], bconv[b][:, :], ACT.Silu,
                                       bias=cols[:, CB, KI - 1:KI]).then_inc(sem("c_xc"), 1)
                    silu_conv(2)
                    for b in range(B):
                        act.wait_ge(sem("c_bc"), b + 1)
                        act.wait_ge(sem("c_zero"), 5)
                        act.activation(bs[b][0:row + 1, :], bproj[b][0:row + 1, :], ACT.Copy).then_inc(sem("c_rows"), 1)
                    act.activation(nega[:, :, :], alog[:, :, :], ACT.Exp).then_inc(sem("c_ea"), 1)
                    for n, (b, m) in enumerate(CH):
                        act.wait_ge(sem("c_v"), n + 1)
                        act.activation(du[:, m, b * S:(b + 1) * S], dt[:, m, b, 0:S], ACT.Abs).then_inc(sem("c_abs"), 1)
                    for n, (b, m) in enumerate(CH):
                        x = du[:, m, b * S:(b + 1) * S]
                        act.wait_ge(sem("c_abs"), n + 1)
                        act.activation(x, x, ACT.Exp, scale=-1.0).then_inc(sem("c_e"), 1)
                    for n, (b, m) in enumerate(CH):
                        x = du[:, m, b * S:(b + 1) * S]
                        act.wait_ge(sem("c_e"), n + 1)
                        act.activation(x, x, ACT.Ln, bias=1.0).then_inc(sem("c_l"), 1)

                    def copy_b(b, n, u):
                        act.wait_ge(sem("c_bb"), n + (b * NS + 1))
                        act.activation(bs[u][:, :], bb[u][:, :], ACT.Copy).then_inc(sem("c_bs"), 1)

                    def two(b, j, last):
                        for u in range(2):
                            for m in range(KI):
                                act.wait_ge(sem("c_scan"), j * (2 * KI) + (b * NS * KI + KI * u + m + 1))
                                act.wait_ge(sem("c_nega"), 1)
                                act.activation(da[m][:, :], dt[:, m, b, 0:S], ACT.Exp,
                                               scale=nega[:, m, ds(j * 2 + u, 1)]).then_inc(sem("c_da"), 1)
                            if not (last and u == 1):
                                act.wait_ge(sem("c_dbu"), j * (2 * KI) + (b * NS * KI + KI * (u + 1)))
                                copy_b(b, j * 2 + (u + 1), (u + 1) % 2)

                    act.wait_ge(sem("c_split"), 2)
                    copy_b(0, 0, 0)

                    def silu_z(b):
                        for m in range(KI):
                            act.wait_ge(sem("c_z"), 2 * m + 2)
                            act.activation(gz[:, m, halved(b)], gz[:, m, halved(b)],
                                           ACT.Silu).then_inc(sem("c_gz"), 1)

                    silu_z(0)
                    for b in range(B):
                        act.wait_ge(sem("c_dt"), (b + 1) * KI)
                        if b:
                            silu_z(1)
                            act.wait_ge(sem("c_dbu"), NS * KI)
                            copy_b(b, 0, 0)
                        with act.Fori(0, NS // 2 - 1) as j:
                            two(b, j, False)
                        two(b, NS // 2 - 1, True)
                    evac_act(act, 3, sem("c_turn2"))

                @blk.vector
                def _(v):
                    own = Order(v, sem("v_own_c"))
                    for half in range(2):
                        v.wait_ge(sem("c_ssq"), HT * (half + 1))
                        norm_var(v, own, half, ssq[:, half * HT:(half + 1) * HT], 1.0 / D)
                    v.wait_ge(sem("c_loaded"), 128)
                    for k in range(TAPS):
                        v.tensor_scalar(dtap[:, k, :], ident[:, :], cw[:, KI - 1, k:k + 1], None,
                                        ALU.mult).then_inc(sem("c_dtap"), 1)
                    for m in range(KI):
                        v.tensor_scalar(dg[:, m, :], ident[:, :], cols[:, DP, m:m + 1], None,
                                        ALU.mult).then_inc(sem("c_hc"), 1)
                    for t in range(NT):
                        if t % HT == 0:
                            v.wait_ge(sem("rstd_ready"), 9 + t // HT)
                        v.tensor_scalar(nrm[:, t, :], res[:, t, :], rstd[:, t:t + 1], None,
                                        ALU.mult).then_inc(sem("c_nrm"), 1)
                    evac_dve(v, own, 2, sem("c_turn"), sem("c_x_lo"), rmsw)
                    v.wait_ge(sem("c_zero"), 2)
                    for m in range(KI - 1):
                        v.wait_ge(sem("c_in_out"), 2 * m + 2)
                        if m >= 2:
                            v.wait_ge(sem("c_xc"), m - 1)
                        own.mark(v.tensor_scalar(conv[m % 2][:, :, :], xin[:, m, :, 0:S], cw[:, m, 0:1], cols[:, CB, m:m + 1],
                                                 ALU.mult, ALU.add))
                        for k in range(1, TAPS):
                            own.sync()
                            ins = v.scalar_tensor_tensor(out=conv[m % 2][:, :, :], in0=xin[:, m, :, k:k + S],
                                                         scalar=cw[:, m, k:k + 1], in1=conv[m % 2][:, :, :],
                                                         op0=ALU.mult, op1=ALU.add)
                            if k < TAPS - 1:
                                own.mark(ins)
                            else:
                                ins.then_inc(sem("c_conv"), 1)
                    v.wait_ge(sem("c_zero"), 5)
                    v.wait_ge(sem("c_rows"), 1)
                    split_rows(v, own, 0)
                    for n, (b, m) in enumerate(CH):
                        v.wait_ge(sem("c_step"), b + 1)
                        v.tensor_scalar(dt[:, m, b, 0:S], bstep[b][:, :], cols[:, DTW, m:m + 1],
                                        cols[:, DTB, m:m + 1], ALU.mult, ALU.add).then_inc(sem("c_v"), 1)
                    for n in range(8):
                        v.wait_ge(sem("c_in"), 8 + n + 1)
                        v.tensor_copy(gz[:, n // 2, n % 2 * S:(n % 2 + 1) * S], bz[n % 4][:, :]).then_inc(sem("c_z"), 1)
                    v.wait_ge(sem("c_ea"), 1)
                    v.tensor_scalar(nega[:, :, :], nega[:, :, :], -1.0, None, ALU.mult).then_inc(sem("c_nega"), 1)
                    def softplus(b, m):
                        v.wait_ge(sem("c_l"), b * KI + m + 1)
                        return v.scalar_tensor_tensor(out=dt[:, m, b, 0:S], in0=dt[:, m, b, 0:S], scalar=0.0,
                                                      in1=du[:, m, halved(b)], op0=ALU.max, op1=ALU.add)

                    def times_u(eng, b, m):
                        eng.wait_ge(sem("c_dt"), b * KI + m + 1)
                        return eng.tensor_tensor(du[:, m, halved(b)], dt[:, m, b, 0:S], xc[:, m, halved(b)], ALU.mult)

                    for m in (0, 1, 2, 3):
                        softplus(0, m).then_inc(sem("c_dt"), 1)
                    for m in (0, 1):
                        times_u(v, 0, m).then_inc(sem("c_du"), 1)
                    for m in range(KI):
                        softplus(1, m).then_inc(sem("c_dt"), 1)
                        times_u(v, 1, m).then_inc(sem("c_scan"), 1)

                    def scan(b, n, m):
                        done = b * NS * KI + m + 1
                        v.wait_ge(sem("c_da"), n * KI + done)
                        v.wait_ge(sem("c_dbu"), n * KI + (KI + done))
                        v.wait_ge(sem("c_hc"), n * KI + done)
                        v.tensor_tensor_scan(st[m][:, :], da[m][:, :], dbu[m][:, :], 0.0, ALU.mult,
                                             ALU.add).then_inc(sem("c_scan"), 1)

                    def times_c(b, n, m, u):
                        done = b * NS * KI + m + 1
                        v.wait_ge(sem("c_scan"), n * KI + (KI + done))
                        if m == 0:
                            v.wait_ge(sem("c_cb"), n + (b * NS + 1))
                        v.wait_ge(sem("c_sum"), n * KI + (b * (NS + 1) * KI + m + 1))
                        v.tensor_tensor(hc[m][:, :], st[m][:, :], cb[u][:, :], ALU.mult).then_inc(sem("c_hc"), 1)

                    def two(b, j):
                        for u in range(2):
                            n = j * 2 + u
                            scan(b, n, 0)
                            for m in range(1, KI):
                                scan(b, n, m)
                                times_c(b, n, m - 1, u)
                            times_c(b, n, KI - 1, u)

                    for b in range(B):
                        with v.Fori(0, NS // 2) as j:
                            two(b, j)
                        for m in range(KI):
                            v.wait_ge(sem("c_sum"), (NS + 1) * KI * (b + 1) - KI + m + 1)
                            v.wait_ge(sem("c_gz"), b * KI + m + 1)
                            z = gz[:, m, b * S:(b + 1) * S]
                            v.tensor_tensor(z, yacc[m][:, :], z, ALU.mult).then_inc(sem("c_y"), 1)
                    for t in range(NT):
                        v.wait_ge(sem("c_oproj"), t + 1)
                        v.scalar_tensor_tensor(out=pre[:, t, :], in0=res[:, t, :], scalar=2.0,
                                               in1=bank[t % 4][:, 0:D], op0=ALU.mult,
                                               op1=ALU.add).then_inc(sem("c_pre"), 1)
                        v.wait_ge(sem("c_pre"), t + 1)
                        norm_stats(v, own, t, pre)
                    norm_apply(v, own, 6, pre, res, sem("c_res"))
                    evac_dve(v, own, 3, sem("c_turn2"), sem("x_lo"))

                @blk.gpsimd
                def _(pool):
                    own = Order(pool, sem("pool_own_c"))
                    for b in range(B):
                        pool.memset(xin[:, :, b, 0:TAPS - 1], 0.0).then_inc(sem("c_zero"), 1)
                    pool_rstd(pool, 5)
                    pool.wait_ge(sem("c_win_hi"), 1)
                    pool.tensor_tensor(win_l[:, :, :], win[:, :, :], win_h[:, :, :].bitcast(F32), ALU.subtract).then_inc(sem("c_win_lo"), 1)
                    pool.memset(bcs[:, :].bitcast(F32), 0.0).then_inc(sem("c_zero"), 1)
                    for b in range(B):
                        ins = pool.memset(bs[b][:, :], 0.0)
                        ins.then_inc(sem("c_zero"), 1)
                    def inputs(b, n, u):
                        pool.wait_ge(sem("c_bs"), n + (b * NS + 1))
                        for m in range(KI):
                            pool.wait_ge(sem("c_scan"), n * KI + (b * NS * KI + m + 1))
                            pool.tensor_tensor(dbu[m][:, :], du[:, m, b * S:(b + 1) * S], bs[u][:, :],
                                               ALU.mult).then_inc(sem("c_dbu"), 1)

                    pool.wait_ge(sem("c_rows"), 2)
                    split_rows(pool, own, 1)
                    pool.wait_ge(sem("c_split"), 2)
                    for m in (2, 3):
                        pool.wait_ge(sem("c_dt"), m + 1)
                        own.mark(pool.tensor_tensor(du[:, m, halved(0)], dt[:, m, 0, 0:S], xc[:, m, halved(0)], ALU.mult))
                    own.sync()
                    pool.sem_inc(sem("c_dbu"), KI)
                    pool.wait_ge(sem("c_du"), 2)
                    for b in range(B):
                        if b:
                            pool.wait_ge(sem("c_scan"), KI)
                        with pool.Fori(0, NS // 2) as j:
                            for u in range(2):
                                inputs(b, j * 2 + u, u)
                    pool_rstd(pool, 6)

        def init_d(v, own, acc, down, bias, ready):
            for t in range(NT):
                v.tensor_copy(acc[:, t, :], res[:, t, :]).then_inc(ready, 1)

        mixture("d", MOE_D, True, init_d, 7)


def kernel(**inputs):
    import numpy as np
    import concourse.bacc as bacc
    from concourse import mybir as _mybir
    from concourse.bass_utils import run_bass_kernel_spmd as run

    x = {k: np.asarray(v) for k, v in inputs.items()}
    bf16 = _mybir.dt.np(_mybir.dt.bfloat16) if hasattr(_mybir.dt, "np") else None
    import ml_dtypes
    bf16 = ml_dtypes.bfloat16
    f32 = np.float32
    arrays = {}

    def put(name, v):
        arrays["in_" + name] = np.ascontiguousarray(v)

    tok = x["L0_attn_hidden_states"].reshape(T, D)
    put("x", tok)
    put("xT", tok.T)

    def by_part(v):
        return v.reshape(-1, P).T

    put("ident", np.eye(P, dtype=f32))
    put("ident_bf", np.eye(P).astype(bf16))
    put("mask_bf", np.where(np.arange(P)[None, :] > np.arange(P)[:, None], -1e30, 0.0).astype(bf16))
    put("iota", np.broadcast_to(np.arange(8, dtype=f32), (P, 8)))
    sel = np.zeros((P, 2 * NS, P), f32)
    for n in range(2 * NS):
        sel[[n, 32 + n, 64 + n], n, :] = 1.0
    put("c_sel", sel.astype(bf16))
    inv = f32(1.0) / np.power(f32(10000.0), np.arange(0, B_HD, 2, dtype=f32) / f32(B_HD)).astype(f32)
    ang = np.arange(S, dtype=f32)[:, None] * inv[None, :]
    cos = np.concatenate([np.cos(ang), np.cos(ang)], 1).T.astype(f32)
    sin = np.concatenate([-np.sin(ang), np.sin(ang)], 1).T.astype(f32)
    sc = 1.0 / np.sqrt(float(B_HD))
    put("b_rope", np.stack([np.stack([cos * sc, sin * sc]), np.stack([cos, sin])]).transpose(2, 0, 1, 3).astype(f32))

    w = x["L0_attn_w_qkv"].reshape(3, A_GROUPS, A_G, A_HD, KD, P)
    wqkv = np.zeros((A_GROUPS, P, 3, KD, A_G, 32), f32)
    wqkv[..., 0:A_HD] = w.transpose(1, 5, 0, 4, 2, 3)
    wqkv[:, :, 0:2, :, :, A_HD:] = wqkv[:, :, 0:2, :, :, 0:A_HD]
    second = (np.arange(P) % 32 >= A_HD).astype(f32)
    put("a_halves", np.stack([1 - 2 * second, second * f32(float(A_HD) ** -0.5)], 1))
    put("a_wqkv", wqkv.reshape(A_GROUPS, P, 3, KD, P))
    wo = np.zeros((A_GROUPS, A_G, 32, D), f32)
    wo[:, :, 0:A_HD] = x["L0_attn_w_o"].T.reshape(A_GROUPS, A_G, A_HD, D)
    put("a_wo", wo.reshape(A_GROUPS * P, D))
    for n, k in (("ln1w", "ln1_w"), ("ln1b", "ln1_b"), ("ln2w", "ln2_w"), ("ln2b", "ln2_b")):
        put(n, by_part(x["L0_ffn_" + k]))
    wq, wk, wv = (x["L0_ffn_" + n].reshape(KD, P, B_H, B_HD) for n in ("wq", "wk", "wv"))
    put("b_wqk", np.stack([wq, wk]).transpose(3, 2, 0, 1, 4))
    put("b_wv", wv.reshape(KD, P, B_H // 2, 2 * B_HD).transpose(2, 1, 0, 3))
    bq, bk = (x["L0_ffn_" + n].reshape(B_H, 2, P // 2) for n in ("bq", "bk"))
    both = np.stack([bq, bk])
    put("b_bqk", np.stack([both, both[:, :, ::-1]], 1).reshape(2, 2, B_H, P).transpose(3, 0, 1, 2))
    put("b_bv", by_part(x["L0_ffn_bv"]))
    put("b_bo", x["L0_ffn_bo"])
    put("b_wo", x["L0_ffn_wo"])
    put("m_wr", x["L0_ffn_w_gate"])
    put("m_wup", x["L0_ffn_we1"].reshape(MOE_B, 1, KD, P, F).transpose(0, 3, 1, 2, 4))
    put("m_wdn", x["L0_ffn_we2"].reshape(MOE_B, KF, P, D).transpose(0, 2, 1, 3))
    put("m_b1", x["L0_ffn_be1"].reshape(MOE_B, KF, P).transpose(2, 1, 0))
    put("m_b2", x["L0_ffn_be2"])
    put("rmsw", by_part(x["L1_attn_norm_w"]))
    put("c_win", x["L1_attn_in_proj_w"].T)
    put("c_wx", x["L1_attn_x_proj_w"].T)
    put("c_sel_step", np.repeat((np.arange(P) == 2 * NS).astype(f32)[:, None], P, 1))
    put("c_wout", x["L1_attn_out_proj_w"].T)
    put("c_cw", x["L1_attn_conv_w"].reshape(KI, P, TAPS).transpose(1, 0, 2))
    put("c_cols", np.stack([by_part(x["L1_attn_conv_b"]), by_part(x["L1_attn_dt_w"].reshape(-1)),
                            by_part(x["L1_attn_dt_b"]), by_part(x["L1_attn_D_param"])], 1))
    put("c_alog", x["L1_attn_A_log"].reshape(KI, P, NS).transpose(1, 0, 2))
    put("d_wr", x["L1_ffn_Wr"])
    put("d_wup", np.stack([x["L1_ffn_Wg"], x["L1_ffn_Wu"]], 1).reshape(MOE_D, 2, KD, P, F).transpose(0, 3, 1, 2, 4))
    put("d_wdn", x["L1_ffn_Wd"].reshape(MOE_D, KF, P, D).transpose(0, 2, 1, 3))

    nc = bacc.Bacc("TRN2", target_bir_lowering=False, num_devices=1)
    aps = {n[3:]: nc.dram_tensor(n, v.shape, _mybir.dt.from_np(v.dtype), kind="ExternalInput").ap()
           for n, v in arrays.items()}
    out = nc.dram_tensor("out_0_dram", (B, S, D), _mybir.dt.float32, kind="ExternalOutput").ap()
    build_program(nc, aps, out)
    r = run(nc, [arrays], core_ids=[0])
    return r.results[0]["out_0_dram"]
```
